# Optimizing a Trainium2 kernel written in Bass

```python
import numpy as np
import jax
import jax.numpy as jnp

def _softmax(x, axis=-1):
    return jax.nn.softmax(x, axis=axis)

def _gelu(x):
    return jax.nn.gelu(x, approximate=True)

def _silu(x):
    return jax.nn.silu(x)

def _sigmoid(x):
    return jax.nn.sigmoid(x)

def _layernorm(x, axis=-1, eps=1e-05):
    m = jnp.mean(x, axis=axis, keepdims=True)
    v = jnp.var(x, axis=axis, keepdims=True)
    return (x - m) / jnp.sqrt(v + eps)

def _scatter_add(tgt, idx, src, axis=0):
    return tgt.at[idx].add(src)

def _segment_sum(src, seg, n):
    return jax.ops.segment_sum(src, seg, n)
kernel_name = 'mk_gnn_preln_d2_gnn_r8_4cc603'

def setup_inputs(seed: int=0):
    np.random.seed(seed)
    _w = jnp.asarray

    def _rec_inputs():
        import jax
        import jax.numpy as jnp
        _gk = jax.random.key(seed)
        x = -0.000202 + 1 * jax.random.normal(jax.random.fold_in(_gk, 1), (6250, 64), jnp.float32)
        _s = jax.random.randint(jax.random.fold_in(_gk, 2), (100000,), 0, 6250, jnp.int32)
        _d = jax.random.randint(jax.random.fold_in(_gk, 3), (100000,), 0, 6250, jnp.int32)
        _loop = jnp.arange(6250, dtype=jnp.int32)
        src = jnp.concatenate([_s, _d, _loop])
        dst = jnp.concatenate([_d, _s, _loop])
        _o = jnp.argsort(dst, stable=True)
        src = src[_o]
        dst = dst[_o]
        edge_attr_16 = 0.000216709 + 1.00012 * jax.random.normal(jax.random.fold_in(_gk, 11), (206250, 16), jnp.float32)
        edge_weight = jax.random.uniform(jax.random.fold_in(_gk, 13), (206250,), jnp.float32, 0.0, 0.999999)
        return (x, src, dst, edge_attr_16, edge_weight)
    x, src, dst, edge_attr_16, edge_weight = _rec_inputs()

    def _L0_gnn_setup():
        import jax, jax.numpy as jnp
        import numpy as np
        N = 12500
        E = 200000
        F_IN = 64
        F_HID = 128
        F_EDGE = 16
        CUTOFF = 5.0
        IN_DIM = 2 * F_IN + F_EDGE + 1
        key = jax.random.key(seed)
        ks = jax.random.split(key, 12)

        def lin(k, fan_in, fan_out):
            bound = 1.0 / np.sqrt(fan_in)
            kw, kb = jax.random.split(k)
            W = jax.random.uniform(kw, (fan_in, fan_out), jnp.float32, -bound, bound)
            b = jax.random.uniform(kb, (fan_out,), jnp.float32, -bound, bound)
            return (W, b)
        x = jax.random.normal(ks[0], (N, F_IN), jnp.float32)
        edge_index = jax.random.randint(ks[1], (2, E), 0, N, jnp.int32)
        edge_weight = jax.random.uniform(ks[2], (E,), jnp.float32)
        edge_attr = jax.random.normal(ks[3], (E, F_EDGE), jnp.float32)
        ew1, eb1 = lin(ks[4], IN_DIM, F_HID)
        ew2, eb2 = lin(ks[5], F_HID, F_HID)
        nw1, nb1 = lin(ks[6], F_IN + F_HID, F_HID)
        nw2, nb2 = lin(ks[7], F_HID, F_IN)
        return {'x': x, 'edge_index': edge_index, 'edge_weight': edge_weight, 'edge_attr': edge_attr, 'ew1': ew1, 'eb1': eb1, 'ew2': ew2, 'eb2': eb2, 'nw1': nw1, 'nb1': nb1, 'nw2': nw2, 'nb2': nb2}
    _L0_gnn_all = _L0_gnn_setup()
    _L0_gnn_in = {k: v for k, v in _L0_gnn_all.items() if k in ('ew1', 'eb1', 'ew2', 'eb2', 'nw1', 'nb1', 'nw2', 'nb2')}
    del _L0_gnn_all

    def _L1_gnn_setup():
        import jax, jax.numpy as jnp
        import numpy as np
        N = 12500
        E = 200000
        IN_DIM = 64
        HID = 32
        HEADS = 4
        OUT_DIM = 64
        NEG_SLOPE = 0.2
        EPS = 1e-16

        def _glorot(key, shape):
            fan_in, fan_out = (shape[0], shape[-1])
            lim = jnp.sqrt(6.0 / (fan_in + fan_out))
            return jax.random.uniform(key, shape, jnp.float32, -lim, lim)

        def _segment_softmax(e, seg, num_segments):
            m = jax.ops.segment_max(e, seg, num_segments=num_segments)
            ex = jnp.exp(e - m[seg])
            s = jax.ops.segment_sum(ex, seg, num_segments=num_segments)
            return ex / (s[seg] + EPS)

        def _gat_layer(x, src, dst, W, a_src, a_dst, b, heads, ch, concat):
            n = x.shape[0]
            h = (x @ W).reshape(n, heads, ch)
            alpha_src = jnp.sum(h * a_src, axis=-1)
            alpha_dst = jnp.sum(h * a_dst, axis=-1)
            e = alpha_src[src] + alpha_dst[dst]
            e = jnp.where(e > 0, e, NEG_SLOPE * e)
            alpha = _segment_softmax(e, dst, n)
            msg = h[src] * alpha[:, :, None]
            out = jax.ops.segment_sum(msg, dst, num_segments=n)
            out = out.reshape(n, heads * ch) if concat else out.mean(axis=1)
            return out + b
        key = jax.random.key(seed)
        ks = jax.random.split(key, 12)
        x = jax.random.normal(ks[0], (N, IN_DIM), jnp.float32)
        edge_index = jax.random.randint(ks[1], (2, E), 0, N, jnp.int32)
        W1 = _glorot(ks[2], (IN_DIM, HEADS * HID))
        a_src1 = _glorot(ks[3], (1, HEADS, HID)) * 0.1
        a_dst1 = _glorot(ks[4], (1, HEADS, HID)) * 0.1
        b1 = jnp.zeros((HEADS * HID,), jnp.float32)
        W2 = _glorot(ks[5], (HEADS * HID, OUT_DIM))
        a_src2 = _glorot(ks[6], (1, 1, OUT_DIM)) * 0.1
        a_dst2 = _glorot(ks[7], (1, 1, OUT_DIM)) * 0.1
        b2 = jnp.zeros((OUT_DIM,), jnp.float32)
        return {'x': x, 'edge_index': edge_index, 'W1': W1, 'a_src1': a_src1, 'a_dst1': a_dst1, 'b1': b1, 'W2': W2, 'a_src2': a_src2, 'a_dst2': a_dst2, 'b2': b2}
    _L1_gnn_all = _L1_gnn_setup()
    _L1_gnn_in = {k: v for k, v in _L1_gnn_all.items() if k in ('W1', 'a_src1', 'a_dst1', 'b1', 'W2', 'a_src2', 'a_dst2', 'b2')}
    del _L1_gnn_all
    return {'x': x, 'src': src, 'dst': dst, 'edge_attr_16': edge_attr_16, 'edge_weight': edge_weight, 'L0_gnn_ew1': _L0_gnn_in['ew1'], 'L0_gnn_eb1': _L0_gnn_in['eb1'], 'L0_gnn_ew2': _L0_gnn_in['ew2'], 'L0_gnn_eb2': _L0_gnn_in['eb2'], 'L0_gnn_nw1': _L0_gnn_in['nw1'], 'L0_gnn_nb1': _L0_gnn_in['nb1'], 'L0_gnn_nw2': _L0_gnn_in['nw2'], 'L0_gnn_nb2': _L0_gnn_in['nb2'], 'L1_gnn_W1': _L1_gnn_in['W1'], 'L1_gnn_a_src1': _L1_gnn_in['a_src1'], 'L1_gnn_a_dst1': _L1_gnn_in['a_dst1'], 'L1_gnn_b1': _L1_gnn_in['b1'], 'L1_gnn_W2': _L1_gnn_in['W2'], 'L1_gnn_a_src2': _L1_gnn_in['a_src2'], 'L1_gnn_a_dst2': _L1_gnn_in['a_dst2'], 'L1_gnn_b2': _L1_gnn_in['b2']}

def reference(x, src, dst, edge_attr_16, edge_weight, L0_gnn_ew1, L0_gnn_eb1, L0_gnn_ew2, L0_gnn_eb2, L0_gnn_nw1, L0_gnn_nb1, L0_gnn_nw2, L0_gnn_nb2, L1_gnn_W1, L1_gnn_a_src1, L1_gnn_a_dst1, L1_gnn_b1, L1_gnn_W2, L1_gnn_a_src2, L1_gnn_a_dst2, L1_gnn_b2):
    import jax
    import jax.numpy as jnp

    def _L0_gnn_ref(x, edge_index, edge_weight, edge_attr, ew1, eb1, ew2, eb2, nw1, nb1, nw2, nb2):
        import jax, jax.numpy as jnp
        import numpy as np
        N = 12500
        E = 200000
        F_IN = 64
        F_HID = 128
        F_EDGE = 16
        CUTOFF = 5.0
        IN_DIM = 2 * F_IN + F_EDGE + 1
        row, col = (edge_index[0], edge_index[1])
        d_raw = (edge_weight / CUTOFF)[:, None]
        edge_input = jnp.concatenate([x[row], x[col], edge_attr, d_raw], axis=-1)
        h = jax.nn.silu(edge_input @ ew1 + eb1)
        m_ij = jax.nn.silu(h @ ew2 + eb2)
        agg = jax.ops.segment_sum(m_ij, row, num_segments=x.shape[0])
        node_in = jnp.concatenate([x, agg], axis=-1)
        upd = jax.nn.silu(node_in @ nw1 + nb1) @ nw2 + nb2
        return x + upd

    def _L1_gnn_ref(x, edge_index, W1, a_src1, a_dst1, b1, W2, a_src2, a_dst2, b2):
        import jax, jax.numpy as jnp
        import numpy as np
        N = 12500
        E = 200000
        IN_DIM = 64
        HID = 32
        HEADS = 4
        OUT_DIM = 64
        NEG_SLOPE = 0.2
        EPS = 1e-16

        def _glorot(key, shape):
            fan_in, fan_out = (shape[0], shape[-1])
            lim = jnp.sqrt(6.0 / (fan_in + fan_out))
            return jax.random.uniform(key, shape, jnp.float32, -lim, lim)

        def _segment_softmax(e, seg, num_segments):
            m = jax.ops.segment_max(e, seg, num_segments=num_segments)
            ex = jnp.exp(e - m[seg])
            s = jax.ops.segment_sum(ex, seg, num_segments=num_segments)
            return ex / (s[seg] + EPS)

        def _gat_layer(x, src, dst, W, a_src, a_dst, b, heads, ch, concat):
            n = x.shape[0]
            h = (x @ W).reshape(n, heads, ch)
            alpha_src = jnp.sum(h * a_src, axis=-1)
            alpha_dst = jnp.sum(h * a_dst, axis=-1)
            e = alpha_src[src] + alpha_dst[dst]
            e = jnp.where(e > 0, e, NEG_SLOPE * e)
            alpha = _segment_softmax(e, dst, n)
            msg = h[src] * alpha[:, :, None]
            out = jax.ops.segment_sum(msg, dst, num_segments=n)
            out = out.reshape(n, heads * ch) if concat else out.mean(axis=1)
            return out + b
        n = x.shape[0]
        loops = jnp.arange(n, dtype=edge_index.dtype)
        src = jnp.concatenate([edge_index[0], loops])
        dst = jnp.concatenate([edge_index[1], loops])
        h = _gat_layer(x, src, dst, W1, a_src1, a_dst1, b1, HEADS, HID, True)
        h = jax.nn.relu(h)
        h = _gat_layer(h, src, dst, W2, a_src2, a_dst2, b2, 1, OUT_DIM, False)
        return h
    edge_index = jnp.stack([src, dst])
    h = jnp.maximum(_layernorm(x, axis=-1), 0.0)
    x = x + _L0_gnn_ref(h, edge_index, edge_weight, edge_attr_16, L0_gnn_ew1, L0_gnn_eb1, L0_gnn_ew2, L0_gnn_eb2, L0_gnn_nw1, L0_gnn_nb1, L0_gnn_nw2, L0_gnn_nb2)
    h = jnp.maximum(_layernorm(x, axis=-1), 0.0)
    x = x + _L1_gnn_ref(h, edge_index, L1_gnn_W1, L1_gnn_a_src1, L1_gnn_a_dst1, L1_gnn_b1, L1_gnn_W2, L1_gnn_a_src2, L1_gnn_a_dst2, L1_gnn_b2)
    return x

_drawn_inputs = setup_inputs


def setup_inputs(seed=0):
    import zlib

    import numpy as np

    out = dict(_drawn_inputs(seed))
    spreads = {'L1_gnn_b1': (0.0, 0.1), 'L1_gnn_b2': (0.0, 0.1)}
    factors = {'edge_attr_16': 3.194,
     'edge_weight': 200.0,
     'L0_gnn_nb1': 6.772,
     'L1_gnn_a_src1': 22.065,
     'L1_gnn_a_dst1': 200.0,
     'L1_gnn_a_src2': 200.0,
     'L1_gnn_a_dst2': 200.0}
    for name, (base, spread) in spreads.items():
        noise = np.random.default_rng([zlib.crc32(name.encode()), seed]).standard_normal(out[name].shape)
        drawn = base * np.exp(spread * noise) if base else spread * noise
        out[name] = jnp.asarray(drawn.astype(out[name].dtype))
    for name, factor in factors.items():
        out[name] = (out[name] * factor).astype(out[name].dtype)
    return out
```

```python
import concourse.bass as bass
from concourse import mybir
from contextlib import ExitStack, contextmanager

F32 = mybir.dt.float32
BF16 = mybir.dt.bfloat16
I32 = mybir.dt.int32
ALU = mybir.AluOpType
ACT = mybir.ActivationFunctionType
AX = mybir.AxisListType

P = 128
N_NODES, N_EDGES = 6250, 206250
F_IN, F_HID, F_EDGE, CUTOFF = 64, 128, 16, 5.0
HEADS, CH, OUT_DIM, SLOPE = 4, 32, 64, 0.2
NT = -(-N_NODES // P)
NB = NT + 1
LANE_BITS = 7
COLS = -(-N_EDGES // P // 52) * 52
U = 4
GE = P * U
GE_BITS = 9
GROUPS = (N_EDGES + NT * (GE - 1)) // GE + 1
ROW_GROUPS = GROUPS + 2
BATCH = 26
REC = F_EDGE + 4
KX = F_IN + REC
BIG = float(2 ** 100)
PEEL = 8
UNROLL = 4
N_WEIGHTS = 19
LAYERS = ((HEADS, CH), (1, OUT_DIM))


class Group:

    def __init__(self, i, off, before):
        self.i, self.off, self.before = i, off, before
        self.at = off if i is None else i + off

    def slot(self, n):
        return self.off % n

    def done(self, per=1):
        n = per * (self.before + self.off + 1)
        return n if self.i is None else self.i * per + n

    def uses(self, slots, per):
        n = per * ((self.before + self.off) // slots + 1)
        return n if self.i is None else self.i * (per // slots) + n

    def back(self, n):
        return Group(self.i, self.off - n, self.before)

    def exists(self):
        return self.i is not None or self.off >= 0


def pipelined(eng, items, depth, step, before=0):
    def lookup(i, t):
        def group_of(stage):
            if i is None and not 0 <= t - stage < items:
                return None
            return Group(i, t - stage, before)
        return group_of

    for t in range(PEEL):
        step(lookup(None, t))
    rounds = (items - PEEL) // UNROLL
    with eng.Fori(0, rounds) as turn:
        i = turn * UNROLL + PEEL
        for k in range(UNROLL):
            step(lookup(i, k))
    for t in range(PEEL + rounds * UNROLL, items + depth):
        step(lookup(None, t))


class Chain:

    def __init__(self, eng, sem):
        self.eng, self.sem, self.count, self.shift = eng, sem, 0, 0

    def __call__(self, ins):
        self.count += 1
        ins.then_inc(self.sem, 1)
        self.eng.wait_ge(self.sem, self.shift + self.count)

    @contextmanager
    def loop(self, times, per):
        first = self.count
        with self.eng.Fori(0, times) as i:
            self.shift = i * per
            yield i
        assert self.count - first == per
        self.shift, self.count = 0, first + times * per


def gnn_kernel(nc, x, src, dst, attr, ew, ew1, eb1, ew2, eb2, nw1, nb1, nw2, nb2,
               W1, a_src1, a_dst1, b1, W2, a_src2, a_dst2, b2, out, dbg=None):
    ctx = ExitStack()
    with ctx:
        def sb(name, shape, dt=F32):
            return ctx.enter_context(nc.sbuf_tensor(name, shape, dt))[tuple(slice(None) for _ in shape)]

        def pb(name):
            return ctx.enter_context(nc.psum_tensor(name, [P, 512], F32))[:, :]

        def sem(name):
            return ctx.enter_context(nc.semaphore(name))

        def dram(name, shape, dt=F32):
            return nc.dram_tensor(name, shape, dt, kind="Internal").ap()

        rec_s = dram("rec_s", [ROW_GROUPS * GE, REC])
        rec_d = dram("rec_d", [ROW_GROUPS * GE, 2])
        h_table = dram("h_table", [NT * P, F_IN])
        tables = [dram(f"table{n}", [NT * P, h * (c + 1)]) for n, (h, c) in enumerate(LAYERS)]
        spills = [dram(f"spill{n}", [GROUPS * P, U * h * (c + 1)]) for n, (h, c) in enumerate(LAYERS)]

        xs = sb("xs", [P, NT, F_IN])
        hs = sb("hs", [P, NT, F_IN])
        acc = sb("acc", [P, NT * (F_HID + HEADS)])
        tab = sb("tab", [P, NT * (F_HID + HEADS)])
        alpha_s = sb("alpha_s", [P, NT * HEADS])
        alpha_d = sb("alpha_d", [P, NT * HEADS])
        seg_max = sb("seg_max", [P, NT * HEADS])
        own_e = sb("own_e", [P, NT * HEADS])
        parts = sb("parts", [P, NT * 3 * 2 * HEADS], BF16)
        both = sb("both", [P, NT * 2 * HEADS])
        stat = sb("stat", [P, 2, NT])
        ident = sb("ident", [P, P])
        ident_b = sb("ident_b", [P, P], BF16)
        neg_ident = sb("neg_ident", [P, P], BF16)
        lanes = sb("lanes", [P, P])
        lower = sb("lower", [P, P])
        ones = sb("ones", [P, P])
        ones3 = sb("ones3", [3, P], BF16)
        zero = sb("zero", [P, 1])
        w_edge = sb("w_edge", [KX, F_HID])
        w_own = sb("w_own", [F_IN, F_HID])
        w_mid = sb("w_mid", [F_HID, F_HID])
        b_mid = sb("b_mid", [1, F_HID])
        b_rest = sb("b_rest", [1, F_HID])
        b_part = sb("b_part", [1, 3, F_HID], BF16)
        b_rows = sb("b_rows", [3, F_HID], BF16)
        w_node_h = sb("w_node_h", [F_IN, F_HID])
        w_node_a = sb("w_node_a", [F_HID, F_HID])
        w_out = sb("w_out", [F_HID, F_IN])
        nb1_col = sb("nb1_col", [F_HID, 1])
        nb2_row = sb("nb2_row", [P, F_IN])
        gat_w = [sb("gat_w1", [F_IN, F_HID]), sb("gat_w2", [F_HID, OUT_DIM])]
        att_s = [sb("att_s1", [P, F_HID]), sb("att_s2", [P, OUT_DIM])]
        att_d = [sb("att_d1", [P, F_HID]), sb("att_d2", [P, OUT_DIM])]
        gat_b = [sb("gat_b1", [P, F_HID]), sb("gat_b2", [P, OUT_DIM])]
        bucket_of = [sb(f"bucket_of{k}", [1, ROW_GROUPS], I32) for k in range(2)]
        group_no = sb("group_no", [1, ROW_GROUPS])
        bucket_f = sb("bucket_f", [1, ROW_GROUPS])
        counts = sb("counts", [P, NB])
        n_groups_i = sb("n_groups_i", [P, NB], I32)
        n_groups = sb("n_groups", [P, NB])
        first_group = sb("first_group", [P, NB])
        base = sb("base", [P, NB])
        tile_in = sb("tile_in", [P, 2, F_IN + F_HID])
        tile_t = sb("tile_t", [P, 2, 2, P])
        mid_t = sb("mid_t", [P, 2, P])
        ARENA = 21300
        arena = sb("arena", [P, ARENA])

        def carve(start, shape, dt=F32):
            words = 1
            for n in shape:
                words *= n
            words = words if dt != BF16 else words // 2
            v = arena[:, start:start + words]
            assert start + words <= ARENA, (start, shape)
            if dt != F32:
                v = v.bitcast(dt)
            names = " ".join("abcd"[:len(shape)])
            kw = {"abcd"[n]: shape[n] for n in range(len(shape))}
            return v.rearrange(f"p ({names}) -> p {names}", **kw), start + words

        at = 0
        src_i, at = carve(at, [COLS], I32)
        dst_i, at = carve(at, [COLS], I32)
        weight, at = carve(at, [COLS])
        bucket, at = carve(at, [COLS])
        lane_s, at = carve(at, [COLS])
        lane_d, at = carve(at, [COLS])
        pos_s, at = carve(at, [COLS], I32)
        pos_d, at = carve(at, [COLS], I32)
        pos_f, at = carve(at, [COLS])
        hit, at = carve(at, [COLS])
        rank, at = carve(at, [COLS])
        dst_c, at = carve(at, [COLS], I32)
        attr_in = [None, None]
        rec_out = [None, None]
        rec2_out = [sb(f"rec2_out{k}", [P, BATCH, 2]) for k in range(2)]
        where = [sb(f"where{k}", [P, BATCH], I32) for k in range(2)]
        for k in range(2):
            rec_out[k], at = carve(at, [BATCH, REC])
            attr_in[k], at = carve(at, [BATCH, F_EDGE])
        FILL = 227
        assert ROW_GROUPS * GE % (P * FILL) == 0
        blank_s = acc[:, 0:FILL * REC].rearrange("p (r w) -> p r w", w=REC)
        blank_d = acc[:, FILL * REC:FILL * (REC + 2)].rearrange("p (r w) -> p r w", w=2)

        at = 0
        own_parts, at = carve(at, [NT, 3, F_HID], BF16)
        xg, at = carve(at, [2, U, KX])
        hot, at = carve(at, [4, U, P], BF16)
        hot_f, at = carve(at, [4, U, P])
        hot_t, at = carve(at, [2, GE], BF16)
        x_t, at = carve(at, [2, GE])
        mid_e, at = carve(at, [2, GE])
        msg, at = carve(at, [2, U, F_HID])
        at = 0
        a_hot, at = carve(at, [4, U, P], BF16)
        a_hot_f, at = carve(at, [4, U, P])
        a_hot_t, at = carve(at, [2, GE], BF16)
        miss, at = carve(at, [4, U, P], BF16)
        ids, at = carve(at, [4, U, 2])
        logit, at = carve(at, [2, U * HEADS])
        logit2, at = carve(at, [2, U * HEADS])
        tile_max, at = carve(at, [2, U * HEADS])
        group_max, at = carve(at, [2, HEADS])
        g_rows, at = carve(at, [4, U * (F_HID + HEADS)])
        g_msg, at = carve(at, [2, U * (F_HID + HEADS)])

        ps = [pb(f"ps{n}") for n in range(8)]

        s = {}

        def S(name):
            if name not in s:
                s[name] = sem(name)
            return s[name]

        agg = acc[:, 0:NT * F_HID].rearrange("p (t f) -> p t f", f=F_HID)

        block = ctx.enter_context(nc.Block())

        def bucket_reg(eng, order, g):
            return eng.value_load(bucket_of[order][0:1, bass.ds(g.at, 1)], min_val=0, max_val=NT - 1)

        @block.sync
        def _(sp):
            sp.dma_start(src_i, src.rearrange("(p j) -> p j", p=P)).then_inc(S("src_in"), 16)
            sp.dma_start(dst_i, dst.rearrange("(p j) -> p j", p=P)).then_inc(S("dst_in"), 16)
            sp.dma_start(weight, ew.rearrange("(p j) -> p j", p=P)).then_inc(S("weight_in"), 16)
            sp.dma_start(xs, x.rearrange("(t p) f -> p t f", p=P)).then_inc(S("x_in"), 16)
            loads = [
                (w_own, ew1[0:F_IN, :]), (w_edge[0:F_IN, :], ew1[F_IN:2 * F_IN, :]),
                (w_edge[F_IN:F_IN + F_EDGE + 1, :], ew1[2 * F_IN:, :]),
                (w_edge[KX - 1:KX, :], eb1.rearrange("(a n) -> a n", a=1)),
                (w_mid, ew2), (b_mid, eb2.rearrange("(a n) -> a n", a=1)),
                (w_node_h, nw1[0:F_IN, :]), (w_node_a, nw1[F_IN:, :]), (w_out, nw2),
                (nb1_col, nb1.rearrange("(n a) -> n a", a=1)),
                (nb2_row, nb2.rearrange("(a n) -> a n", a=1).broadcast_to([P, F_IN])),
                (gat_w[0], W1), (gat_w[1], W2),
                (gat_b[0], b1.rearrange("(a n) -> a n", a=1).broadcast_to([P, F_HID])),
                (gat_b[1], b2.rearrange("(a n) -> a n", a=1).broadcast_to([P, OUT_DIM])),
                (att_s[0], a_src1.rearrange("a h c -> a (h c)").broadcast_to([P, F_HID])),
                (att_s[1], a_src2.rearrange("a h c -> a (h c)").broadcast_to([P, OUT_DIM])),
                (att_d[0], a_dst1.rearrange("a h c -> a (h c)").broadcast_to([P, F_HID])),
                (att_d[1], a_dst2.rearrange("a h c -> a (h c)").broadcast_to([P, OUT_DIM])),
            ]
            assert len(loads) == N_WEIGHTS
            sp.wait_ge(S("zero_ready"), 1)
            for to, what in loads:
                sp.dma_start(to, what).then_inc(S("weights_in"), 16)
            sp.wait_ge(S("blank_ready"), 2)
            n = ROW_GROUPS * GE // (P * FILL)
            to_s = rec_s.rearrange("(p n r) w -> n p (r w)", p=P, n=n)
            to_d = rec_d.rearrange("(p n r) w -> n p (r w)", p=P, n=n)
            for k in range(n):
                sp.dma_start(to_s[k], blank_s.rearrange("p r w -> p (r w)")).then_inc(S("blank_s_out"), 16)
            for k in range(n):
                sp.dma_start(to_d[k], blank_d.rearrange("p r w -> p (r w)")).then_inc(S("blank_d_out"), 16)
            at_v = attr.rearrange("(p j) f -> p (j f)", p=P)
            with sp.Fori(0, COLS // BATCH // 2) as i:
                for k in range(2):
                    sp.wait_ge(S("attr_used"), 2 * i + k + 1)
                    sp.dma_start(attr_in[k].rearrange("p u w -> p (u w)"),
                                 at_v[:, bass.ds((2 * i + k) * (BATCH * F_EDGE), BATCH * F_EDGE)]
                                 ).then_inc(S(f"attr_in{k}"), 16)
            sp.wait_ge(S("h_ready"), 1)
            sp.dma_start(h_table.rearrange("(t p) f -> p t f", p=P), hs).then_inc(S("h_table_out"), 16)

            sp.wait_ge(S("b_part_ready"), 1)
            sp.dma_start(b_rows, b_part.rearrange("a k f -> a (k f)")).then_inc(S("b_rows_in"), 16)

            sp.wait_ge(S("sorted_s"), 1)
            sp.wait_ge(S("arena_free"), 1)
            rs = rec_s.rearrange("(g p u) w -> g p u w", p=P, u=U)

            def load_records(of):
                g = of(0)
                if g is None:
                    return
                if g.back(2).exists():
                    sp.wait_ge(S("x_transposed"), g.back(2).done())
                    sp.wait_ge(S("hot_ready"), g.back(2).done())
                sp.dma_start(xg[:, g.slot(2), :, F_IN:KX], rs[bass.ds(g.at, 1)].rearrange("a p u w -> p (a u) w")
                             ).then_inc(S(f"rec_in{g.slot(2)}"), 16)

            pipelined(sp, GROUPS, 0, load_records)

            rd = rec_d.rearrange("(g p u) w -> g p (u w)", p=P, u=U)
            for n, (heads, ch) in enumerate(LAYERS):
                row = heads * (ch + 1)
                sp.wait_ge(S("table_ready"), n + 1)
                sp.dma_start(tables[n].rearrange("(t p) f -> p t f", p=P),
                             tab[:, 0:NT * row].rearrange("p (t f) -> p t f", f=row)).then_inc(S("table_out"), 16)
                if n == 0:
                    sp.wait_ge(S("sorted_d"), 1)
                    sp.wait_ge(S("mlp_done"), 1)
                spill = spills[n].rearrange("(g p) w -> g p w", p=P)

                def maxima(of):
                    g = of(0)
                    if g is not None:
                        if g.back(4).exists():
                            sp.wait_ge(S("miss_ready"), g.back(4).done())
                            for k in (g.slot(4),):
                                sp.wait_ge(S(f"gathered_{k}"), g.back(4).uses(4, 16 * U))
                        sp.dma_start(ids[:, g.slot(4), :, :].rearrange("p u w -> p (u w)"),
                                     rd[bass.ds(g.at, 1)].rearrange("a p w -> p (a w)")
                                     ).then_inc(S(f"ids_in_{g.slot(4)}"), 16)
                    g = of(1)
                    if g is not None:
                        sp.wait_ge(S(f"gathered_{g.slot(4)}"), g.uses(4, 16 * U))
                        sp.dma_start(spill[bass.ds(g.at, 1)].rearrange("a p w -> p (a w)"),
                                     g_rows[:, g.slot(4), 0:U * row]).then_inc(S(f"spilled_{g.slot(4)}"), 16)

                pipelined(sp, GROUPS, 1, maxima, n * GROUPS)
                for k in range(4):
                    sp.wait_ge(S(f"spilled_{k}"), 16 * (n + 1) * (GROUPS // 4))
                sp.wait_ge(S("maxima_done"), n + 1)

                def weighted(of):
                    g = of(0)
                    if g is None:
                        return
                    if g.back(4).exists():
                        sp.wait_ge(S("a_hot_ready"), g.back(4).done())
                        sp.wait_ge(S("msg_ready"), g.back(4).done())
                    sp.dma_start(ids[:, g.slot(4), :, :].rearrange("p u w -> p (u w)"),
                                 rd[bass.ds(g.at, 1)].rearrange("a p w -> p (a w)")
                                 ).then_inc(S(f"ids2_in_{g.slot(4)}"), 16)
                    sp.dma_start(g_rows[:, g.slot(4), 0:U * row], spill[bass.ds(g.at, 1)].rearrange("a p w -> p (a w)")
                                 ).then_inc(S(f"rows_in_{g.slot(4)}"), 16)

                pipelined(sp, GROUPS, 0, weighted, n * GROUPS)

            sp.wait_ge(S("out_ready"), 1)
            sp.dma_start(out.rearrange("(t p) f -> p t f", p=P), hs).then_inc(S("out_done"), 16)
            sp.wait_ge(S("out_done"), 16)

        @block.gpsimd
        def _(pool):
            pool.memset(ident, 0.0).then_inc(S("const0"), 1)
            pool.memset(lower, 1.0).then_inc(S("const0"), 1)
            pool.memset(ones, 1.0).then_inc(S("const0"), 1)
            pool.memset(tile_in, 0.0).then_inc(S("const0"), 1)
            pool.wait_ge(S("const0"), 4)
            pool.affine_select(out=ident, in_=ident, compare_op=ALU.not_equal, fill=1.0, base=0,
                               pattern=[[-1, P]], channel_multiplier=1).then_inc(S("const1"), 1)
            pool.affine_select(out=lower, in_=lower, compare_op=ALU.is_gt, fill=0.0, base=0,
                               pattern=[[1, P]], channel_multiplier=-1).then_inc(S("const1"), 1)
            pool.iota(lanes, [[1, P]], base=0, channel_multiplier=0,
                      allow_small_or_imprecise_dtypes=True).then_inc(S("const1"), 1)
            pool.iota(group_no, [[1, ROW_GROUPS]], base=0, channel_multiplier=0,
                      allow_small_or_imprecise_dtypes=True).then_inc(S("const1"), 1)
            pool.memset(blank_s, 0.0).then_inc(S("blank0"), 1)
            pool.memset(blank_d, 0.0).then_inc(S("blank0"), 1)
            for k in range(2):
                pool.memset(rec_out[k][:, :, REC - 1:REC], 1.0).then_inc(S("blank0"), 1)
            pool.wait_ge(S("blank0"), 4)
            pool.memset(blank_s[:, :, REC - 3:REC - 2], -1.0).then_inc(S("blank_ready"), 1)
            pool.memset(blank_d[:, :, 0:1], -1.0).then_inc(S("blank_ready"), 1)

            def tile_inputs(ready, count, name, sources, transposed, before=0):
                pool.wait_ge(S(ready), count)

                def copy(of):
                    g = of(0)
                    if g is None:
                        return
                    if g.back(2).exists():
                        pool.wait_ge(S(transposed), g.back(2).done())
                    at = 0
                    for rows, width in sources:
                        pool.tensor_copy(tile_in[:, g.slot(2), at:at + width],
                                         rows[:, bass.ds(g.at, 1), 0:width].rearrange("p a f -> p (a f)")
                                         ).then_inc(S(name), 1)
                        at += width

                pipelined(pool, NT, 0, copy, before)

            fills = ROW_GROUPS * GE // (P * FILL)
            for name, rows, bufs in (("s", rec_s, rec_out), ("d", rec_d, rec2_out)):
                pool.wait_ge(S(f"blank_{name}_out"), 16 * fills)
                with pool.Fori(0, COLS // BATCH // 2) as i:
                    for k in range(2):
                        pool.wait_ge(S(f"staged_{name}"), 2 * i + k + 1)
                        pool.sem_inc(S("pool_go"), 1)
                        for c in range(BATCH):
                            pool.indirect_dma_start(
                                rows, bass.IndirectOffsetOnAxis(ap=where[k][:, c:c + 1], axis=0),
                                bufs[k][:, c, :], None).then_inc(S(f"sorted_{name}_slot{k}"), 16)
                for k in range(2):
                    pool.wait_ge(S(f"sorted_{name}_slot{k}"), 16 * COLS // 2)
                pool.sem_inc(S(f"sorted_{name}"), 1)

            tile_inputs("h_ready", 1, "own_in", [(hs, F_IN)], "own_t")
            pool.wait_ge(S("h_table_out"), 16)
            pool.wait_ge(S("arena_free"), 1)

            def gather_h(of):
                g = of(0)
                if g is None:
                    return
                pool.wait_ge(S(f"rec_in{g.slot(2)}"), g.uses(2, 16))
                pool.sem_inc(S("pool_go"), 1)
                for u in range(U):
                    pool.indirect_dma_start(
                        xg[:, g.slot(2), u, 0:F_IN], None, h_table,
                        bass.IndirectOffsetOnAxis(
                            ap=xg[:, g.slot(2), u, KX - 2:KX - 1].bitcast(I32), axis=0)
                    ).then_inc(S(f"h_in{g.slot(2)}"), 16)

            pipelined(pool, GROUPS, 0, gather_h)

            tile_inputs("mlp_done", 1, "node_in", [(hs, F_IN), (agg, F_HID)], "node_t")
            for n, (heads, ch) in enumerate(LAYERS):
                row = heads * (ch + 1)
                if n == 0:
                    tile_inputs("gat_in", 1, "gat_x", [(hs, F_IN)], "gat_t")
                else:
                    tile_inputs("gat_in", 2, "gat_x", [(acc.rearrange("p (t f) -> p t f", t=NT), F_HID)], "gat_t", NT)
                pool.wait_ge(S("table_out"), 16 * (n + 1))

                def gather_rows(of):
                    g = of(0)
                    if g is None:
                        return
                    if g.back(4).exists():
                        pool.wait_ge(S(f"spilled_{g.slot(4)}"), g.back(4).uses(4, 16))
                        pool.wait_ge(S("shown"), g.back(4).done())
                    pool.wait_ge(S(f"ids_in_{g.slot(4)}"), g.uses(4, 16))
                    pool.sem_inc(S("pool_go"), 1)
                    for u in range(U):
                        pool.indirect_dma_start(
                            g_rows[:, g.slot(4), u * row:(u + 1) * row], None, tables[n],
                            bass.IndirectOffsetOnAxis(ap=ids[:, g.slot(4), u, 1:2].bitcast(I32), axis=0)
                        ).then_inc(S(f"gathered_{g.slot(4)}"), 16)

                pipelined(pool, GROUPS, 0, gather_rows, n * GROUPS)

        @block.scalar
        def _(act):
            act.sem_inc(S("attr_used"), 2)
            for name, pos, bufs in (("s", pos_s, rec_out), ("d", pos_d, rec2_out)):
                act.wait_ge(S(f"pos_ready_{name}"), 1)
                if name == "s":
                    act.wait_ge(S("weight_in"), 16)

                def stage(i):
                    for k in range(2):
                        cols = bass.ds((2 * i + k) * BATCH, BATCH)
                        if not (isinstance(i, int) and i == 0):
                            act.wait_ge(S(f"sorted_{name}_slot{k}"), i * (16 * BATCH))
                        if name == "s":
                            act.activation(bufs[k][:, :, F_EDGE], weight[:, cols], ACT.Copy, scale=1.0 / CUTOFF).then_inc(S(f"staging_{name}"), 1)
                            act.activation(bufs[k][:, :, F_EDGE + 1], lane_s[:, cols], ACT.Copy).then_inc(S(f"staging_{name}"), 1)
                            act.activation(bufs[k][:, :, F_EDGE + 2].bitcast(I32), dst_c[:, cols], ACT.Copy).then_inc(S(f"staging_{name}"), 1)
                            act.wait_ge(S(f"attr_in{k}"), 16 * i + 16)
                            act.activation(bufs[k][:, :, 0:F_EDGE], attr_in[k], ACT.Copy).then_inc(S("attr_used"), 1)
                        else:
                            act.activation(bufs[k][:, :, 0], lane_d[:, cols], ACT.Copy).then_inc(S(f"staging_{name}"), 1)
                            act.activation(bufs[k][:, :, 1].bitcast(I32), src_i[:, cols], ACT.Copy).then_inc(S(f"staging_{name}"), 1)
                        act.activation(where[k], pos[:, cols], ACT.Copy).then_inc(S(f"staging_{name}"), 1)
                        per = 4 if name == "s" else 3
                        if name == "s":
                            act.wait_ge(S("attr_used"), 2 * i + k + 3)
                        act.wait_ge(S(f"staging_{name}"), i * (2 * per) + per * (k + 1))
                        act.sem_inc(S(f"staged_{name}"), 1)

                stage(0)
                with act.Fori(1, COLS // BATCH // 2) as i:
                    stage(i)
                if name == "s":
                    act.wait_ge(S("sorted_s"), 1)
            act.wait_ge(S("sorted_d"), 1)
            act.sem_inc(S("arena_free"), 1)

            act.wait_ge(S("var_ready"), 1)
            act.activation(stat[:, 1, :], stat[:, 1, :], ACT.Sqrt).then_inc(S("std_ready"), 1)

            def own_tiles(of):
                g = of(0)
                if g is not None:
                    if g.back(2).exists():
                        act.wait_ge(S("own_done"), g.back(2).done())
                    act.wait_ge(S("own_t"), g.done())
                    act.activation(tile_t[0:F_IN, g.slot(2), 0, :], ps[g.slot(2)][0:F_IN, 0:P], ACT.Copy).then_inc(S("own_tt"), 1)

            pipelined(act, NT, 0, own_tiles)

            def edge_mlp(of):
                g = of(0)
                if g is not None:
                    act.wait_ge(S("hot_ready"), g.done())
                    if g.back(4).exists():
                        act.wait_ge(S("summed"), g.back(4).done())
                    act.activation(hot_f[:, g.slot(4)], hot[:, g.slot(4)], ACT.Copy).then_inc(S("hot_f_ready"), 1)
                    act.wait_ge(S("x_transposed"), g.done())
                    if g.back(2).exists():
                        act.wait_ge(S("hidden1"), g.back(2).done())
                    act.activation(x_t[0:KX, g.slot(2), :], ps[0][0:KX, :], ACT.Copy).then_inc(S("x_t_ready"), 1)
                g = of(1)
                if g is not None:
                    act.wait_ge(S("hidden1"), g.done())
                    if g.back(2).exists():
                        act.wait_ge(S("hidden2"), g.back(2).done())
                    act.activation(mid_e[:, g.slot(2), :], ps[2 + g.slot(2)][:, :], ACT.Silu).then_inc(S("mid_ready"), 1)
                g = of(2)
                if g is not None:
                    act.wait_ge(S("hidden2"), g.done())
                    if g.back(2).exists():
                        act.wait_ge(S("summed"), g.back(2).done())
                    act.activation(msg[:, g.slot(2)].rearrange("p u f -> p (u f)"), ps[4 + g.slot(2)][:, :], ACT.Silu).then_inc(S("message_ready"), 1)

            pipelined(act, GROUPS, 2, edge_mlp)

            def node_mlp(of):
                g = of(0)
                if g is not None:
                    act.wait_ge(S("node_t"), g.done())
                    if g.back(2).exists():
                        act.wait_ge(S("node_mid"), g.back(2).done())
                    act.activation(tile_t[0:F_IN, g.slot(2), 0, :], ps[g.slot(2)][0:F_IN, 0:P], ACT.Copy).then_inc(S("node_tt"), 1)
                    act.activation(tile_t[:, g.slot(2), 1, :], ps[g.slot(2)][:, P:2 * P], ACT.Copy).then_inc(S("node_tt"), 1)
                g = of(1)
                if g is not None:
                    act.wait_ge(S("node_mid"), g.done())
                    if g.back(2).exists():
                        act.wait_ge(S("node_out"), g.back(2).done())
                    act.activation(mid_t[:, g.slot(2), :], ps[2 + g.slot(2)][:, 0:P], ACT.Silu, bias=nb1_col).then_inc(S("node_act"), 1)

            pipelined(act, NT, 1, node_mlp)
            act.wait_ge(S("var_ready"), 2)
            act.activation(stat[:, 1, :], stat[:, 1, :], ACT.Sqrt).then_inc(S("std_ready"), 1)

            for n, (heads, ch) in enumerate(LAYERS):
                row = heads * (ch + 1)
                k_in = F_IN if n == 0 else F_HID

                def gat_tiles(of):
                    g = of(0)
                    if g is not None:
                        act.wait_ge(S("gat_t"), g.done())
                        if g.back(2).exists():
                            act.wait_ge(S("gat_mm"), g.back(2).done())
                        act.activation(tile_t[0:k_in, g.slot(2), 0, :], ps[g.slot(2)][0:k_in, 0:P], ACT.Copy).then_inc(S("gat_tt"), 1)

                pipelined(act, NT, 0, gat_tiles, n * NT)

                act.wait_ge(S("own_logit"), n + 1)
                act.activation(own_e[:, 0:NT * heads], own_e[:, 0:NT * heads], ACT.Exp).then_inc(S("own_exp"), 1)

                def weights(of):
                    g = of(0)
                    if g is not None:
                        act.wait_ge(S("a_hot_ready"), g.done())
                        if g.back(4).exists():
                            act.wait_ge(S("a_summed"), g.back(4).done())
                        act.activation(a_hot_f[:, g.slot(4)], a_hot[:, g.slot(4)], ACT.Copy).then_inc(S("a_hot_f_ready"), 1)
                    g = of(1)
                    if g is not None:
                        act.wait_ge(S("logit_ready"), g.done())
                        if g.back(2).exists():
                            act.wait_ge(S("a_summed"), g.back(2).done())
                        m = g_msg[:, g.slot(2), 0:U * row].rearrange("p (u w) -> p u w", u=U)
                        act.activation(m[:, :, heads * ch:row], logit[:, g.slot(2), 0:U * heads].rearrange("p (u h) -> p u h", u=U), ACT.Exp).then_inc(S("exp_ready"), 1)

                pipelined(act, GROUPS, 1, weights, n * GROUPS)

        @block.tensor
        def _(pe):
            pe.wait_ge(S("const1"), 4)
            for k in range(2):
                pe.wait_ge(S("counts_ready"), k + 1)
                pe.matmul(ps[7][:, 0:NB], lower, counts, start=True, stop=True)
                pe.matmul(ps[7][:, 256:256 + NB], ones, counts, start=True, stop=True).then_inc(S("prefix_ready"), 1)

            pe.wait_ge(S("weights_in"), 16 * N_WEIGHTS)
            pe.wait_ge(S("h_ready"), 1)

            def own_tiles(of):
                g = of(0)
                if g is not None:
                    if g.back(2).exists():
                        pe.wait_ge(S("own_tt"), g.back(2).done())
                    pe.wait_ge(S("own_in"), g.done())
                    pe.transpose(ps[g.slot(2)][:, 0:P], tile_in[:, g.slot(2), 0:P], ident).then_inc(S("own_t"), 1)
                g = of(1)
                if g is not None:
                    pe.wait_ge(S("own_tt"), g.done())
                    if g.back(2).exists():
                        pe.wait_ge(S("own_copied"), g.back(2).done())
                    pe.matmul(ps[2 + g.slot(2)][:, 0:F_HID], tile_t[0:F_IN, g.slot(2), 0, :], w_own, start=True, stop=True).then_inc(S("own_done"), 1)

            pipelined(pe, NT, 1, own_tiles)

            pe.wait_ge(S("own_parts_ready"), 1)
            pe.wait_ge(S("b_rows_in"), 16)

            def edge_mlp(of):
                g = of(0)
                if g is not None:
                    r = g.slot(2)
                    pe.wait_ge(S(f"h_in{r}"), g.uses(2, 16 * U))
                    if g.back(1).exists():
                        pe.wait_ge(S("x_t_ready"), g.back(1).done())
                    for u in range(U):
                        mm = pe.transpose(ps[0][0:KX, u * P:(u + 1) * P], xg[:, r, u, :], ident)
                    mm.then_inc(S("x_transposed"), 1)
                    pe.wait_ge(S("hot_ready"), g.done())
                    if g.back(1).exists():
                        pe.wait_ge(S("hot_t_ready"), g.back(1).done())
                    for u in range(U):
                        mm = pe.transpose(ps[1][:, 0:GE // 2].bitcast(BF16)[:, u * P:(u + 1) * P], hot[:, g.slot(4), u, :], ident_b)
                    mm.then_inc(S("hot_transposed"), 1)
                g = of(1)
                if g is not None:
                    r = g.slot(2)
                    b = bucket_reg(pe, 0, g)
                    pe.wait_ge(S("x_t_ready"), g.done())
                    if g.back(2).exists():
                        pe.wait_ge(S("mid_ready"), g.back(2).done())
                    pe.matmul(ps[2 + r][:, :], w_edge, x_t[0:KX, r, :], start=True, stop=False)
                    pe.wait_ge(S("hot_t_ready"), g.done())
                    for part in range(3):
                        mm = pe.matmul(ps[2 + r][:, :], own_parts[:, bass.ds(b, 1), part, :].rearrange("p a f -> p (a f)"), hot_t[:, r, :],
                                       start=False, stop=(part == 2))
                    mm.then_inc(S("hidden1"), 1)
                g = of(2)
                if g is not None:
                    r = g.slot(2)
                    pe.wait_ge(S("mid_ready"), g.done())
                    if g.back(2).exists():
                        pe.wait_ge(S("message_ready"), g.back(2).done())
                    for u in range(U):
                        pe.matmul(ps[4 + r][:, u * P:(u + 1) * P], mid_e[:, r, u * P:(u + 1) * P], w_mid,
                                  start=(u == 0), stop=False, skip_group_check=True)
                    mm = pe.matmul(ps[4 + r][:, :].rearrange("p (u f) -> p u f", u=U), ones3,
                                   b_rows.unsqueeze(1).broadcast_to([3, U, F_HID]), start=False, stop=True,
                                   skip_group_check=True)
                    mm.then_inc(S("hidden2"), 1)
                g = of(3)
                if g is not None:
                    r = g.slot(2)
                    pe.wait_ge(S("message_ready"), g.done())
                    pe.wait_ge(S("hot_f_ready"), g.done())
                    if g.back(2).exists():
                        pe.wait_ge(S("added"), g.back(2).done())
                    for u in range(U):
                        mm = pe.matmul(ps[6 + r][:, 0:F_HID], hot_f[:, g.slot(4), u, :], msg[:, r, u, :],
                                       start=(u == 0), stop=(u == U - 1))
                    mm.then_inc(S("summed"), 1)

            pipelined(pe, GROUPS, 3, edge_mlp)

            pe.wait_ge(S("added"), GROUPS)

            def node_mlp(of):
                g = of(0)
                if g is not None:
                    r = g.slot(2)
                    if g.back(2).exists():
                        pe.wait_ge(S("node_tt"), g.back(2).done(2))
                    pe.wait_ge(S("node_in"), g.done(2))
                    pe.transpose(ps[r][:, 0:P], tile_in[:, r, 0:P], ident)
                    pe.transpose(ps[r][:, P:2 * P], tile_in[:, r, F_IN:], ident).then_inc(S("node_t"), 1)
                g = of(1)
                if g is not None:
                    r = g.slot(2)
                    pe.wait_ge(S("node_tt"), g.done(2))
                    if g.back(2).exists():
                        pe.wait_ge(S("node_act"), g.back(2).done())
                    pe.matmul(ps[2 + r][:, 0:P], w_node_h, tile_t[0:F_IN, r, 0, :], start=True, stop=False)
                    pe.matmul(ps[2 + r][:, 0:P], w_node_a, tile_t[:, r, 1, :], start=False, stop=True).then_inc(S("node_mid"), 1)
                g = of(2)
                if g is not None:
                    r = g.slot(2)
                    pe.wait_ge(S("node_act"), g.done())
                    if g.back(2).exists():
                        pe.wait_ge(S("node_added"), g.back(2).done())
                    pe.matmul(ps[4 + r][:, 0:F_IN], mid_t[:, r, :], w_out, start=True, stop=True).then_inc(S("node_out"), 1)

            pipelined(pe, NT, 2, node_mlp)

            for n, (heads, ch) in enumerate(LAYERS):
                row, width = heads * (ch + 1), heads * ch
                k_in = F_IN if n == 0 else F_HID

                def gat_tiles(of):
                    g = of(0)
                    if g is not None:
                        if g.back(2).exists():
                            pe.wait_ge(S("gat_tt"), g.back(2).done())
                        pe.wait_ge(S("gat_x"), g.done())
                        pe.transpose(ps[g.slot(2)][:, 0:P], tile_in[:, g.slot(2), 0:P], ident).then_inc(S("gat_t"), 1)
                    g = of(1)
                    if g is not None:
                        pe.wait_ge(S("gat_tt"), g.done())
                        if g.back(2).exists():
                            pe.wait_ge(S("gat_copied"), g.back(2).done())
                        pe.matmul(ps[2 + g.slot(2)][:, 0:width], tile_t[0:k_in, g.slot(2), 0, :], gat_w[n], start=True, stop=True).then_inc(S("gat_mm"), 1)

                pipelined(pe, NT, 1, gat_tiles, n * NT)

                def maxima(of):
                    g = of(1)
                    if g is None:
                        return
                    pe.wait_ge(S("miss_ready"), g.done())
                    pe.wait_ge(S(f"gathered_{g.slot(4)}"), g.uses(4, 16 * U))
                    rows = g_rows[:, g.slot(4), 0:U * row].rearrange("p (u w) -> p u w", u=U)
                    for u in range(U):
                        bank = ps[4 * g.slot(2) + u]
                        if g.back(2).exists() and u == 0:
                            pe.wait_ge(S("tile_max"), g.back(2).done())
                        for h in range(heads):
                            pe.matmul(bank[:, h * P:(h + 1) * P],
                                      rows[:, u, width + h:width + h + 1].broadcast_to([P, P]), ident,
                                      start=(h == 0), stop=False, skip_group_check=True)
                        mm = pe.matmul(bank[:, 0:heads * P].rearrange("p (h e) -> p h e", h=heads), miss[:, g.slot(4), u, :],
                                       neg_ident.unsqueeze(1).broadcast_to([P, heads, P]), start=False, stop=True,
                                       skip_group_check=True)
                    mm.then_inc(S("shown"), 1)

                pipelined(pe, GROUPS, 1, maxima, n * GROUPS)

                pe.wait_ge(S("parts_ready"), n + 1)
                pt = parts[:, 0:NT * 6 * heads].rearrange("p (t k w) -> p t k w", t=NT, k=3)

                def weights(of):
                    g = of(0)
                    if g is not None:
                        pe.wait_ge(S("a_hot_ready"), g.done())
                        if g.back(1).exists():
                            pe.wait_ge(S("a_hot_t_ready"), g.back(1).done())
                        for u in range(U):
                            mm = pe.transpose(ps[0][:, 0:GE // 2].bitcast(BF16)[:, u * P:(u + 1) * P], a_hot[:, g.slot(4), u, :], ident_b)
                        mm.then_inc(S("a_hot_transposed"), 1)
                    g = of(1)
                    if g is not None:
                        r = g.slot(2)
                        b = bucket_reg(pe, 1, g)
                        pe.wait_ge(S("a_hot_t_ready"), g.done())
                        if g.back(2).exists():
                            pe.wait_ge(S("logit_ready"), g.back(2).done())
                        for u in range(U):
                            for part in range(3):
                                mm = pe.matmul(ps[2 + r][:, u * 2 * heads:(u + 1) * 2 * heads], a_hot_t[:, r, u * P:(u + 1) * P],
                                               pt[:, bass.ds(b, 1), part, :].rearrange("p a w -> p (a w)"),
                                               start=(part == 0), stop=(part == 2))
                        mm.then_inc(S("looked_up"), 1)
                    g = of(2)
                    if g is not None:
                        r = g.slot(2)
                        pe.wait_ge(S("a_hot_f_ready"), g.done())
                        pe.wait_ge(S("exp_ready"), g.done())
                        pe.wait_ge(S("msg_ready"), g.done())
                        if g.back(2).exists():
                            pe.wait_ge(S("a_added"), g.back(2).done())
                        for u in range(U):
                            mm = pe.matmul(ps[4 + r][:, 0:row], a_hot_f[:, g.slot(4), u, :], g_msg[:, r, u * row:(u + 1) * row],
                                           start=(u == 0), stop=(u == U - 1))
                        mm.then_inc(S("a_summed"), 1)

                pipelined(pe, GROUPS, 2, weights, n * GROUPS)

        @block.vector
        def _(dve):
            link = Chain(dve, S("dve_step"))
            link(dve.memset(zero, 0.0))
            link(dve.memset(w_edge, 0.0))
            dve.sem_inc(S("zero_ready"), 1)
            dve.wait_ge(S("const1"), 4)
            link(dve.tensor_copy(ident_b, ident))
            link(dve.tensor_scalar(neg_ident, ident, -BIG, None, ALU.mult))
            link(dve.memset(ones3, 1.0))

            for order, (name, key, lane, pos) in enumerate((("s", src_i, lane_s, pos_s), ("d", dst_i, lane_d, pos_d))):
                dve.wait_ge(S("src_in" if order == 0 else "dst_in"), 16)
                link(dve.tensor_scalar(rank.bitcast(I32), key, LANE_BITS, None, ALU.arith_shift_right))
                link(dve.tensor_copy(bucket, rank.bitcast(I32)))
                link(dve.tensor_scalar(rank.bitcast(I32), key, P - 1, None, ALU.bitwise_and))
                link(dve.tensor_copy(hit, rank.bitcast(I32)))
                link(dve.tensor_scalar(lane, bucket, float(NT), None, ALU.is_ge))
                link(dve.tensor_tensor(lane, hit, lane, ALU.subtract))
                with link.loop(NB, 1) as b:
                    link(dve.tensor_scalar(hit, bucket, lanes[:, bass.ds(b, 1)], None, ALU.is_equal, ALU.add,
                                           accum_out=counts[:, bass.ds(b, 1)]))
                dve.sem_inc(S("counts_ready"), 1)
                dve.wait_ge(S("prefix_ready"), order + 1)
                link(dve.tensor_scalar(n_groups_i, ps[7][:, 256:256 + NB], float(GE - 1), None, ALU.add))
                link(dve.tensor_scalar(n_groups_i, n_groups_i, GE_BITS, None, ALU.arith_shift_right))
                link(dve.tensor_copy(n_groups, n_groups_i))
                link(dve.tensor_tensor_scan(first_group, n_groups, zero.broadcast_to([P, NB]), 0.0, ALU.add, ALU.add))
                link(dve.tensor_tensor(first_group, first_group, n_groups, ALU.subtract))
                link(dve.scalar_tensor_tensor(base, first_group, float(GE), ps[7][:, 0:NB], ALU.mult, ALU.add))
                link(dve.tensor_scalar(base, base, -1.0, None, ALU.add))
                link(dve.memset(pos_f, 0.0))
                with link.loop(NB, 4) as b:
                    no = lanes[:, bass.ds(b, 1)]
                    link(dve.tensor_scalar(hit, bucket, no, None, ALU.is_equal))
                    link(dve.tensor_tensor_scan(rank, hit, zero.broadcast_to([P, COLS]), base[:, bass.ds(b, 1)], ALU.add, ALU.add))
                    link(dve.scalar_tensor_tensor(rank, bucket, no, rank, ALU.is_equal, ALU.mult))
                    link(dve.tensor_tensor(pos_f, pos_f, rank, ALU.add))
                link(dve.tensor_copy(pos, pos_f))
                if name == "s":
                    dve.wait_ge(S("dst_in"), 16)
                    link(dve.tensor_scalar(dst_c, dst_i, float(NT * P - 1), None, ALU.min))
                else:
                    link(dve.tensor_scalar(src_i, src_i, float(NT * P - 1), None, ALU.min))
                dve.sem_inc(S(f"pos_ready_{name}"), 1)
                link(dve.memset(bucket_f, 0.0))
                with link.loop(NT - 1, 1) as b:
                    link(dve.scalar_tensor_tensor(bucket_f, group_no, first_group[0:1, bass.ds(b + 1, 1)], bucket_f, ALU.is_ge, ALU.add))
                link(dve.tensor_copy(bucket_of[order], bucket_f))
                dve.sem_inc(S("bucket_of_ready"), 1)

            def layer_norm(which):
                if which == 0:
                    dve.wait_ge(S("x_in"), 16)
                link(dve.tensor_reduce(stat[:, 0, :], xs, op=ALU.add, axis=AX.X))
                link(dve.tensor_scalar(stat[:, 0, :], stat[:, 0, :], 1.0 / F_IN, None, ALU.mult))
                link(dve.tensor_tensor(hs, xs, stat[:, 0, :].unsqueeze(2).broadcast_to([P, NT, F_IN]), ALU.subtract))
                sq = tab[:, 0:NT * F_IN].rearrange("p (t f) -> p t f", t=NT)
                link(dve.tensor_tensor(sq, hs, hs, ALU.mult))
                link(dve.tensor_reduce(stat[:, 1, :], sq, op=ALU.add, axis=AX.X))
                link(dve.tensor_scalar(stat[:, 1, :], stat[:, 1, :], 1.0 / F_IN, 1e-5, ALU.mult, ALU.add))
                dve.sem_inc(S("var_ready"), 1)
                dve.wait_ge(S("std_ready"), which + 1)
                link(dve.reciprocal(stat[:, 0, :], stat[:, 1, :]))
                link(dve.tensor_tensor(hs, hs, stat[:, 0, :].unsqueeze(2).broadcast_to([P, NT, F_IN]), ALU.mult))
                link(dve.tensor_scalar(hs, hs, 0.0, None, ALU.max))

            layer_norm(0)
            dve.sem_inc(S("h_ready"), 1)
            dve.wait_ge(S("weights_in"), 16 * N_WEIGHTS)
            link(dve.tensor_copy(b_part[:, 0, :], b_mid))
            link(dve.tensor_tensor(b_rest, b_mid, b_part[:, 0, :], ALU.subtract))
            link(dve.tensor_copy(b_part[:, 1, :], b_rest))
            link(dve.tensor_tensor(b_rest, b_rest, b_part[:, 1, :], ALU.subtract))
            link(dve.tensor_copy(b_part[:, 2, :], b_rest))
            dve.sem_inc(S("b_part_ready"), 1)

            own = tab[:, 0:NT * F_HID].rearrange("p (t f) -> p t f", f=F_HID)

            def own_tiles(of):
                g = of(1)
                if g is not None:
                    dve.wait_ge(S("own_done"), g.done())
                    dve.tensor_copy(own[:, g.at, :], ps[2 + g.slot(2)][:, 0:F_HID]).then_inc(S("own_copied"), 1)

            pipelined(dve, NT, 1, own_tiles)
            dve.wait_ge(S("own_copied"), NT)
            dve.wait_ge(S("arena_free"), 1)
            for part in range(3):
                link(dve.tensor_copy(own_parts[:, :, part, :], own))
                if part < 2:
                    link(dve.tensor_tensor(own, own, own_parts[:, :, part, :], ALU.subtract))
            fills = ROW_GROUPS * GE // (P * FILL)
            dve.wait_ge(S("blank_d_out"), 16 * fills)
            dve.wait_ge(S("blank_s_out"), 16 * fills)
            link(dve.memset(acc, 0.0))
            dve.sem_inc(S("own_parts_ready"), 1)

            def edge_mlp(of):
                g = of(0)
                if g is not None:
                    r = g.slot(4)
                    dve.wait_ge(S(f"rec_in{g.slot(2)}"), g.uses(2, 16))
                    if g.back(4).exists():
                        dve.wait_ge(S("hot_transposed"), g.back(4).done())
                        dve.wait_ge(S("hot_f_ready"), g.back(4).done())
                    dve.tensor_tensor(hot[:, r], lanes.unsqueeze(1).broadcast_to([P, U, P]),
                                      xg[:, g.slot(2), :, KX - 3:KX - 2].broadcast_to([P, U, P]), ALU.is_equal).then_inc(S("hot_ready"), 1)
                    dve.wait_ge(S("hot_transposed"), g.done())
                    if g.back(2).exists():
                        dve.wait_ge(S("hidden1"), g.back(2).done())
                    dve.tensor_copy(hot_t[:, g.slot(2), :], ps[1][:, 0:GE // 2].bitcast(BF16)).then_inc(S("hot_t_ready"), 1)
                g = of(3)
                if g is not None:
                    b = bucket_reg(dve, 0, g)
                    if g.back(1).exists():
                        dve.wait_ge(S("added"), g.back(1).done())
                    dve.wait_ge(S("summed"), g.done())
                    to = agg[:, bass.ds(b, 1), :].rearrange("p a f -> p (a f)")
                    dve.tensor_tensor(to, to, ps[6 + g.slot(2)][:, 0:F_HID], ALU.add).then_inc(S("added"), 1)

            pipelined(dve, GROUPS, 3, edge_mlp)
            dve.wait_ge(S("added"), GROUPS)
            dve.sem_inc(S("mlp_done"), 1)

            link(dve.tensor_tensor(xs, xs, hs, ALU.add))
            link(dve.tensor_tensor(xs, xs, nb2_row.unsqueeze(1).broadcast_to([P, NT, F_IN]), ALU.add))

            def node_mlp(of):
                g = of(2)
                if g is not None:
                    dve.wait_ge(S("node_out"), g.done())
                    dve.tensor_tensor(xs[:, g.at, :], xs[:, g.at, :], ps[4 + g.slot(2)][:, 0:F_IN], ALU.add).then_inc(S("node_added"), 1)

            pipelined(dve, NT, 2, node_mlp)
            dve.wait_ge(S("node_added"), NT)
            layer_norm(1)
            dve.sem_inc(S("gat_in"), 1)

            for n, (heads, ch) in enumerate(LAYERS):
                row, width = heads * (ch + 1), heads * ch
                tb = tab[:, 0:NT * row].rearrange("p (t f) -> p t f", f=row)
                ac = acc[:, 0:NT * row].rearrange("p (t f) -> p t f", f=row)
                a_s = alpha_s[:, 0:NT * heads].rearrange("p (t h) -> p t h", h=heads)
                a_d = alpha_d[:, 0:NT * heads].rearrange("p (t h) -> p t h", h=heads)
                mx = seg_max[:, 0:NT * heads].rearrange("p (t h) -> p t h", h=heads)
                oe = own_e[:, 0:NT * heads].rearrange("p (t h) -> p t h", h=heads)
                bo = both[:, 0:NT * 2 * heads].rearrange("p (t w) -> p t w", t=NT)
                pt = parts[:, 0:NT * 6 * heads].rearrange("p (t k w) -> p t k w", t=NT, k=3)

                def gat_tiles(of):
                    g = of(1)
                    if g is not None:
                        dve.wait_ge(S("gat_mm"), g.done())
                        dve.tensor_copy(tb[:, g.at, 0:width], ps[2 + g.slot(2)][:, 0:width]).then_inc(S("gat_copied"), 1)

                pipelined(dve, NT, 1, gat_tiles, n * NT)
                dve.wait_ge(S("gat_copied"), NT * (n + 1))
                for vec, to in ((att_s[n], a_s), (att_d[n], a_d)):
                    link(dve.tensor_tensor(ac[:, :, 0:width], tb[:, :, 0:width], vec.unsqueeze(1).broadcast_to([P, NT, width]), ALU.mult))
                    for h in range(heads):
                        link(dve.tensor_reduce(to[:, :, h], ac[:, :, h * ch:(h + 1) * ch], op=ALU.add, axis=AX.X))
                link(dve.tensor_copy(tb[:, :, width:row], a_s))
                link(dve.tensor_copy(mx, a_s))
                dve.sem_inc(S("table_ready"), 1)

                def maxima(of):
                    g = of(0)
                    if g is not None:
                        r = g.slot(4)
                        dve.wait_ge(S(f"ids_in_{r}"), g.uses(4, 16))
                        if g.back(4).exists():
                            dve.wait_ge(S("shown"), g.back(4).done())
                        dve.tensor_tensor(miss[:, r], lanes.unsqueeze(1).broadcast_to([P, U, P]),
                                          ids[:, r, :, 0:1].broadcast_to([P, U, P]), ALU.not_equal).then_inc(S("miss_ready"), 1)
                    g = of(1)
                    if g is not None:
                        r = g.slot(2)
                        b = bucket_reg(dve, 1, g)
                        dve.wait_ge(S("shown"), g.done())
                        for u in range(U):
                            red = dve.tensor_reduce(tile_max[:, r, u * heads:(u + 1) * heads],
                                                    ps[4 * r + u][:, 0:heads * P].rearrange("p (h e) -> p h e", h=heads), op=ALU.max, axis=AX.X)
                        red.then_inc(S("tile_max"), 1)
                        dve.wait_ge(S("tile_max"), g.done())
                        dve.tensor_reduce(group_max[:, r, 0:heads], tile_max[:, r, 0:U * heads].rearrange("p (u h) -> p h u", u=U),
                                          op=ALU.max, axis=AX.X).then_inc(S("group_max"), 1)
                        dve.wait_ge(S("group_max"), g.done())
                        if g.back(1).exists():
                            dve.wait_ge(S("max_updated"), g.back(1).done())
                        to = mx[:, bass.ds(b, 1), :].rearrange("p a h -> p (a h)")
                        dve.tensor_tensor(to, to, group_max[:, r, 0:heads], ALU.max).then_inc(S("max_updated"), 1)

                pipelined(dve, GROUPS, 1, maxima, n * GROUPS)
                dve.wait_ge(S("max_updated"), GROUPS * (n + 1))
                link(dve.tensor_tensor(mx, mx, a_d, ALU.add))
                link(dve.scalar_tensor_tensor(bo[:, :, heads:], mx, SLOPE, mx, ALU.mult, ALU.max))
                link(dve.tensor_copy(bo[:, :, 0:heads], a_d))
                link(dve.tensor_tensor(oe, a_s, a_d, ALU.add))
                link(dve.scalar_tensor_tensor(oe, oe, SLOPE, oe, ALU.mult, ALU.max))
                link(dve.tensor_tensor(oe, oe, bo[:, :, heads:], ALU.subtract))
                dve.sem_inc(S("own_logit"), 1)
                for part in range(3):
                    link(dve.tensor_copy(pt[:, :, part, :], bo))
                    if part < 2:
                        link(dve.tensor_tensor(bo, bo, pt[:, :, part, :], ALU.subtract))
                dve.wait_ge(S("own_exp"), n + 1)
                for h in range(heads):
                    link(dve.tensor_tensor(ac[:, :, h * ch:(h + 1) * ch], tb[:, :, h * ch:(h + 1) * ch],
                                           oe[:, :, h:h + 1].broadcast_to([P, NT, ch]), ALU.mult))
                link(dve.tensor_copy(ac[:, :, width:row], oe))
                dve.sem_inc(S("parts_ready"), 1)
                dve.sem_inc(S("maxima_done"), 1)

                def weights(of):
                    g = of(0)
                    if g is not None:
                        r = g.slot(4)
                        dve.wait_ge(S(f"ids2_in_{r}"), g.uses(4, 16))
                        if g.back(4).exists():
                            dve.wait_ge(S("a_hot_transposed"), g.back(4).done())
                            dve.wait_ge(S("a_hot_f_ready"), g.back(4).done())
                        dve.tensor_tensor(a_hot[:, r], lanes.unsqueeze(1).broadcast_to([P, U, P]),
                                          ids[:, r, :, 0:1].broadcast_to([P, U, P]), ALU.is_equal).then_inc(S("a_hot_ready"), 1)
                        dve.wait_ge(S("a_hot_transposed"), g.done())
                        if g.back(2).exists():
                            dve.wait_ge(S("looked_up"), g.back(2).done())
                        dve.tensor_copy(a_hot_t[:, g.slot(2), :], ps[0][:, 0:GE // 2].bitcast(BF16)).then_inc(S("a_hot_t_ready"), 1)
                    g = of(1)
                    if g is not None:
                        r = g.slot(2)
                        rows = g_rows[:, g.slot(4), 0:U * row].rearrange("p (u w) -> p u w", u=U)
                        look = ps[2 + r][:, 0:U * 2 * heads].rearrange("p (u w) -> p u w", u=U)
                        lg = logit[:, r, 0:U * heads].rearrange("p (u h) -> p u h", u=U)
                        l2 = logit2[:, r, 0:U * heads].rearrange("p (u h) -> p u h", u=U)
                        dve.wait_ge(S("looked_up"), g.done())
                        dve.wait_ge(S(f"rows_in_{g.slot(4)}"), g.uses(4, 16))
                        link2 = S("logit_step")
                        if g.back(2).exists():
                            dve.wait_ge(S("exp_ready"), g.back(2).done())
                        dve.tensor_tensor(l2, rows[:, :, width:row], look[:, :, 0:heads], ALU.add).then_inc(link2, 1)
                        dve.wait_ge(link2, g.back(1).done(3) + 1)
                        dve.scalar_tensor_tensor(lg, l2, SLOPE, l2, ALU.mult, ALU.max).then_inc(link2, 1)
                        dve.wait_ge(link2, g.back(1).done(3) + 2)
                        dve.tensor_tensor(l2, lg, look[:, :, heads:], ALU.subtract).then_inc(link2, 1)
                        dve.wait_ge(link2, g.back(1).done(3) + 3)
                        dve.tensor_scalar(lg, l2, 0.0, None, ALU.min).then_inc(S("logit_ready"), 1)
                        m = g_msg[:, r, 0:U * row].rearrange("p (u w) -> p u w", u=U)
                        dve.wait_ge(S("exp_ready"), g.done())
                        dve.tensor_tensor(m[:, :, 0:width].rearrange("p u (h c) -> p u h c", h=heads),
                                          rows[:, :, 0:width].rearrange("p u (h c) -> p u h c", h=heads),
                                          m[:, :, width:row].unsqueeze(3).broadcast_to([P, U, heads, ch]), ALU.mult).then_inc(S("msg_ready"), 1)
                    g = of(2)
                    if g is not None:
                        b = bucket_reg(dve, 1, g)
                        if g.back(1).exists():
                            dve.wait_ge(S("a_added"), g.back(1).done())
                        dve.wait_ge(S("a_summed"), g.done())
                        to = ac[:, bass.ds(b, 1), :].rearrange("p a f -> p (a f)")
                        dve.tensor_tensor(to, to, ps[4 + g.slot(2)][:, 0:row], ALU.add).then_inc(S("a_added"), 1)

                pipelined(dve, GROUPS, 2, weights, n * GROUPS)
                dve.wait_ge(S("a_added"), GROUPS * (n + 1))
                link(dve.tensor_scalar(oe, ac[:, :, width:row], 1e-16, None, ALU.add))
                link(dve.reciprocal(oe, oe))
                for h in range(heads):
                    link(dve.tensor_tensor(ac[:, :, h * ch:(h + 1) * ch], ac[:, :, h * ch:(h + 1) * ch],
                                           oe[:, :, h:h + 1].broadcast_to([P, NT, ch]), ALU.mult))
                link(dve.tensor_tensor(ac[:, :, 0:width], ac[:, :, 0:width], gat_b[n].unsqueeze(1).broadcast_to([P, NT, width]), ALU.add))
                if n == 0:
                    link(dve.tensor_scalar(ac[:, :, 0:width], ac[:, :, 0:width], 0.0, None, ALU.max))
                    dve.sem_inc(S("gat_in"), 1)
                else:
                    link(dve.tensor_tensor(hs, xs, ac[:, :, 0:width], ALU.add))
                    dve.sem_inc(S("out_ready"), 1)


_INS = ["x", "src", "dst", "edge_attr_16", "edge_weight", "L0_gnn_ew1", "L0_gnn_eb1", "L0_gnn_ew2",
        "L0_gnn_eb2", "L0_gnn_nw1", "L0_gnn_nb1", "L0_gnn_nw2", "L0_gnn_nb2", "L1_gnn_W1",
        "L1_gnn_a_src1", "L1_gnn_a_dst1", "L1_gnn_b1", "L1_gnn_W2", "L1_gnn_a_src2",
        "L1_gnn_a_dst2", "L1_gnn_b2"]


def kernel(**inputs):
    import numpy as np
    import concourse.bacc as bacc
    from concourse.bass_utils import run_bass_kernel_spmd

    def padded(a, rows, fill):
        full = np.full((rows,) + a.shape[1:], fill, a.dtype)
        full[:a.shape[0]] = a
        return full

    nc = bacc.Bacc("TRN2", target_bir_lowering=False, num_devices=1)
    arrays, args = {}, []
    for name in _INS:
        a = np.ascontiguousarray(inputs[name])
        if name == "x":
            a = padded(a, NT * P, 0)
        elif name in ("src", "dst"):
            a = padded(a, COLS * P, NT * P)
        elif name.startswith("edge"):
            a = padded(a, COLS * P, 0)
        arrays[f"in_{name}"] = a
        args.append(nc.dram_tensor(f"in_{name}", a.shape, mybir.dt.from_np(a.dtype), kind="ExternalInput").ap())
    args.append(nc.dram_tensor("out_0", (NT * P, F_IN), F32, kind="ExternalOutput").ap())
    gnn_kernel(nc, *args)
    r = run_bass_kernel_spmd(nc, [arrays], core_ids=[0])
    return r.results[0]["out_0"][:N_NODES]
```

```python
import concourse.bass as bass
from concourse import mybir
from contextlib import ExitStack, contextmanager

F32 = mybir.dt.float32
BF16 = mybir.dt.bfloat16
I32 = mybir.dt.int32
ALU = mybir.AluOpType
ACT = mybir.ActivationFunctionType
AX = mybir.AxisListType

P = 128
N_NODES, N_EDGES = 6250, 206250
F_IN, F_HID, F_EDGE, CUTOFF = 64, 128, 16, 5.0
HEADS, CH, OUT_DIM, SLOPE = 4, 32, 64, 0.2
NT = -(-N_NODES // P)
NB = NT + 1
LANE_BITS = 7
COLS = -(-N_EDGES // P // 52) * 52
U = 4
GE = P * U
GE_BITS = 9
GROUPS = (N_EDGES + NT * (GE - 1)) // GE + 1
ROW_GROUPS = GROUPS + 2
BATCH = 26
REC = F_EDGE + 4
KX = F_IN + REC
BIG = float(2 ** 100)
PEEL = 8
UNROLL = 4
SLOTS = 8
MAX_STEPS, LOGIT_STEPS = 11, 4
N_WEIGHTS = 19
LAYERS = ((HEADS, CH), (1, OUT_DIM))
LINEAR = COLS * P


def part_words(heads):
    return -(-3 * heads // 2)


def row_words(heads, ch):
    return part_words(heads) + heads * (ch + 1)




class Group:

    def __init__(self, i, off, before):
        self.i, self.off, self.before = i, off, before
        self.at = off if i is None else i + off

    def slot(self, n):
        return self.off % n

    def done(self, per=1):
        n = per * (self.before + self.off + 1)
        return n if self.i is None else self.i * per + n

    def uses(self, slots, per):
        earlier = (self.before - self.slot(slots) + slots - 1) // slots
        n = per * (earlier + self.off // slots + 1)
        return n if self.i is None else self.i * (per // slots) + n

    def back(self, n):
        return Group(self.i, self.off - n, self.before)

    def exists(self):
        return self.i is not None or self.off >= 0


def pipelined(eng, items, depth, step, before=0, peel=PEEL, unroll=UNROLL):
    def lookup(i, t):
        def group_of(stage):
            if i is None and not 0 <= t - stage < items:
                return None
            return Group(i, t - stage, before)
        return group_of

    for t in range(peel):
        step(lookup(None, t))
    rounds = (items - peel) // unroll
    with eng.Fori(0, rounds) as turn:
        i = turn * unroll + peel
        for k in range(unroll):
            step(lookup(i, k))
    for t in range(peel + rounds * unroll, items + depth):
        step(lookup(None, t))


def attention_pipeline(eng, depth, step, layer):
    pipelined(eng, GROUPS, depth, step, layer * GROUPS, peel=2 * SLOTS, unroll=SLOTS)


class Chain:

    def __init__(self, eng, sem):
        self.eng, self.sem, self.count, self.shift = eng, sem, 0, 0

    def __call__(self, ins):
        self.count += 1
        ins.then_inc(self.sem, 1)
        self.eng.wait_ge(self.sem, self.shift + self.count)

    @contextmanager
    def loop(self, times, per):
        first = self.count
        with self.eng.Fori(0, times) as i:
            self.shift = i * per
            yield i
        assert self.count - first == per
        self.shift, self.count = 0, first + times * per


def gnn_kernel(nc, x, src, dst, dst_next, attr, ew, ew1, eb1, ew2, eb2, nw1, nb1, nw2, nb2,
               W1, a_src1, a_dst1, b1, W2, a_src2, a_dst2, b2, out):
    ctx = ExitStack()
    with ctx:
        def sb(name, shape, dt=F32):
            return ctx.enter_context(nc.sbuf_tensor(name, shape, dt))[tuple(slice(None) for _ in shape)]

        def pb(name):
            return ctx.enter_context(nc.psum_tensor(name, [P, 512], F32))[:, :]

        def sem(name):
            return ctx.enter_context(nc.semaphore(name))

        def dram(name, shape, dt=F32):
            return nc.dram_tensor(name, shape, dt, kind="Internal").ap()

        rec_s = dram("rec_s", [ROW_GROUPS * GE, REC])
        rec_d = dram("rec_d", [LINEAR + GE, 2])
        h_table = dram("h_table", [NT * P, F_IN])
        tables = [dram(f"table{n}", [NT * P, row_words(*layer)]) for n, layer in enumerate(LAYERS)]

        xs = sb("xs", [P, NT, F_IN])
        hs = sb("hs", [P, NT, F_IN])
        acc = sb("acc", [P, NT * (F_HID + HEADS)])
        tab = sb("tab", [P, NT * row_words(*LAYERS[0])])
        alpha_s = sb("alpha_s", [P, NT * HEADS])
        alpha_d = sb("alpha_d", [P, NT * HEADS])
        shift = sb("shift", [P, NT * HEADS])
        rest = sb("rest", [P, NT * HEADS])
        dst_parts = sb("dst_parts", [P, NT * 3 * HEADS], BF16)
        stat = sb("stat", [P, 2, NT])
        ident = sb("ident", [P, P])
        ident_b = sb("ident_b", [P, P], BF16)
        neg_ident = sb("neg_ident", [P, P], BF16)
        lanes = sb("lanes", [P, P])
        lanes_b = sb("lanes_b", [P, P], BF16)
        picks = [sb(f"pick{n}", [3 * h, h, P], BF16) for n, (h, _) in enumerate(LAYERS)]
        lower = sb("lower", [P, P])
        ones = sb("ones", [P, P])
        ones3 = sb("ones3", [3, P], BF16)
        zero = sb("zero", [P, 1])
        w_edge = sb("w_edge", [KX, F_HID])
        w_own = sb("w_own", [F_IN, F_HID])
        w_mid = sb("w_mid", [F_HID, F_HID])
        b_mid = sb("b_mid", [1, F_HID])
        b_rest = sb("b_rest", [1, F_HID])
        b_part = sb("b_part", [1, 3, F_HID], BF16)
        b_rows = sb("b_rows", [3, F_HID], BF16)
        w_node_h = sb("w_node_h", [F_IN, F_HID])
        w_node_a = sb("w_node_a", [F_HID, F_HID])
        w_out = sb("w_out", [F_HID, F_IN])
        nb1_col = sb("nb1_col", [F_HID, 1])
        nb2_row = sb("nb2_row", [P, F_IN])
        gat_w = [sb("gat_w1", [F_IN, F_HID]), sb("gat_w2", [F_HID, OUT_DIM])]
        att_s = [sb("att_s1", [P, F_HID]), sb("att_s2", [P, OUT_DIM])]
        att_d = [sb("att_d1", [P, F_HID]), sb("att_d2", [P, OUT_DIM])]
        gat_b = [sb("gat_b1", [P, F_HID]), sb("gat_b2", [P, OUT_DIM])]
        bucket_of = [sb(f"bucket_of{k}", [1, ROW_GROUPS], I32) for k in range(2)]
        first_edge = sb("first_edge", [1, ROW_GROUPS], I32)
        first_node = sb("first_node", [P, ROW_GROUPS])
        group_no = sb("group_no", [P, ROW_GROUPS])
        bucket_f = sb("bucket_f", [P, ROW_GROUPS])
        start_f = sb("start_f", [P, ROW_GROUPS])
        term = sb("term", [P, ROW_GROUPS])
        total = sb("total", [P, NB])
        gap = sb("gap", [P, NB])
        falls = sb("falls", [P, 1])
        is_sorted = sb("is_sorted", [1, 1], I32)
        counts = sb("counts", [P, NB])
        n_groups_i = sb("n_groups_i", [P, NB], I32)
        n_groups = sb("n_groups", [P, NB])
        first_group = sb("first_group", [P, NB])
        base = sb("base", [P, NB])
        tile_in = sb("tile_in", [P, 2, F_IN + F_HID])
        tile_t = sb("tile_t", [P, 2, 2, P])
        mid_t = sb("mid_t", [P, 2, P])
        ARENA = 22900
        arena = sb("arena", [P, ARENA])

        def carve(start, shape, dt=F32):
            words = 1
            for n in shape:
                words *= n
            words = words if dt != BF16 else words // 2
            v = arena[:, start:start + words]
            assert start + words <= ARENA, (start, shape)
            if dt != F32:
                v = v.bitcast(dt)
            names = " ".join("abcd"[:len(shape)])
            kw = {"abcd"[n]: shape[n] for n in range(len(shape))}
            return v.rearrange(f"p ({names}) -> p {names}", **kw), start + words

        at = 0
        src_i, at = carve(at, [COLS], I32)
        dst_i, at = carve(at, [COLS], I32)
        weight, at = carve(at, [COLS])
        bucket, at = carve(at, [COLS])
        lane_s, at = carve(at, [COLS])
        edge_d, at = carve(at, [COLS, 2])
        pos_s, at = carve(at, [COLS], I32)
        pos_d, at = carve(at, [COLS], I32)
        pos_f, at = carve(at, [COLS])
        hit, at = carve(at, [COLS])
        rank, at = carve(at, [COLS])
        dst_c, at = carve(at, [COLS], I32)
        attr_in = [None, None]
        rec_out = [None, None]
        rec2_out = [sb(f"rec2_out{k}", [P, BATCH, 2]) for k in range(2)]
        where = [sb(f"where{k}", [P, BATCH], I32) for k in range(2)]
        for k in range(2):
            rec_out[k], at = carve(at, [BATCH, REC])
            attr_in[k], at = carve(at, [BATCH, F_EDGE])
        FILL = 227
        assert ROW_GROUPS * GE % (P * FILL) == 0
        blank_s = acc[:, 0:FILL * REC].rearrange("p (r w) -> p r w", w=REC)
        blank_d = acc[:, FILL * REC:FILL * REC + U * 2].rearrange("p (r w) -> p r w", w=2)

        at = 0
        own_parts, at = carve(at, [NT, 3, F_HID], BF16)
        xg, at = carve(at, [4, U, KX])
        hot, at = carve(at, [4, U, P], BF16)
        hot_f, at = carve(at, [4, U, P])
        hot_t, at = carve(at, [2, GE], BF16)
        x_t, at = carve(at, [2, GE])
        mid_e, at = carve(at, [2, GE])
        msg, at = carve(at, [2, U, F_HID])
        lane_e, at = carve(at, [2, U], BF16)
        at = 0
        a_hot, at = carve(at, [SLOTS, U, P], BF16)
        a_hot_f, at = carve(at, [4, U, P])
        turned, at = carve(at, [SLOTS, 2, GE], BF16)
        miss, at = carve(at, [4, U, P], BF16)
        ids, at = carve(at, [SLOTS, U, 2])
        a_lane, at = carve(at, [4, U], BF16)
        logit, at = carve(at, [4, U * HEADS])
        logit2, at = carve(at, [4, U * HEADS])
        part_max, at = carve(at, [4, 2 * HEADS])
        new_max, at = carve(at, [4, HEADS])
        new_shift, at = carve(at, [4, HEADS])
        shrink, at = carve(at, [SLOTS, HEADS])
        left, at = carve(at, [4, HEADS])
        look, at = carve(at, [4, 3 * 2 * HEADS], BF16)
        g_rows, at = carve(at, [SLOTS, U * row_words(*LAYERS[0])])
        g_msg, at = carve(at, [4, U * (F_HID + HEADS)])

        ps_all = ctx.enter_context(nc.psum_tensor("ps_all", [P, 8 * 512], F32))[:, :]
        ps = [ps_all[:, 512 * n:512 * (n + 1)] for n in range(8)]

        s = {}

        def S(name):
            if name not in s:
                s[name] = sem(name)
            return s[name]

        agg = acc[:, 0:NT * F_HID].rearrange("p (t f) -> p t f", f=F_HID)

        block = ctx.enter_context(nc.Block())

        def bucket_reg(eng, order, g):
            return eng.value_load(bucket_of[order][0:1, bass.ds(g.at, 1)], min_val=0, max_val=NT - 1)

        @block.sync
        def _(sp):
            sp.dma_start(src_i, src.rearrange("(p j) -> p j", p=P)).then_inc(S("src_in"), 16)
            sp.dma_start(dst_i, dst.rearrange("(p j) -> p j", p=P)).then_inc(S("dst_in"), 16)
            sp.dma_start(pos_d, dst_next.rearrange("(p j) -> p j", p=P)).then_inc(S("next_in"), 16)
            sp.dma_start(weight, ew.rearrange("(p j) -> p j", p=P)).then_inc(S("weight_in"), 16)
            sp.dma_start(xs, x.rearrange("(t p) f -> p t f", p=P)).then_inc(S("x_in"), 16)
            loads = [
                (w_own, ew1[0:F_IN, :]), (w_edge[0:F_IN, :], ew1[F_IN:2 * F_IN, :]),
                (w_edge[F_IN:F_IN + F_EDGE + 1, :], ew1[2 * F_IN:, :]),
                (w_edge[KX - 1:KX, :], eb1.rearrange("(a n) -> a n", a=1)),
                (w_mid, ew2), (b_mid, eb2.rearrange("(a n) -> a n", a=1)),
                (w_node_h, nw1[0:F_IN, :]), (w_node_a, nw1[F_IN:, :]), (w_out, nw2),
                (nb1_col, nb1.rearrange("(n a) -> n a", a=1)),
                (nb2_row, nb2.rearrange("(a n) -> a n", a=1).broadcast_to([P, F_IN])),
                (gat_w[0], W1), (gat_w[1], W2),
                (gat_b[0], b1.rearrange("(a n) -> a n", a=1).broadcast_to([P, F_HID])),
                (gat_b[1], b2.rearrange("(a n) -> a n", a=1).broadcast_to([P, OUT_DIM])),
                (att_s[0], a_src1.rearrange("a h c -> a (h c)").broadcast_to([P, F_HID])),
                (att_s[1], a_src2.rearrange("a h c -> a (h c)").broadcast_to([P, OUT_DIM])),
                (att_d[0], a_dst1.rearrange("a h c -> a (h c)").broadcast_to([P, F_HID])),
                (att_d[1], a_dst2.rearrange("a h c -> a (h c)").broadcast_to([P, OUT_DIM])),
            ]
            assert len(loads) == N_WEIGHTS
            sp.wait_ge(S("zero_ready"), 1)
            for to, what in loads:
                sp.dma_start(to, what).then_inc(S("weights_in"), 16)
            sp.wait_ge(S("blank_ready"), 2)
            n = ROW_GROUPS * GE // (P * FILL)
            to_s = rec_s.rearrange("(p n r) w -> n p (r w)", p=P, n=n)
            for k in range(n):
                sp.dma_start(to_s[k], blank_s.rearrange("p r w -> p (r w)")).then_inc(S("blank_s_out"), 16)
            sp.dma_start(rec_d[LINEAR:, :].rearrange("(p r) w -> p (r w)", p=P),
                         blank_d.rearrange("p r w -> p (r w)")).then_inc(S("blank_d_out"), 16)
            at_v = attr.rearrange("(p j) f -> p (j f)", p=P)
            with sp.Fori(0, COLS // BATCH // 2) as i:
                for k in range(2):
                    sp.wait_ge(S("attr_used"), 2 * i + k + 1)
                    sp.dma_start(attr_in[k].rearrange("p u w -> p (u w)"),
                                 at_v[:, bass.ds((2 * i + k) * (BATCH * F_EDGE), BATCH * F_EDGE)]
                                 ).then_inc(S(f"attr_in{k}"), 16)
            sp.wait_ge(S("h_ready"), 1)
            sp.dma_start(h_table.rearrange("(t p) f -> p t f", p=P), hs).then_inc(S("h_table_out"), 16)

            sp.wait_ge(S("b_part_ready"), 1)
            sp.dma_start(b_rows, b_part.rearrange("a k f -> a (k f)")).then_inc(S("b_rows_in"), 16)

            sp.wait_ge(S("sorted_s"), 1)
            sp.wait_ge(S("arena_free"), 1)
            rs = rec_s.rearrange("(g p u) w -> g p u w", p=P, u=U)

            def load_records(of):
                g = of(0)
                if g is None:
                    return
                if g.back(4).exists():
                    sp.wait_ge(S("x_transposed"), g.back(4).done())
                    sp.wait_ge(S("lane_ready"), g.back(4).done())
                sp.dma_start(xg[:, g.slot(4), :, F_IN:KX], rs[bass.ds(g.at, 1)].rearrange("a p u w -> p (a u) w")
                             ).then_inc(S(f"rec_in{g.slot(4)}"), 16)

            pipelined(sp, GROUPS, 0, load_records)

            for n, (heads, ch) in enumerate(LAYERS):
                row = row_words(heads, ch)
                sp.wait_ge(S("table_ready"), n + 1)
                sp.dma_start(tables[n].rearrange("(t p) f -> p t f", p=P),
                             tab[:, 0:NT * row].rearrange("p (t f) -> p t f", f=row)).then_inc(S("table_out"), 16)
                if n == 0:
                    sp.wait_ge(S("sorted_d"), 1)

                def load_ids(of):
                    g = of(0)
                    if g is None:
                        return
                    first = sp.value_load(first_edge[0:1, bass.ds(g.at, 1)], min_val=0, max_val=LINEAR)
                    r = g.slot(SLOTS)
                    if g.back(SLOTS).exists():
                        sp.wait_ge(S("a_lane_ready"), g.back(SLOTS).done())
                        sp.sem_inc(S("sp_go"), 1)
                        sp.wait_ge(S(f"gathered_{r}"), g.back(SLOTS).uses(SLOTS, 16 * U))
                        sp.sem_inc(S("sp_go"), 1)
                    sp.dma_start(ids[:, r, :, :].rearrange("p u w -> p (u w)"),
                                 rec_d[bass.ds(first, GE), :].rearrange("(p u) w -> p (u w)", u=U)
                                 ).then_inc(S(f"ids_in_{r}"), 16)

                attention_pipeline(sp, 0, load_ids, n)

            sp.wait_ge(S("out_ready"), 1)
            sp.dma_start(out.rearrange("(t p) f -> p t f", p=P), hs).then_inc(S("out_done"), 16)
            sp.wait_ge(S("out_done"), 16)

        @block.gpsimd
        def _(pool):
            pool.memset(ident, 0.0).then_inc(S("const0"), 1)
            pool.memset(lower, 1.0).then_inc(S("const0"), 1)
            pool.memset(ones, 1.0).then_inc(S("const0"), 1)
            pool.memset(tile_in, 0.0).then_inc(S("const0"), 1)
            pool.wait_ge(S("const0"), 4)
            pool.affine_select(out=ident, in_=ident, compare_op=ALU.not_equal, fill=1.0, base=0,
                               pattern=[[-1, P]], channel_multiplier=1).then_inc(S("const1"), 1)
            pool.affine_select(out=lower, in_=lower, compare_op=ALU.is_gt, fill=0.0, base=0,
                               pattern=[[1, P]], channel_multiplier=-1).then_inc(S("const1"), 1)
            pool.iota(lanes, [[1, P]], base=0, channel_multiplier=0,
                      allow_small_or_imprecise_dtypes=True).then_inc(S("const1"), 1)
            pool.iota(group_no, [[1, ROW_GROUPS]], base=0, channel_multiplier=0,
                      allow_small_or_imprecise_dtypes=True).then_inc(S("const1"), 1)
            pool.memset(blank_s, 0.0).then_inc(S("blank0"), 1)
            pool.memset(blank_d, 0.0).then_inc(S("blank0"), 1)
            for pick in picks:
                pool.memset(pick, 0.0).then_inc(S("pick0"), 1)
            for k in range(2):
                pool.memset(rec_out[k][:, :, REC - 1:REC], 1.0).then_inc(S("blank0"), 1)
            pool.wait_ge(S("blank0"), 4)
            pool.memset(blank_s[:, :, REC - 3:REC - 2], -1.0).then_inc(S("blank_ready"), 1)
            pool.memset(blank_d[:, :, 0:1], -1.0).then_inc(S("blank_ready"), 1)

            def tile_inputs(ready, count, name, sources, transposed, before=0):
                pool.wait_ge(S(ready), count)

                def copy(of):
                    g = of(0)
                    if g is None:
                        return
                    if g.back(2).exists():
                        pool.wait_ge(S(transposed), g.back(2).done())
                    at = 0
                    for rows, width in sources:
                        pool.tensor_copy(tile_in[:, g.slot(2), at:at + width],
                                         rows[:, bass.ds(g.at, 1), 0:width].rearrange("p a f -> p (a f)")
                                         ).then_inc(S(name), 1)
                        at += width

                pipelined(pool, NT, 0, copy, before)

            pool.wait_ge(S("pick0"), 2)
            for n, (heads, _) in enumerate(LAYERS):
                for part in range(3):
                    pool.affine_select(out=picks[n], in_=picks[n], compare_op=ALU.not_equal, fill=1.0,
                                       base=-heads * part, pattern=[[-1, heads], [0, P]],
                                       channel_multiplier=1).then_inc(S("picks_ready"), 1)
                    pool.wait_ge(S("picks_ready"), 3 * n + part + 1)

            fills = ROW_GROUPS * GE // (P * FILL)
            pool.wait_ge(S("blank_s_out"), 16 * fills)
            with pool.Fori(0, COLS // BATCH // 2) as i:
                for k in range(2):
                    pool.wait_ge(S("staged_s"), 2 * i + k + 1)
                    pool.sem_inc(S("pool_go"), 1)
                    for c in range(BATCH):
                        pool.indirect_dma_start(
                            rec_s, bass.IndirectOffsetOnAxis(ap=where[k][:, c:c + 1], axis=0),
                            rec_out[k][:, c, :], None).then_inc(S(f"sorted_s_slot{k}"), 16)
            for k in range(2):
                pool.wait_ge(S(f"sorted_s_slot{k}"), 16 * COLS // 2)
            pool.sem_inc(S("sorted_s"), 1)

            pool.wait_ge(S("pos_ready_d"), 1)
            in_order = pool.value_load(is_sorted[0:1, 0:1], min_val=0, max_val=1)
            with pool.If(in_order):
                pool.dma_start(rec_d[0:LINEAR, :].rearrange("(p j) w -> p (j w)", p=P),
                               edge_d.rearrange("p j w -> p (j w)")).then_inc(S("copied_d"), 16)
                pool.wait_ge(S("copied_d"), 16)
            with pool.Else():
                def scatter_d(i):
                    for k in range(2):
                        cols = bass.ds((2 * i + k) * BATCH, BATCH)
                        if not (isinstance(i, int) and i == 0):
                            pool.wait_ge(S(f"sorted_d_slot{k}"), i * (16 * BATCH))
                        pool.tensor_copy(where[k], pos_d[:, cols]).then_inc(S("staged_d"), 1)
                        pool.tensor_copy(rec2_out[k], edge_d[:, cols, :]).then_inc(S("staged_d"), 1)
                        pool.wait_ge(S("staged_d"), 4 * i + 2 * k + 2)
                        pool.sem_inc(S("pool_go"), 1)
                        for c in range(BATCH):
                            pool.indirect_dma_start(
                                rec_d, bass.IndirectOffsetOnAxis(ap=where[k][:, c:c + 1], axis=0),
                                rec2_out[k][:, c, :], None).then_inc(S(f"sorted_d_slot{k}"), 16)

                scatter_d(0)
                with pool.Fori(1, COLS // BATCH // 2) as i:
                    scatter_d(i)
                for k in range(2):
                    pool.wait_ge(S(f"sorted_d_slot{k}"), 16 * COLS // 2)
            pool.wait_ge(S("blank_d_out"), 16)
            pool.sem_inc(S("sorted_d"), 1)
            pool.sem_inc(S("arena_free"), 1)

            tile_inputs("h_ready", 1, "own_in", [(hs, F_IN)], "own_t")
            pool.wait_ge(S("h_table_out"), 16)
            pool.wait_ge(S("arena_free"), 1)

            def gather_h(of):
                g = of(0)
                if g is None:
                    return
                pool.wait_ge(S(f"rec_in{g.slot(4)}"), g.uses(4, 16))
                pool.sem_inc(S("pool_go"), 1)
                for u in range(U):
                    pool.indirect_dma_start(
                        xg[:, g.slot(4), u, 0:F_IN], None, h_table,
                        bass.IndirectOffsetOnAxis(
                            ap=xg[:, g.slot(4), u, KX - 2:KX - 1].bitcast(I32), axis=0)
                    ).then_inc(S(f"h_in{g.slot(4)}"), 16)

            pipelined(pool, GROUPS, 0, gather_h)

            tile_inputs("mlp_done", 1, "node_in", [(hs, F_IN), (agg, F_HID)], "node_t")
            for n, (heads, ch) in enumerate(LAYERS):
                row = row_words(heads, ch)
                node_in = hs if n == 0 else acc[:, 0:NT * F_HID].rearrange("p (t f) -> p t f", t=NT)
                tile_inputs("gat_in", n + 1, "gat_x", [(node_in, F_HID if n else F_IN)], "gat_t", n * NT)
                pool.wait_ge(S("table_out"), 16 * (n + 1))

                def gather_rows(of):
                    g = of(0)
                    if g is None:
                        return
                    r = g.slot(SLOTS)
                    if g.back(SLOTS).exists():
                        pool.wait_ge(S("msg_ready"), g.back(SLOTS).done())
                        pool.wait_ge(S("turned"), g.back(SLOTS).done())
                    pool.wait_ge(S(f"ids_in_{r}"), g.uses(SLOTS, 16))
                    pool.sem_inc(S("pool_go"), 1)
                    for u in range(U):
                        pool.indirect_dma_start(
                            g_rows[:, r, u * row:(u + 1) * row], None, tables[n],
                            bass.IndirectOffsetOnAxis(ap=ids[:, r, u, 1:2].bitcast(I32), axis=0)
                        ).then_inc(S(f"gathered_{r}"), 16)

                attention_pipeline(pool, 0, gather_rows, n)

        @block.scalar
        def _(act):
            act.sem_inc(S("attr_used"), 2)
            act.wait_ge(S("pos_ready_s"), 1)
            act.wait_ge(S("weight_in"), 16)

            def stage(i):
                for k in range(2):
                    cols = bass.ds((2 * i + k) * BATCH, BATCH)
                    if not (isinstance(i, int) and i == 0):
                        act.wait_ge(S(f"sorted_s_slot{k}"), i * (16 * BATCH))
                    rec = rec_out[k]
                    act.activation(rec[:, :, F_EDGE], weight[:, cols], ACT.Copy, scale=1.0 / CUTOFF).then_inc(S("staging"), 1)
                    act.activation(rec[:, :, F_EDGE + 1], lane_s[:, cols], ACT.Copy).then_inc(S("staging"), 1)
                    act.activation(rec[:, :, F_EDGE + 2].bitcast(I32), dst_c[:, cols], ACT.Copy).then_inc(S("staging"), 1)
                    act.activation(where[k], pos_s[:, cols], ACT.Copy).then_inc(S("staging"), 1)
                    act.wait_ge(S(f"attr_in{k}"), 16 * i + 16)
                    act.activation(rec[:, :, 0:F_EDGE], attr_in[k], ACT.Copy).then_inc(S("attr_used"), 1)
                    act.wait_ge(S("attr_used"), 2 * i + k + 3)
                    act.wait_ge(S("staging"), 8 * i + 4 * (k + 1))
                    act.sem_inc(S("staged_s"), 1)

            stage(0)
            with act.Fori(1, COLS // BATCH // 2) as i:
                stage(i)

            act.wait_ge(S("var_ready"), 1)
            act.activation(stat[:, 1, :], stat[:, 1, :], ACT.Sqrt).then_inc(S("std_ready"), 1)

            def own_tiles(of):
                g = of(0)
                if g is not None:
                    if g.back(2).exists():
                        act.wait_ge(S("own_done"), g.back(2).done())
                    act.wait_ge(S("own_t"), g.done())
                    act.activation(tile_t[0:F_IN, g.slot(2), 0, :], ps[g.slot(2)][0:F_IN, 0:P], ACT.Copy).then_inc(S("own_tt"), 1)

            pipelined(act, NT, 0, own_tiles)

            def edge_mlp(of):
                g = of(0)
                if g is not None:
                    act.wait_ge(S("hot_ready"), g.done())
                    if g.back(4).exists():
                        act.wait_ge(S("summed"), g.back(4).done())
                    act.activation(hot_f[:, g.slot(4)], hot[:, g.slot(4)], ACT.Copy).then_inc(S("hot_f_ready"), 1)
                    act.wait_ge(S("x_transposed"), g.done())
                    if g.back(2).exists():
                        act.wait_ge(S("hidden1"), g.back(2).done())
                    act.activation(x_t[0:KX, g.slot(2), :], ps[0][0:KX, :], ACT.Copy).then_inc(S("x_t_ready"), 1)
                g = of(1)
                if g is not None:
                    act.wait_ge(S("hidden1"), g.done())
                    if g.back(2).exists():
                        act.wait_ge(S("hidden2"), g.back(2).done())
                    act.activation(mid_e[:, g.slot(2), :], ps[2 + g.slot(2)][:, :], ACT.Silu).then_inc(S("mid_ready"), 1)
                g = of(2)
                if g is not None:
                    act.wait_ge(S("hidden2"), g.done())
                    if g.back(2).exists():
                        act.wait_ge(S("summed"), g.back(2).done())
                    act.activation(msg[:, g.slot(2)].rearrange("p u f -> p (u f)"), ps[4 + g.slot(2)][:, :], ACT.Silu).then_inc(S("message_ready"), 1)

            pipelined(act, GROUPS, 2, edge_mlp)

            def node_mlp(of):
                g = of(0)
                if g is not None:
                    act.wait_ge(S("node_t"), g.done())
                    if g.back(2).exists():
                        act.wait_ge(S("node_mid"), g.back(2).done())
                    act.activation(tile_t[0:F_IN, g.slot(2), 0, :], ps[g.slot(2)][0:F_IN, 0:P], ACT.Copy).then_inc(S("node_tt"), 1)
                    act.activation(tile_t[:, g.slot(2), 1, :], ps[g.slot(2)][:, P:2 * P], ACT.Copy).then_inc(S("node_tt"), 1)
                g = of(1)
                if g is not None:
                    act.wait_ge(S("node_mid"), g.done())
                    if g.back(2).exists():
                        act.wait_ge(S("node_out"), g.back(2).done())
                    act.activation(mid_t[:, g.slot(2), :], ps[2 + g.slot(2)][:, 0:P], ACT.Silu, bias=nb1_col).then_inc(S("node_act"), 1)

            pipelined(act, NT, 1, node_mlp)
            act.wait_ge(S("var_ready"), 2)
            act.activation(stat[:, 1, :], stat[:, 1, :], ACT.Sqrt).then_inc(S("std_ready"), 1)

            for n, (heads, ch) in enumerate(LAYERS):
                width = heads * ch
                k_in = F_IN if n == 0 else F_HID

                def gat_tiles(of):
                    g = of(0)
                    if g is not None:
                        act.wait_ge(S("gat_t"), g.done())
                        if g.back(2).exists():
                            act.wait_ge(S("gat_mm"), g.back(2).done())
                        act.activation(tile_t[0:k_in, g.slot(2), 0, :], ps[g.slot(2)][0:k_in, 0:P], ACT.Copy).then_inc(S("gat_tt"), 1)

                pipelined(act, NT, 0, gat_tiles, n * NT)

                def attend(of):
                    g = of(5)
                    if g is not None:
                        act.wait_ge(S("max_step"), g.done(MAX_STEPS))
                        if g.back(SLOTS).exists():
                            act.wait_ge(S("a_shrunk"), g.back(SLOTS).done())
                        act.activation(shrink[:, g.slot(SLOTS), 0:heads], left[:, g.slot(4), 0:heads], ACT.Exp
                                       ).then_inc(S("shrink_ready"), 1)
                    g = of(1)
                    if g is not None:
                        act.wait_ge(S("a_hot_ready"), g.done())
                        if g.back(4).exists():
                            act.wait_ge(S("shown"), g.back(4).done())
                        act.activation(miss[:, g.slot(4)], a_hot[:, g.slot(SLOTS)], ACT.Copy, scale=-1.0, bias=1.0
                                       ).then_inc(S("miss_ready"), 1)
                        act.wait_ge(S("turned"), g.done())
                        if g.back(SLOTS).exists():
                            act.wait_ge(S("looked_up"), g.back(SLOTS).done())
                            act.wait_ge(S("shown"), g.back(SLOTS).done())
                        bank = ps[(4, 7)[g.slot(2)]].bitcast(BF16)
                        act.activation(turned[0:3 * heads, g.slot(SLOTS), 1, :], bank[0:3 * heads, GE:2 * GE], ACT.Copy
                                       ).then_inc(S("turned_copied"), 1)
                        act.activation(turned[:, g.slot(SLOTS), 0, :], bank[:, 0:GE], ACT.Copy).then_inc(S("turned_copied"), 1)
                    g = of(6)
                    if g is not None:
                        if g.back(4).exists():
                            act.wait_ge(S("a_summed"), g.back(4).done())
                        act.activation(a_hot_f[:, g.slot(4)], a_hot[:, g.slot(SLOTS)], ACT.Copy).then_inc(S("a_hot_f_ready"), 1)
                        act.wait_ge(S("logit_step"), g.done(LOGIT_STEPS))
                        m = g_msg[:, g.slot(4), 0:U * (width + heads)].rearrange("p (u h c) -> p u h c", u=U, h=heads)
                        act.activation(m[:, :, :, ch], logit[:, g.slot(4), 0:U * heads].rearrange("p (u h) -> p u h", u=U), ACT.Exp
                                       ).then_inc(S("exp_ready"), 1)

                attention_pipeline(act, 6, attend, n)

        @block.tensor
        def _(pe):
            pe.wait_ge(S("const1"), 4)
            for k in range(2):
                pe.wait_ge(S("counts_ready"), k + 1)
                pe.matmul(ps[7][:, 0:NB], lower, counts, start=True, stop=True)
                pe.matmul(ps[7][:, 256:256 + NB], ones, counts, start=True, stop=True).then_inc(S("prefix_ready"), 1)
            pe.wait_ge(S("falls_ready"), 1)
            pe.matmul(ps[6][:, 0:1], ones, falls, start=True, stop=True).then_inc(S("falls_summed"), 1)

            pe.wait_ge(S("weights_in"), 16 * N_WEIGHTS)
            pe.wait_ge(S("h_ready"), 1)

            def own_tiles(of):
                g = of(0)
                if g is not None:
                    if g.back(2).exists():
                        pe.wait_ge(S("own_tt"), g.back(2).done())
                    pe.wait_ge(S("own_in"), g.done())
                    pe.transpose(ps[g.slot(2)][:, 0:P], tile_in[:, g.slot(2), 0:P], ident).then_inc(S("own_t"), 1)
                g = of(1)
                if g is not None:
                    pe.wait_ge(S("own_tt"), g.done())
                    if g.back(2).exists():
                        pe.wait_ge(S("own_copied"), g.back(2).done())
                    pe.matmul(ps[2 + g.slot(2)][:, 0:F_HID], tile_t[0:F_IN, g.slot(2), 0, :], w_own, start=True, stop=True).then_inc(S("own_done"), 1)

            pipelined(pe, NT, 1, own_tiles)

            pe.wait_ge(S("own_parts_ready"), 1)
            pe.wait_ge(S("b_rows_in"), 16)

            def edge_mlp(of):
                g = of(0)
                if g is not None:
                    r = g.slot(2)
                    pe.wait_ge(S(f"h_in{g.slot(4)}"), g.uses(4, 16 * U))
                    if g.back(1).exists():
                        pe.wait_ge(S("x_t_ready"), g.back(1).done())
                    for u in range(U):
                        mm = pe.transpose(ps[0][0:KX, u * P:(u + 1) * P], xg[:, g.slot(4), u, :], ident)
                    mm.then_inc(S("x_transposed"), 1)
                    pe.wait_ge(S("hot_ready"), g.done())
                    if g.back(1).exists():
                        pe.wait_ge(S("hot_t_ready"), g.back(1).done())
                    for u in range(U):
                        mm = pe.transpose(ps[1][:, 0:GE // 2].bitcast(BF16)[:, u * P:(u + 1) * P], hot[:, g.slot(4), u, :], ident_b)
                    mm.then_inc(S("hot_transposed"), 1)
                g = of(1)
                if g is not None:
                    r = g.slot(2)
                    b = bucket_reg(pe, 0, g)
                    pe.wait_ge(S("x_t_ready"), g.done())
                    if g.back(2).exists():
                        pe.wait_ge(S("mid_ready"), g.back(2).done())
                    pe.matmul(ps[2 + r][:, :], w_edge, x_t[0:KX, r, :], start=True, stop=False)
                    pe.wait_ge(S("hot_t_ready"), g.done())
                    for part in range(3):
                        mm = pe.matmul(ps[2 + r][:, :], own_parts[:, bass.ds(b, 1), part, :].rearrange("p a f -> p (a f)"), hot_t[:, r, :],
                                       start=False, stop=(part == 2))
                    mm.then_inc(S("hidden1"), 1)
                g = of(2)
                if g is not None:
                    r = g.slot(2)
                    pe.wait_ge(S("mid_ready"), g.done())
                    if g.back(2).exists():
                        pe.wait_ge(S("message_ready"), g.back(2).done())
                    for u in range(U):
                        pe.matmul(ps[4 + r][:, u * P:(u + 1) * P], mid_e[:, r, u * P:(u + 1) * P], w_mid,
                                  start=(u == 0), stop=False, skip_group_check=True)
                    mm = pe.matmul(ps[4 + r][:, :].rearrange("p (u f) -> p u f", u=U), ones3,
                                   b_rows.unsqueeze(1).broadcast_to([3, U, F_HID]), start=False, stop=True,
                                   skip_group_check=True)
                    mm.then_inc(S("hidden2"), 1)
                g = of(3)
                if g is not None:
                    r = g.slot(2)
                    pe.wait_ge(S("message_ready"), g.done())
                    pe.wait_ge(S("hot_f_ready"), g.done())
                    if g.back(2).exists():
                        pe.wait_ge(S("added"), g.back(2).done())
                    for u in range(U):
                        mm = pe.matmul(ps[6 + r][:, 0:F_HID], hot_f[:, g.slot(4), u, :], msg[:, r, u, :],
                                       start=(u == 0), stop=(u == U - 1))
                    mm.then_inc(S("summed"), 1)

            pipelined(pe, GROUPS, 3, edge_mlp)

            pe.wait_ge(S("added"), GROUPS)

            def node_mlp(of):
                g = of(0)
                if g is not None:
                    r = g.slot(2)
                    if g.back(2).exists():
                        pe.wait_ge(S("node_tt"), g.back(2).done(2))
                    pe.wait_ge(S("node_in"), g.done(2))
                    pe.transpose(ps[r][:, 0:P], tile_in[:, r, 0:P], ident)
                    pe.transpose(ps[r][:, P:2 * P], tile_in[:, r, F_IN:], ident).then_inc(S("node_t"), 1)
                g = of(1)
                if g is not None:
                    r = g.slot(2)
                    pe.wait_ge(S("node_tt"), g.done(2))
                    if g.back(2).exists():
                        pe.wait_ge(S("node_act"), g.back(2).done())
                    pe.matmul(ps[2 + r][:, 0:P], w_node_h, tile_t[0:F_IN, r, 0, :], start=True, stop=False)
                    pe.matmul(ps[2 + r][:, 0:P], w_node_a, tile_t[:, r, 1, :], start=False, stop=True).then_inc(S("node_mid"), 1)
                g = of(2)
                if g is not None:
                    r = g.slot(2)
                    pe.wait_ge(S("node_act"), g.done())
                    if g.back(2).exists():
                        pe.wait_ge(S("node_added"), g.back(2).done())
                    pe.matmul(ps[4 + r][:, 0:F_IN], mid_t[:, r, :], w_out, start=True, stop=True).then_inc(S("node_out"), 1)

            pipelined(pe, NT, 2, node_mlp)

            for n, (heads, ch) in enumerate(LAYERS):
                row, width = row_words(heads, ch), heads * ch
                k_in = F_IN if n == 0 else F_HID

                def gat_tiles(of):
                    g = of(0)
                    if g is not None:
                        if g.back(2).exists():
                            pe.wait_ge(S("gat_tt"), g.back(2).done())
                        pe.wait_ge(S("gat_x"), g.done())
                        pe.transpose(ps[g.slot(2)][:, 0:P], tile_in[:, g.slot(2), 0:P], ident).then_inc(S("gat_t"), 1)
                    g = of(1)
                    if g is not None:
                        pe.wait_ge(S("gat_tt"), g.done())
                        if g.back(2).exists():
                            pe.wait_ge(S("gat_copied"), g.back(2).done())
                        pe.matmul(ps[2 + g.slot(2)][:, 0:width], tile_t[0:k_in, g.slot(2), 0, :], gat_w[n], start=True, stop=True).then_inc(S("gat_mm"), 1)

                pipelined(pe, NT, 1, gat_tiles, n * NT)

                rows_t = 3 * heads
                halves = 2 if heads > 1 else 1
                pe.wait_ge(S("table_ready"), n + 1)
                pe.wait_ge(S("picks_ready"), 6)

                def attend(of):
                    g = of(1)
                    if g is not None:
                        r = g.slot(SLOTS)
                        bank = ps[(4, 7)[g.slot(2)]].bitcast(BF16)
                        if g.back(2).exists():
                            pe.wait_ge(S("turned_copied"), g.back(2).done(2))
                        pe.wait_ge(S("a_hot_ready"), g.done())
                        for u in range(U):
                            pe.transpose(bank[:, u * P:(u + 1) * P], a_hot[:, r, u, :], ident_b)
                        pe.wait_ge(S(f"gathered_{r}"), g.uses(SLOTS, 16 * U))
                        for u in range(U):
                            mm = pe.transpose(bank[:, GE + u * P:GE + (u + 1) * P],
                                              g_rows[:, r, u * row:u * row + P // 2].bitcast(BF16), ident_b)
                        mm.then_inc(S("turned"), 1)
                    g = of(5)
                    if g is not None:
                        pe.wait_ge(S("max_step"), g.done(MAX_STEPS))
                        if g.back(1).exists():
                            pe.wait_ge(S("logit_step"), g.back(1).done(LOGIT_STEPS))
                        lk = look[:, g.slot(4), 0:6 * heads].rearrange("p (k w) -> p k w", k=3)
                        for u in range(U):
                            for part in range(3):
                                mm = pe.matmul(ps[5][:, u * 2 * heads:(u + 1) * 2 * heads], turned[:, g.slot(SLOTS), 0, u * P:(u + 1) * P],
                                               lk[:, part, :], start=(part == 0), stop=(part == 2))
                        mm.then_inc(S("looked_up"), 1)
                    g = of(7)
                    if g is not None:
                        out_w = width + heads
                        pe.wait_ge(S("a_hot_f_ready"), g.done())
                        pe.wait_ge(S("msg_ready"), g.done())
                        if g.back(1).exists():
                            pe.wait_ge(S("a_added"), g.back(1).done())
                        for u in range(U):
                            mm = pe.matmul(ps[6][:, 0:out_w], a_hot_f[:, g.slot(4), u, :], g_msg[:, g.slot(4), u * out_w:(u + 1) * out_w],
                                           start=(u == 0), stop=(u == U - 1))
                        mm.then_inc(S("a_summed"), 1)
                    g = of(2)
                    if g is not None:
                        pe.wait_ge(S("miss_ready"), g.done())
                        pe.wait_ge(S("turned_copied"), g.done(2))
                        for half in range(halves):
                            if halves == 2:
                                if g.back(1).exists():
                                    pe.wait_ge(S(f"half_max{half}"), g.back(1).done())
                            elif g.back(2).exists():
                                pe.wait_ge(S("half_max0"), g.back(2).done())
                            for u in range(half * (U // halves), (half + 1) * (U // halves)):
                                bank = ps[u] if halves == 2 else ps[g.slot(2)]
                                at = 0 if halves == 2 else u * P
                                for h in range(heads):
                                    pe.matmul(bank[:, at + h * P:at + (h + 1) * P], picks[n][:, h, :],
                                              turned[0:rows_t, g.slot(SLOTS), 1, u * P:(u + 1) * P],
                                              start=(at + h == 0), stop=False, skip_group_check=True)
                                if halves == 2:
                                    mm = pe.matmul(bank.rearrange("p (h e) -> p h e", h=heads), miss[:, g.slot(4), u, :],
                                                   neg_ident.unsqueeze(1).broadcast_to([P, heads, P]), start=False, stop=True,
                                                   skip_group_check=True)
                                else:
                                    mm = pe.matmul(bank[:, at:at + P], miss[:, g.slot(4), u, :], neg_ident,
                                                   start=False, stop=(u == U - 1), skip_group_check=True)
                            mm.then_inc(S("shown" if half == halves - 1 else "shown_half"), 1)

                attention_pipeline(pe, 7, attend, n)

        @block.vector
        def _(dve):
            link = Chain(dve, S("dve_step"))
            link(dve.memset(zero, 0.0))
            link(dve.memset(w_edge, 0.0))
            dve.sem_inc(S("zero_ready"), 1)
            dve.wait_ge(S("const1"), 4)
            link(dve.tensor_copy(ident_b, ident))
            link(dve.tensor_copy(lanes_b, lanes))
            link(dve.tensor_scalar(neg_ident, ident, -BIG, None, ALU.mult))
            link(dve.memset(ones3, 1.0))

            for order, (name, key, lane, pos) in enumerate((("s", src_i, lane_s, pos_s), ("d", dst_i, None, pos_d))):
                dve.wait_ge(S("src_in" if order == 0 else "dst_in"), 16)
                link(dve.tensor_scalar(rank.bitcast(I32), key, LANE_BITS, None, ALU.arith_shift_right))
                link(dve.tensor_copy(bucket, rank.bitcast(I32)))
                if name == "s":
                    link(dve.tensor_scalar(rank.bitcast(I32), key, P - 1, None, ALU.bitwise_and))
                    link(dve.tensor_copy(hit, rank.bitcast(I32)))
                    link(dve.tensor_scalar(lane, bucket, float(NT), None, ALU.is_ge))
                    link(dve.tensor_tensor(lane, hit, lane, ALU.subtract))
                else:
                    dve.wait_ge(S("next_in"), 16)
                    link(dve.tensor_tensor(hit, key, pos_d, ALU.is_gt))
                    link(dve.tensor_reduce(falls, hit, op=ALU.add, axis=AX.X))
                    dve.sem_inc(S("falls_ready"), 1)
                with link.loop(NB, 1) as b:
                    link(dve.tensor_scalar(hit, bucket, lanes[:, bass.ds(b, 1)], None, ALU.is_equal, ALU.add,
                                           accum_out=counts[:, bass.ds(b, 1)]))
                dve.sem_inc(S("counts_ready"), 1)
                dve.wait_ge(S("prefix_ready"), order + 1)
                link(dve.tensor_copy(total, ps[7][:, 256:256 + NB]))
                link(dve.tensor_scalar(n_groups_i, ps[7][:, 256:256 + NB], float(GE - 1), None, ALU.add))
                link(dve.tensor_scalar(n_groups_i, n_groups_i, GE_BITS, None, ALU.arith_shift_right))
                link(dve.tensor_copy(n_groups, n_groups_i))
                link(dve.tensor_tensor_scan(first_group, n_groups, zero.broadcast_to([P, NB]), 0.0, ALU.add, ALU.add))
                link(dve.tensor_tensor(first_group, first_group, n_groups, ALU.subtract))
                if name == "s":
                    link(dve.scalar_tensor_tensor(base, first_group, float(GE), ps[7][:, 0:NB], ALU.mult, ALU.add))
                else:
                    link(dve.tensor_tensor_scan(base, total, zero.broadcast_to([P, NB]), 0.0, ALU.add, ALU.add))
                    link(dve.tensor_tensor(base, base, total, ALU.subtract))
                    link(dve.tensor_tensor(base, base, ps[7][:, 0:NB], ALU.add))
                link(dve.tensor_scalar(base, base, -1.0, None, ALU.add))
                link(dve.memset(pos_f, 0.0))
                with link.loop(NB, 4) as b:
                    no = lanes[:, bass.ds(b, 1)]
                    link(dve.tensor_scalar(hit, bucket, no, None, ALU.is_equal))
                    link(dve.tensor_tensor_scan(rank, hit, zero.broadcast_to([P, COLS]), base[:, bass.ds(b, 1)], ALU.add, ALU.add))
                    link(dve.scalar_tensor_tensor(rank, bucket, no, rank, ALU.is_equal, ALU.mult))
                    link(dve.tensor_tensor(pos_f, pos_f, rank, ALU.add))
                link(dve.tensor_copy(pos, pos_f))
                if name == "s":
                    dve.wait_ge(S("dst_in"), 16)
                    link(dve.tensor_scalar(dst_c, dst_i, float(NT * P - 1), None, ALU.min))
                else:
                    link(dve.tensor_copy(edge_d[:, :, 0], dst_i))
                    link(dve.tensor_scalar(edge_d[:, :, 1].bitcast(I32), src_i, float(NT * P - 1), None, ALU.min))
                    dve.wait_ge(S("falls_summed"), 1)
                    link(dve.tensor_scalar(is_sorted, ps[6][0:1, 0:1], 0.0, None, ALU.is_equal))
                dve.sem_inc(S(f"pos_ready_{name}"), 1)
                link(dve.memset(bucket_f, 0.0))
                with link.loop(NT - 1, 1) as b:
                    link(dve.scalar_tensor_tensor(bucket_f, group_no, first_group[:, bass.ds(b + 1, 1)], bucket_f, ALU.is_ge, ALU.add))
                link(dve.tensor_copy(bucket_of[order], bucket_f[0:1, :]))
                if name == "d":
                    link(dve.tensor_scalar(first_node, bucket_f, float(P), None, ALU.mult))
                    link(dve.scalar_tensor_tensor(gap, n_groups, -float(GE), total, ALU.mult, ALU.add))
                    link(dve.tensor_scalar(start_f, group_no, float(GE), None, ALU.mult))
                    with link.loop(NT - 1, 2) as b:
                        link(dve.tensor_scalar(term, group_no, first_group[:, bass.ds(b + 1, 1)], gap[:, bass.ds(b, 1)], ALU.is_ge, ALU.mult))
                        link(dve.tensor_tensor(start_f, start_f, term, ALU.add))
                    link(dve.tensor_scalar(start_f, start_f, float(LINEAR), None, ALU.min))
                    link(dve.tensor_copy(first_edge, start_f[0:1, :]))

            def layer_norm(which):
                if which == 0:
                    dve.wait_ge(S("x_in"), 16)
                link(dve.tensor_reduce(stat[:, 0, :], xs, op=ALU.add, axis=AX.X))
                link(dve.tensor_scalar(stat[:, 0, :], stat[:, 0, :], 1.0 / F_IN, None, ALU.mult))
                link(dve.tensor_tensor(hs, xs, stat[:, 0, :].unsqueeze(2).broadcast_to([P, NT, F_IN]), ALU.subtract))
                sq = tab[:, 0:NT * F_IN].rearrange("p (t f) -> p t f", t=NT)
                link(dve.tensor_tensor(sq, hs, hs, ALU.mult))
                link(dve.tensor_reduce(stat[:, 1, :], sq, op=ALU.add, axis=AX.X))
                link(dve.tensor_scalar(stat[:, 1, :], stat[:, 1, :], 1.0 / F_IN, 1e-5, ALU.mult, ALU.add))
                dve.sem_inc(S("var_ready"), 1)
                dve.wait_ge(S("std_ready"), which + 1)
                link(dve.reciprocal(stat[:, 0, :], stat[:, 1, :]))
                link(dve.tensor_tensor(hs, hs, stat[:, 0, :].unsqueeze(2).broadcast_to([P, NT, F_IN]), ALU.mult))
                link(dve.tensor_scalar(hs, hs, 0.0, None, ALU.max))

            layer_norm(0)
            dve.sem_inc(S("h_ready"), 1)
            dve.wait_ge(S("weights_in"), 16 * N_WEIGHTS)
            link(dve.tensor_copy(b_part[:, 0, :], b_mid))
            link(dve.tensor_tensor(b_rest, b_mid, b_part[:, 0, :], ALU.subtract))
            link(dve.tensor_copy(b_part[:, 1, :], b_rest))
            link(dve.tensor_tensor(b_rest, b_rest, b_part[:, 1, :], ALU.subtract))
            link(dve.tensor_copy(b_part[:, 2, :], b_rest))
            dve.sem_inc(S("b_part_ready"), 1)

            own = tab[:, 0:NT * F_HID].rearrange("p (t f) -> p t f", f=F_HID)

            def own_tiles(of):
                g = of(1)
                if g is not None:
                    dve.wait_ge(S("own_done"), g.done())
                    dve.tensor_copy(own[:, g.at, :], ps[2 + g.slot(2)][:, 0:F_HID]).then_inc(S("own_copied"), 1)

            pipelined(dve, NT, 1, own_tiles)
            dve.wait_ge(S("own_copied"), NT)
            dve.wait_ge(S("arena_free"), 1)
            for part in range(3):
                link(dve.tensor_copy(own_parts[:, :, part, :], own))
                if part < 2:
                    link(dve.tensor_tensor(own, own, own_parts[:, :, part, :], ALU.subtract))
            fills = ROW_GROUPS * GE // (P * FILL)
            dve.wait_ge(S("blank_d_out"), 16)
            dve.wait_ge(S("blank_s_out"), 16 * fills)
            link(dve.memset(acc, 0.0))
            dve.sem_inc(S("own_parts_ready"), 1)

            def edge_mlp(of):
                g = of(0)
                if g is not None:
                    r = g.slot(4)
                    dve.wait_ge(S(f"rec_in{r}"), g.uses(4, 16))
                    dve.tensor_copy(lane_e[:, g.slot(2), :], xg[:, r, :, KX - 3]).then_inc(S("lane_ready"), 1)
                    if g.back(4).exists():
                        dve.wait_ge(S("hot_transposed"), g.back(4).done())
                        dve.wait_ge(S("hot_f_ready"), g.back(4).done())
                    dve.wait_ge(S("lane_ready"), g.done())
                    dve.tensor_tensor(hot[:, r], lanes_b.unsqueeze(1).broadcast_to([P, U, P]),
                                      lane_e[:, g.slot(2), :].unsqueeze(2).broadcast_to([P, U, P]), ALU.is_equal).then_inc(S("hot_ready"), 1)
                    dve.wait_ge(S("hot_transposed"), g.done())
                    if g.back(2).exists():
                        dve.wait_ge(S("hidden1"), g.back(2).done())
                    dve.tensor_copy(hot_t[:, g.slot(2), :], ps[1][:, 0:GE // 2].bitcast(BF16)).then_inc(S("hot_t_ready"), 1)
                g = of(3)
                if g is not None:
                    b = bucket_reg(dve, 0, g)
                    if g.back(1).exists():
                        dve.wait_ge(S("added"), g.back(1).done())
                    dve.wait_ge(S("summed"), g.done())
                    to = agg[:, bass.ds(b, 1), :].rearrange("p a f -> p (a f)")
                    dve.tensor_tensor(to, to, ps[6 + g.slot(2)][:, 0:F_HID], ALU.add).then_inc(S("added"), 1)

            pipelined(dve, GROUPS, 3, edge_mlp)
            dve.wait_ge(S("added"), GROUPS)
            dve.sem_inc(S("mlp_done"), 1)

            link(dve.tensor_tensor(xs, xs, hs, ALU.add))
            link(dve.tensor_tensor(xs, xs, nb2_row.unsqueeze(1).broadcast_to([P, NT, F_IN]), ALU.add))

            def node_mlp(of):
                g = of(2)
                if g is not None:
                    dve.wait_ge(S("node_out"), g.done())
                    dve.tensor_tensor(xs[:, g.at, :], xs[:, g.at, :], ps[4 + g.slot(2)][:, 0:F_IN], ALU.add).then_inc(S("node_added"), 1)

            pipelined(dve, NT, 2, node_mlp)
            dve.wait_ge(S("node_added"), NT)
            layer_norm(1)
            dve.sem_inc(S("gat_in"), 1)

            for n, (heads, ch) in enumerate(LAYERS):
                row, width = row_words(heads, ch), heads * ch
                tb = tab[:, 0:NT * row].rearrange("p (t f) -> p t f", f=row)
                at_s, at_f = part_words(heads), part_words(heads) + heads
                tb_parts = tab[:, 0:NT * row].bitcast(BF16).rearrange("p (t f) -> p t f", t=NT)[
                    :, :, 0:3 * heads].rearrange("p t (k h) -> p t k h", k=3)
                ac = acc[:, 0:NT * (width + heads)].rearrange("p (t h c) -> p t h c", t=NT, h=heads)
                plain = acc[:, 0:NT * width].rearrange("p (t f) -> p t f", t=NT)
                a_s = alpha_s[:, 0:NT * heads].rearrange("p (t h) -> p t h", h=heads)
                a_d = alpha_d[:, 0:NT * heads].rearrange("p (t h) -> p t h", h=heads)
                sh = shift[:, 0:NT * heads].rearrange("p (t h) -> p t h", h=heads)
                rs = rest[:, 0:NT * heads].rearrange("p (t h) -> p t h", h=heads)
                dp = dst_parts[:, 0:NT * 3 * heads].rearrange("p (t k h) -> p t k h", t=NT, k=3)

                def gat_tiles(of):
                    g = of(1)
                    if g is not None:
                        dve.wait_ge(S("gat_mm"), g.done())
                        dve.tensor_copy(tb[:, g.at, at_f:row], ps[2 + g.slot(2)][:, 0:width]).then_inc(S("gat_copied"), 1)

                pipelined(dve, NT, 1, gat_tiles, n * NT)
                dve.wait_ge(S("gat_copied"), NT * (n + 1))
                for vec, to in ((att_s[n], a_s), (att_d[n], a_d)):
                    link(dve.tensor_tensor(plain, tb[:, :, at_f:row], vec.unsqueeze(1).broadcast_to([P, NT, width]), ALU.mult))
                    for h in range(heads):
                        link(dve.tensor_reduce(to[:, :, h], plain[:, :, h * ch:(h + 1) * ch], op=ALU.add, axis=AX.X))
                link(dve.memset(tb[:, :, 0:at_s], 0.0))
                link(dve.tensor_copy(tb[:, :, at_s:at_f], a_s))
                for value, to in ((a_s, tb_parts), (a_d, dp)):
                    link(dve.tensor_copy(rs, value))
                    for part in range(3):
                        link(dve.tensor_copy(to[:, :, part, :], rs))
                        if part < 2:
                            link(dve.tensor_tensor(rs, rs, to[:, :, part, :], ALU.subtract))
                link(dve.tensor_tensor(sh, a_s, a_d, ALU.add))
                link(dve.scalar_tensor_tensor(sh, sh, SLOPE, sh, ALU.mult, ALU.max))
                for h in range(heads):
                    link(dve.tensor_copy(ac[:, :, h, 0:ch], tb[:, :, at_f + h * ch:at_f + (h + 1) * ch]))
                link(dve.memset(ac[:, :, :, ch:ch + 1], 1.0))
                dve.sem_inc(S("table_ready"), 1)

                halves = 2 if heads > 1 else 1

                def one_hots(g):
                    if g is None:
                        return
                    r = g.slot(SLOTS)
                    dve.wait_ge(S(f"ids_in_{r}"), g.uses(SLOTS, 16))
                    dve.tensor_scalar(a_lane[:, g.slot(4), :], ids[:, r, :, 0], first_node[:, bass.ds(g.at, 1)], None, ALU.subtract
                                      ).then_inc(S("a_lane_ready"), 1)
                    yield
                    if g.back(SLOTS).exists():
                        dve.wait_ge(S("turned"), g.back(SLOTS).done())
                        dve.wait_ge(S("a_hot_f_ready"), g.back(SLOTS).done())
                        dve.wait_ge(S("miss_ready"), g.back(SLOTS).done())
                    dve.wait_ge(S("a_lane_ready"), g.done())
                    dve.tensor_tensor(a_hot[:, r], lanes_b.unsqueeze(1).broadcast_to([P, U, P]),
                                      a_lane[:, g.slot(4), :].unsqueeze(2).broadcast_to([P, U, P]), ALU.is_equal
                                      ).then_inc(S("a_hot_ready"), 1)

                def largest_shares(g):
                    if g is None:
                        return
                    halves = 2 if heads > 1 else 1
                    pm = part_max[:, g.slot(4), 0:halves * heads].rearrange("p (k h) -> p k h", k=halves)
                    if halves == 1:
                        dve.wait_ge(S("shown"), g.done())
                        dve.tensor_reduce(pm[:, 0, :], ps[g.slot(2)], op=ALU.max, axis=AX.X).then_inc(S("half_max0"), 1)
                        return
                    for half, name in enumerate(("shown_half", "shown")):
                        shown = ps_all[:, half * 1024:(half + 1) * 1024].rearrange("p (u h e) -> p h u e", u=2, h=heads)
                        dve.wait_ge(S(name), g.done())
                        dve.tensor_reduce(pm[:, half, :], shown, op=ALU.max, axis=AX.XY).then_inc(S(f"half_max{half}"), 1)
                        yield

                def new_shifts(g):
                    if g is None:
                        return
                    step = S("max_step")

                    def after(k):
                        dve.wait_ge(step, g.back(1).done(MAX_STEPS) + k)

                    b = bucket_reg(dve, 1, g)
                    here = sh[:, bass.ds(b, 1), :].rearrange("p a h -> p (a h)")
                    dst_share = a_d[:, bass.ds(b, 1), :].rearrange("p a h -> p (a h)")
                    parts_here = dp[:, bass.ds(b, 1), :, :].rearrange("p a k h -> p (a k) h")
                    r = g.slot(4)
                    lk = look[:, r, 0:6 * heads].rearrange("p (k w) -> p k w", k=3)
                    pm = part_max[:, r, 0:halves * heads].rearrange("p (k h) -> p k h", k=halves)
                    nm, ns = new_max[:, r, 0:heads], new_shift[:, r, 0:heads]
                    lf = left[:, r, 0:heads]
                    if g.back(4).exists():
                        dve.wait_ge(S("looked_up"), g.back(4).done())
                        dve.wait_ge(S("shrink_ready"), g.back(4).done())
                    dve.tensor_scalar(lk[:, :, 0:heads], parts_here, 1.0, None, ALU.mult).then_inc(step, 1)
                    dve.wait_ge(S(f"half_max{halves - 1}"), g.done())
                    dve.tensor_tensor(nm, pm[:, 0, :], pm[:, halves - 1, :], ALU.max).then_inc(step, 1)
                    yield
                    after(2)
                    dve.tensor_tensor(nm, nm, dst_share, ALU.add).then_inc(step, 1)
                    yield
                    after(3)
                    dve.scalar_tensor_tensor(nm, nm, SLOPE, nm, ALU.mult, ALU.max).then_inc(step, 1)
                    yield
                    after(4)
                    dve.tensor_tensor(ns, nm, here, ALU.max).then_inc(step, 1)
                    yield
                    after(5)
                    dve.tensor_tensor(lf, here, ns, ALU.subtract).then_inc(step, 1)
                    dve.tensor_copy(lk[:, 0, heads:], ns).then_inc(step, 1)
                    yield
                    after(7)
                    dve.tensor_scalar(here, ns, 1.0, None, ALU.mult).then_inc(step, 1)
                    dve.tensor_tensor(nm, ns, lk[:, 0, heads:], ALU.subtract).then_inc(step, 1)
                    yield
                    after(9)
                    dve.tensor_copy(lk[:, 1, heads:], nm).then_inc(step, 1)
                    yield
                    after(10)
                    dve.tensor_tensor(lk[:, 2, heads:], nm, lk[:, 1, heads:], ALU.subtract).then_inc(step, 1)

                def logits(g):
                    if g is None:
                        return
                    step = S("logit_step")

                    def after(k):
                        dve.wait_ge(step, g.back(1).done(LOGIT_STEPS) + k)

                    r = g.slot(4)
                    rows = g_rows[:, g.slot(SLOTS), 0:U * row].rearrange("p (u w) -> p u w", u=U)
                    found = ps[5][:, 0:U * 2 * heads].rearrange("p (u w) -> p u w", u=U)
                    lg = logit[:, r, 0:U * heads].rearrange("p (u h) -> p u h", u=U)
                    l2 = logit2[:, r, 0:U * heads].rearrange("p (u h) -> p u h", u=U)
                    dve.wait_ge(S("looked_up"), g.done())
                    dve.tensor_tensor(l2, rows[:, :, at_s:at_f], found[:, :, 0:heads], ALU.add).then_inc(step, 1)
                    yield
                    if g.back(4).exists():
                        dve.wait_ge(S("exp_ready"), g.back(4).done())
                    after(1)
                    dve.scalar_tensor_tensor(lg, l2, SLOPE, l2, ALU.mult, ALU.max).then_inc(step, 1)
                    yield
                    after(2)
                    dve.tensor_tensor(l2, lg, found[:, :, heads:], ALU.subtract).then_inc(step, 1)
                    yield
                    after(3)
                    dve.tensor_scalar(lg, l2, 0.0, None, ALU.min).then_inc(step, 1)

                def messages(g):
                    if g is None:
                        return
                    rows = g_rows[:, g.slot(SLOTS), 0:U * row].rearrange("p (u w) -> p u w", u=U)
                    m = g_msg[:, g.slot(4), 0:U * (width + heads)].rearrange("p (u h c) -> p u h c", u=U, h=heads)
                    dve.wait_ge(S("exp_ready"), g.done())
                    dve.tensor_tensor(m[:, :, :, 0:ch], rows[:, :, at_f:row].rearrange("p u (h c) -> p u h c", h=heads),
                                      m[:, :, :, ch:ch + 1].broadcast_to([P, U, heads, ch]), ALU.mult).then_inc(S("msg_ready"), 1)

                def sums(g):
                    if g is None:
                        return
                    b = bucket_reg(dve, 1, g)
                    to = ac[:, bass.ds(b, 1), :, :].rearrange("p a h c -> p (a h) c")
                    if g.back(1).exists():
                        dve.wait_ge(S("a_added"), g.back(1).done())
                    dve.wait_ge(S("shrink_ready"), g.done())
                    dve.tensor_tensor(to, to, shrink[:, g.slot(SLOTS), 0:heads].unsqueeze(2).broadcast_to([P, heads, ch + 1]), ALU.mult
                                      ).then_inc(S("a_shrunk"), 1)
                    yield
                    dve.wait_ge(S("a_summed"), g.done())
                    dve.wait_ge(S("a_shrunk"), g.done())
                    dve.tensor_tensor(to, to, ps[6][:, 0:width + heads].rearrange("p (h c) -> p h c", h=heads), ALU.add
                                      ).then_inc(S("a_added"), 1)

                def attend(of):
                    hot, large, shifts = one_hots(of(0)), largest_shares(of(3)), new_shifts(of(4))
                    logs, adds = logits(of(6)), sums(of(8))
                    for part in (shifts, hot, logs, shifts, adds, logs, shifts, logs, shifts, adds, logs,
                                 shifts, large, shifts, large):
                        next(part, None)
                    messages(of(6))
                    for part in (shifts, hot, shifts):
                        next(part, None)

                attention_pipeline(dve, 8, attend, n)
                dve.wait_ge(S("a_added"), GROUPS * (n + 1))
                link(dve.tensor_scalar(rs, ac[:, :, :, ch], 1e-16, None, ALU.add))
                link(dve.reciprocal(rs, rs))
                res = tab[:, 0:NT * width].rearrange("p (t f) -> p t f", t=NT)
                for h in range(heads):
                    link(dve.tensor_tensor(res[:, :, h * ch:(h + 1) * ch], ac[:, :, h, 0:ch],
                                           rs[:, :, h:h + 1].broadcast_to([P, NT, ch]), ALU.mult))
                link(dve.tensor_tensor(res, res, gat_b[n].unsqueeze(1).broadcast_to([P, NT, width]), ALU.add))
                if n == 0:
                    link(dve.tensor_scalar(plain, res, 0.0, None, ALU.max))
                    dve.sem_inc(S("gat_in"), 1)
                else:
                    link(dve.tensor_tensor(hs, xs, res, ALU.add))
                    dve.sem_inc(S("out_ready"), 1)


_INS = ["x", "src", "dst", "dst_next", "edge_attr_16", "edge_weight", "L0_gnn_ew1", "L0_gnn_eb1", "L0_gnn_ew2",
        "L0_gnn_eb2", "L0_gnn_nw1", "L0_gnn_nb1", "L0_gnn_nw2", "L0_gnn_nb2", "L1_gnn_W1",
        "L1_gnn_a_src1", "L1_gnn_a_dst1", "L1_gnn_b1", "L1_gnn_W2", "L1_gnn_a_src2",
        "L1_gnn_a_dst2", "L1_gnn_b2"]


def kernel(**inputs):
    import numpy as np
    import concourse.bacc as bacc
    from concourse.bass_utils import run_bass_kernel_spmd

    def padded(a, rows, fill):
        full = np.full((rows,) + a.shape[1:], fill, a.dtype)
        full[:a.shape[0]] = a
        return full

    nc = bacc.Bacc("TRN2", target_bir_lowering=False, num_devices=1)
    arrays, args = {}, []
    for name in _INS:
        a = np.ascontiguousarray(inputs["dst"][1:] if name == "dst_next" else inputs[name])
        if name == "x":
            a = padded(a, NT * P, 0)
        elif name in ("src", "dst", "dst_next"):
            a = padded(a, COLS * P, NT * P)
        elif name.startswith("edge"):
            a = padded(a, COLS * P, 0)
        arrays[f"in_{name}"] = a
        args.append(nc.dram_tensor(f"in_{name}", a.shape, mybir.dt.from_np(a.dtype), kind="ExternalInput").ap())
    args.append(nc.dram_tensor("out_0", (NT * P, F_IN), F32, kind="ExternalOutput").ap())
    gnn_kernel(nc, *args)
    r = run_bass_kernel_spmd(nc, [arrays], core_ids=[0])
    return r.results[0]["out_0"][:N_NODES]
```

```python
import concourse.bass as bass
from concourse import mybir
from contextlib import ExitStack, contextmanager

F32 = mybir.dt.float32
BF16 = mybir.dt.bfloat16
I32 = mybir.dt.int32
ALU = mybir.AluOpType
ACT = mybir.ActivationFunctionType
AX = mybir.AxisListType

P = 128
N_NODES, N_EDGES = 6250, 206250
F_IN, F_HID, F_EDGE, CUTOFF = 64, 128, 16, 5.0
HEADS, CH, OUT_DIM, SLOPE = 4, 32, 64, 0.2
NT = -(-N_NODES // P)
NB = NT + 1
LANE_BITS = 7
COLS = -(-N_EDGES // P // 52) * 52
U = 4
GE = P * U
GE_BITS = 9
GROUPS = (N_EDGES + NT * (GE - 1)) // GE + 1
ROW_GROUPS = GROUPS + 2
BATCH = 26
REC = F_EDGE + 4
KX = F_IN + REC
BIG = float(2 ** 100)
PEEL = 8
UNROLL = 4
CODE = 16
CODE_WORDS = CODE // 2
SLOTS = 8
MAX_STEPS, LOGIT_STEPS = 10, 4
N_WEIGHTS = 19
LAYERS = ((HEADS, CH), (1, OUT_DIM))
LINEAR = COLS * P


def part_words(heads):
    return -(-3 * heads // 2)


def row_words(heads, ch):
    return part_words(heads) + heads * (ch + 1)



class Group:

    def __init__(self, i, off, before):
        self.i, self.off, self.before = i, off, before
        self.at = off if i is None else i + off

    def slot(self, n):
        return self.off % n

    def done(self, per=1):
        n = per * (self.before + self.off + 1)
        return n if self.i is None else self.i * per + n

    def uses(self, slots, per):
        earlier = (self.before - self.slot(slots) + slots - 1) // slots
        n = per * (earlier + self.off // slots + 1)
        return n if self.i is None else self.i * (per // slots) + n

    def back(self, n):
        return Group(self.i, self.off - n, self.before)

    def exists(self):
        return self.i is not None or self.off >= 0


def pipelined(eng, items, depth, step, before=0, peel=PEEL, unroll=UNROLL, each_round=None):
    def lookup(i, t):
        def group_of(stage):
            if i is None and not 0 <= t - stage < items:
                return None
            return Group(i, t - stage, before)
        return group_of

    for t in range(peel):
        step(lookup(None, t))
    rounds = (items - peel) // unroll
    with eng.Fori(0, rounds) as turn:
        i = turn * unroll + peel
        if each_round is not None:
            each_round(i)
        for k in range(unroll):
            step(lookup(i, k))
    for t in range(peel + rounds * unroll, items + depth):
        step(lookup(None, t))


def attention_pipeline(eng, depth, step, layer, each_round=None):
    pipelined(eng, GROUPS, depth, step, layer * GROUPS, peel=2 * SLOTS, unroll=SLOTS, each_round=each_round)


class Chain:

    def __init__(self, eng, sem):
        self.eng, self.sem, self.count, self.shift = eng, sem, 0, 0

    def __call__(self, ins):
        self.count += 1
        ins.then_inc(self.sem, 1)
        self.eng.wait_ge(self.sem, self.shift + self.count)

    @contextmanager
    def loop(self, times, per):
        first = self.count
        with self.eng.Fori(0, times) as i:
            self.shift = i * per
            yield i
        assert self.count - first == per
        self.shift, self.count = 0, first + times * per


def gnn_kernel(nc, x, src, dst, dst_next, attr, ew, ew1, eb1, ew2, eb2, nw1, nb1, nw2, nb2,
               W1, a_src1, a_dst1, b1, W2, a_src2, a_dst2, b2, out):
    ctx = ExitStack()
    with ctx:
        def sb(name, shape, dt=F32):
            return ctx.enter_context(nc.sbuf_tensor(name, shape, dt))[tuple(slice(None) for _ in shape)]

        def pb(name):
            return ctx.enter_context(nc.psum_tensor(name, [P, 512], F32))[:, :]

        def sem(name):
            return ctx.enter_context(nc.semaphore(name))

        def dram(name, shape, dt=F32):
            return nc.dram_tensor(name, shape, dt, kind="Internal").ap()

        rec_s = dram("rec_s", [ROW_GROUPS * GE, REC])
        rec_d = dram("rec_d", [LINEAR + GE, 2])
        h_table = dram("h_table", [NT * P, F_IN])
        tables = [dram(f"table{n}", [NT * P, row_words(*layer)]) for n, layer in enumerate(LAYERS)]

        xs = sb("xs", [P, NT, F_IN])
        hs = sb("hs", [P, NT, F_IN])
        acc = sb("acc", [P, NT * (F_HID + HEADS)])
        tab = sb("tab", [P, NT * row_words(*LAYERS[0])])
        alpha_s = sb("alpha_s", [P, NT * HEADS])
        alpha_d = sb("alpha_d", [P, NT * HEADS])
        shift = sb("shift", [P, NT * HEADS])
        rest = sb("rest", [P, NT * HEADS])
        dst_parts = sb("dst_parts", [P, NT * 3 * HEADS], BF16)
        stat = sb("stat", [P, 2, NT])
        ident = sb("ident", [P, P])
        ident_b = sb("ident_b", [P, P], BF16)
        bit_masks = sb("bit_masks", [P, CODE], I32)
        lane_no = sb("lane_no", [P, CODE], I32)
        lane_code = sb("lane_code", [P, P])
        lanes = sb("lanes", [P, P])
        lanes_b = sb("lanes_b", [P, P], BF16)
        picks = [sb(f"pick{n}", [CODE + 3 * h, h, P], BF16) for n, (h, _) in enumerate(LAYERS)]
        lower = sb("lower", [P, P])
        ones = sb("ones", [P, P])
        ones3 = sb("ones3", [3, P], BF16)
        zero = sb("zero", [P, 1])
        w_edge = sb("w_edge", [KX, F_HID])
        w_own = sb("w_own", [F_IN, F_HID])
        w_mid = sb("w_mid", [F_HID, F_HID])
        b_mid = sb("b_mid", [1, F_HID])
        b_rest = sb("b_rest", [1, F_HID])
        b_part = sb("b_part", [1, 3, F_HID], BF16)
        b_rows = sb("b_rows", [3, F_HID], BF16)
        w_node_h = sb("w_node_h", [F_IN, F_HID])
        w_node_a = sb("w_node_a", [F_HID, F_HID])
        w_out = sb("w_out", [F_HID, F_IN])
        nb1_col = sb("nb1_col", [F_HID, 1])
        nb2_row = sb("nb2_row", [P, F_IN])
        gat_w = [sb("gat_w1", [F_IN, F_HID]), sb("gat_w2", [F_HID, OUT_DIM])]
        att_s = [sb("att_s1", [P, F_HID]), sb("att_s2", [P, OUT_DIM])]
        att_d = [sb("att_d1", [P, F_HID]), sb("att_d2", [P, OUT_DIM])]
        gat_b = [sb("gat_b1", [P, F_HID]), sb("gat_b2", [P, OUT_DIM])]
        bucket_of = [sb(f"bucket_of{k}", [1, ROW_GROUPS + 2], I32) for k in range(2)]
        first_edge = sb("first_edge", [1, ROW_GROUPS], I32)
        first_node = sb("first_node", [P, ROW_GROUPS])
        group_no = sb("group_no", [P, ROW_GROUPS])
        bucket_f = sb("bucket_f", [P, ROW_GROUPS])
        start_f = sb("start_f", [P, ROW_GROUPS])
        room = sb("room", [P, ROW_GROUPS])
        total = sb("total", [P, NB])
        gap = sb("gap", [P, NB])
        falls = sb("falls", [P, 1])
        is_sorted = sb("is_sorted", [1, 1], I32)
        counts = sb("counts", [P, NB])
        n_groups_i = sb("n_groups_i", [P, NB], I32)
        n_groups = sb("n_groups", [P, NB])
        first_group = sb("first_group", [P, NB])
        base = sb("base", [P, NB])
        tile_in = sb("tile_in", [P, 2, F_IN + F_HID])
        tile_t = sb("tile_t", [P, 2, 2, P])
        mid_t = sb("mid_t", [P, 2, P])
        ARENA = 22900
        arena = sb("arena", [P, ARENA])

        def carve(start, shape, dt=F32):
            words = 1
            for n in shape:
                words *= n
            words = words if dt != BF16 else words // 2
            v = arena[:, start:start + words]
            assert start + words <= ARENA, (start, shape)
            if dt != F32:
                v = v.bitcast(dt)
            names = " ".join("abcd"[:len(shape)])
            kw = {"abcd"[n]: shape[n] for n in range(len(shape))}
            return v.rearrange(f"p ({names}) -> p {names}", **kw), start + words

        at = 0
        src_i, at = carve(at, [COLS], I32)
        dst_i, at = carve(at, [COLS], I32)
        weight, at = carve(at, [COLS])
        bucket, at = carve(at, [COLS])
        lane_s, at = carve(at, [COLS])
        edge_d, at = carve(at, [COLS, 2])
        pos_s, at = carve(at, [COLS], I32)
        pos_d, at = carve(at, [COLS], I32)
        pos_f, at = carve(at, [COLS])
        hit, at = carve(at, [COLS])
        rank, at = carve(at, [COLS])
        dst_c, at = carve(at, [COLS], I32)
        places = [rank, dst_c.bitcast(F32)]
        attr_in = [None, None]
        rec_out = [None, None]
        rec2_out = [sb(f"rec2_out{k}", [P, BATCH, 2]) for k in range(2)]
        where = [sb(f"where{k}", [P, BATCH], I32) for k in range(2)]
        for k in range(2):
            rec_out[k], at = carve(at, [BATCH, REC])
            attr_in[k], at = carve(at, [BATCH, F_EDGE])
        FILL = 227
        assert ROW_GROUPS * GE % (P * FILL) == 0
        blank_s = acc[:, 0:FILL * REC].rearrange("p (r w) -> p r w", w=REC)
        blank_d = acc[:, FILL * REC:FILL * REC + U * 2].rearrange("p (r w) -> p r w", w=2)

        at = 0
        own_parts, at = carve(at, [NT, 3, F_HID], BF16)
        xg, at = carve(at, [4, U, KX])
        hot, at = carve(at, [4, U, P], BF16)
        hot_f, at = carve(at, [4, U, P])
        hot_t, at = carve(at, [2, GE], BF16)
        x_t, at = carve(at, [2, GE])
        mid_e, at = carve(at, [2, GE])
        msg, at = carve(at, [2, U, F_HID])
        lane_e, at = carve(at, [2, U], BF16)
        at = 0
        a_hot, at = carve(at, [SLOTS, U, P], BF16)
        a_hot_f, at = carve(at, [4, U, P])
        turned, at = carve(at, [SLOTS, 2, GE], BF16)
        lane_int, at = carve(at, [4, U], I32)
        lane_bits, at = carve(at, [4, U, CODE], I32)
        ids, at = carve(at, [SLOTS, U, 2])
        neg_lane, at = carve(at, [4, U])
        lane_gap, at = carve(at, [2, U, P], BF16)
        logit, at = carve(at, [4, U * HEADS])
        logit2, at = carve(at, [4, U * HEADS])
        part_max, at = carve(at, [4, HEADS])
        new_max, at = carve(at, [4, HEADS])
        new_shift, at = carve(at, [4, HEADS])
        shrink, at = carve(at, [SLOTS, HEADS])
        left, at = carve(at, [4, HEADS])
        look, at = carve(at, [4, 3 * 2 * HEADS], BF16)
        g_rows, at = carve(at, [SLOTS, U * (CODE_WORDS + row_words(*LAYERS[0]))])
        g_msg, at = carve(at, [4, U * (F_HID + HEADS)])

        ps_all = ctx.enter_context(nc.psum_tensor("ps_all", [P, 8 * 512], F32))[:, :]
        ps = [ps_all[:, 512 * n:512 * (n + 1)] for n in range(8)]

        s = {}

        def S(name):
            if name not in s:
                s[name] = sem(name)
            return s[name]

        agg = acc[:, 0:NT * F_HID].rearrange("p (t f) -> p t f", f=F_HID)

        block = ctx.enter_context(nc.Block())

        def bucket_reg(eng, order, g):
            return eng.value_load(bucket_of[order][0:1, bass.ds(g.at, 1)], min_val=0, max_val=NT - 1)

        class Buckets:

            def __init__(self, eng, engine, order, back, count):
                self.eng, self.engine, self.order, self.back, self.count = eng, engine, order, back, count

            def load(self, i):
                _, self.values = nc.values_load_multi_w_load_instructions(
                    bucket_of[self.order][0:1, bass.ds(i - self.back, self.count)], engines=(self.engine,), min_val=0, max_val=NT - 1,
                    skip_runtime_bounds_check_because="a bucket is a count of at most NT - 1 comparisons")

            def of(self, g):
                return bucket_reg(self.eng, self.order, g) if g.i is None else self.values[g.off + self.back]

        @block.sync
        def _(sp):
            sp.dma_start(src_i, src.rearrange("(p j) -> p j", p=P)).then_inc(S("src_in"), 16)
            sp.dma_start(dst_i, dst.rearrange("(p j) -> p j", p=P)).then_inc(S("dst_in"), 16)
            sp.dma_start(pos_d, dst_next.rearrange("(p j) -> p j", p=P)).then_inc(S("next_in"), 16)
            sp.dma_start(weight, ew.rearrange("(p j) -> p j", p=P)).then_inc(S("weight_in"), 16)
            sp.dma_start(xs, x.rearrange("(t p) f -> p t f", p=P)).then_inc(S("x_in"), 16)
            loads = [
                (w_own, ew1[0:F_IN, :]), (w_edge[0:F_IN, :], ew1[F_IN:2 * F_IN, :]),
                (w_edge[F_IN:F_IN + F_EDGE + 1, :], ew1[2 * F_IN:, :]),
                (w_edge[KX - 1:KX, :], eb1.rearrange("(a n) -> a n", a=1)),
                (w_mid, ew2), (b_mid, eb2.rearrange("(a n) -> a n", a=1)),
                (w_node_h, nw1[0:F_IN, :]), (w_node_a, nw1[F_IN:, :]), (w_out, nw2),
                (nb1_col, nb1.rearrange("(n a) -> n a", a=1)),
                (nb2_row, nb2.rearrange("(a n) -> a n", a=1).broadcast_to([P, F_IN])),
                (gat_w[0], W1), (gat_w[1], W2),
                (gat_b[0], b1.rearrange("(a n) -> a n", a=1).broadcast_to([P, F_HID])),
                (gat_b[1], b2.rearrange("(a n) -> a n", a=1).broadcast_to([P, OUT_DIM])),
                (att_s[0], a_src1.rearrange("a h c -> a (h c)").broadcast_to([P, F_HID])),
                (att_s[1], a_src2.rearrange("a h c -> a (h c)").broadcast_to([P, OUT_DIM])),
                (att_d[0], a_dst1.rearrange("a h c -> a (h c)").broadcast_to([P, F_HID])),
                (att_d[1], a_dst2.rearrange("a h c -> a (h c)").broadcast_to([P, OUT_DIM])),
            ]
            assert len(loads) == N_WEIGHTS
            sp.wait_ge(S("zero_ready"), 1)
            for to, what in loads:
                sp.dma_start(to, what).then_inc(S("weights_in"), 16)
            sp.wait_ge(S("blank_ready"), 2)
            n = ROW_GROUPS * GE // (P * FILL)
            to_s = rec_s.rearrange("(p n r) w -> n p (r w)", p=P, n=n)
            for k in range(n):
                sp.dma_start(to_s[k], blank_s.rearrange("p r w -> p (r w)")).then_inc(S("blank_s_out"), 16)
            sp.dma_start(rec_d[LINEAR:, :].rearrange("(p r) w -> p (r w)", p=P),
                         blank_d.rearrange("p r w -> p (r w)")).then_inc(S("blank_d_out"), 16)
            at_v = attr.rearrange("(p j) f -> p (j f)", p=P)
            with sp.Fori(0, COLS // BATCH // 2) as i:
                for k in range(2):
                    sp.wait_ge(S("attr_used"), 2 * i + k + 1)
                    sp.dma_start(attr_in[k].rearrange("p u w -> p (u w)"),
                                 at_v[:, bass.ds((2 * i + k) * (BATCH * F_EDGE), BATCH * F_EDGE)]
                                 ).then_inc(S(f"attr_in{k}"), 16)
            sp.wait_ge(S("h_ready"), 1)
            sp.dma_start(h_table.rearrange("(t p) f -> p t f", p=P), hs).then_inc(S("h_table_out"), 16)

            sp.wait_ge(S("b_part_ready"), 1)
            sp.dma_start(b_rows, b_part.rearrange("a k f -> a (k f)")).then_inc(S("b_rows_in"), 16)

            sp.wait_ge(S("sorted_s"), 1)
            sp.wait_ge(S("arena_free"), 1)
            rs = rec_s.rearrange("(g p u) w -> g p u w", p=P, u=U)

            def load_records(of):
                g = of(0)
                if g is None:
                    return
                if g.back(4).exists():
                    sp.wait_ge(S("x_transposed"), g.back(4).done())
                    sp.wait_ge(S("lane_ready"), g.back(4).done())
                sp.dma_start(xg[:, g.slot(4), :, F_IN:KX], rs[bass.ds(g.at, 1)].rearrange("a p u w -> p (a u) w")
                             ).then_inc(S(f"rec_in{g.slot(4)}"), 16)

            pipelined(sp, GROUPS, 0, load_records)

            for n, (heads, ch) in enumerate(LAYERS):
                row = row_words(heads, ch)
                sp.wait_ge(S("table_ready"), n + 1)
                sp.dma_start(tables[n].rearrange("(t p) f -> p t f", p=P),
                             tab[:, 0:NT * row].rearrange("p (t f) -> p t f", f=row)).then_inc(S("table_out"), 16)
                if n == 0:
                    sp.wait_ge(S("sorted_d"), 1)

                def load_ids(of):
                    g = of(0)
                    if g is None:
                        return
                    first = sp.value_load(first_edge[0:1, bass.ds(g.at, 1)], min_val=0, max_val=LINEAR)
                    r = g.slot(SLOTS)
                    if g.back(SLOTS).exists():
                        sp.wait_ge(S("a_lane_ready"), g.back(SLOTS).done(2))
                        sp.sem_inc(S("sp_go"), 1)
                        sp.wait_ge(S(f"gathered_{r}"), g.back(SLOTS).uses(SLOTS, 16 * U))
                        sp.sem_inc(S("sp_go"), 1)
                    sp.dma_start(ids[:, r, :, :].rearrange("p u w -> p (u w)"),
                                 rec_d[bass.ds(first, GE), :].rearrange("(p u) w -> p (u w)", u=U)
                                 ).then_inc(S(f"ids_in_{r}"), 16)

                attention_pipeline(sp, 0, load_ids, n)

            sp.wait_ge(S("out_ready"), 1)
            sp.dma_start(out.rearrange("(t p) f -> p t f", p=P), hs).then_inc(S("out_done"), 16)
            sp.wait_ge(S("out_done"), 16)

        @block.gpsimd
        def _(pool):
            pool.memset(ident, 0.0).then_inc(S("const0"), 1)
            pool.memset(lower, 1.0).then_inc(S("const0"), 1)
            pool.memset(ones, 1.0).then_inc(S("const0"), 1)
            pool.memset(tile_in, 0.0).then_inc(S("const0"), 1)
            pool.wait_ge(S("const0"), 4)
            pool.affine_select(out=ident, in_=ident, compare_op=ALU.not_equal, fill=1.0, base=0,
                               pattern=[[-1, P]], channel_multiplier=1).then_inc(S("const1"), 1)
            pool.affine_select(out=lower, in_=lower, compare_op=ALU.is_gt, fill=0.0, base=0,
                               pattern=[[1, P]], channel_multiplier=-1).then_inc(S("const1"), 1)
            pool.iota(lanes, [[1, P]], base=0, channel_multiplier=0,
                      allow_small_or_imprecise_dtypes=True).then_inc(S("const1"), 1)
            pool.iota(group_no, [[1, ROW_GROUPS]], base=0, channel_multiplier=0,
                      allow_small_or_imprecise_dtypes=True).then_inc(S("const1"), 1)
            pool.iota(lane_no, [[0, CODE]], base=0, channel_multiplier=1).then_inc(S("const1"), 1)
            pool.memset(blank_s, 0.0).then_inc(S("blank0"), 1)
            pool.memset(blank_d, 0.0).then_inc(S("blank0"), 1)
            for pick in picks:
                pool.memset(pick, 0.0).then_inc(S("pick0"), 1)
            for k in range(2):
                pool.memset(rec_out[k][:, :, REC - 1:REC], 1.0).then_inc(S("blank0"), 1)
            pool.wait_ge(S("blank0"), 4)
            pool.memset(blank_s[:, :, REC - 3:REC - 2], -1.0).then_inc(S("blank_ready"), 1)
            pool.memset(blank_d[:, :, 0:1], -1.0).then_inc(S("blank_ready"), 1)

            def tile_inputs(ready, count, name, sources, transposed, before=0):
                pool.wait_ge(S(ready), count)

                def copy(of):
                    g = of(0)
                    if g is None:
                        return
                    if g.back(2).exists():
                        pool.wait_ge(S(transposed), g.back(2).done())
                    at = 0
                    for rows, width in sources:
                        pool.tensor_copy(tile_in[:, g.slot(2), at:at + width],
                                         rows[:, bass.ds(g.at, 1), 0:width].rearrange("p a f -> p (a f)")
                                         ).then_inc(S(name), 1)
                        at += width

                pipelined(pool, NT, 0, copy, before)

            pool.wait_ge(S("pick0"), 2)
            for n, (heads, _) in enumerate(LAYERS):
                for part in range(3):
                    pool.affine_select(out=picks[n], in_=picks[n], compare_op=ALU.not_equal, fill=1.0,
                                       base=-CODE - heads * part, pattern=[[-1, heads], [0, P]],
                                       channel_multiplier=1).then_inc(S("picks_ready"), 1)
                    pool.wait_ge(S("picks_ready"), 3 * n + part + 1)

            assert NB % 2 == 0
            pool.sem_inc(S("places_added"), 2)
            with pool.Fori(0, NB // 2) as pair:
                for k in range(2):
                    pool.wait_ge(S("places_ready"), 2 * pair + k + 1)
                    pool.wait_ge(S("places_added"), 2 * pair + k + 2)
                    pool.tensor_tensor(pos_f, pos_f, places[k], ALU.add).then_inc(S("places_added"), 1)

            fills = ROW_GROUPS * GE // (P * FILL)
            pool.wait_ge(S("blank_s_out"), 16 * fills)
            with pool.Fori(0, COLS // BATCH // 2) as i:
                for k in range(2):
                    pool.wait_ge(S("staged_s"), 2 * i + k + 1)
                    pool.sem_inc(S("pool_go"), 1)
                    for c in range(BATCH):
                        pool.indirect_dma_start(
                            rec_s, bass.IndirectOffsetOnAxis(ap=where[k][:, c:c + 1], axis=0),
                            rec_out[k][:, c, :], None).then_inc(S(f"sorted_s_slot{k}"), 16)
            for k in range(2):
                pool.wait_ge(S(f"sorted_s_slot{k}"), 16 * COLS // 2)
            pool.sem_inc(S("sorted_s"), 1)

            pool.wait_ge(S("pos_ready_d"), 1)
            in_order = pool.value_load(is_sorted[0:1, 0:1], min_val=0, max_val=1)
            with pool.If(in_order):
                pool.dma_start(rec_d[0:LINEAR, :].rearrange("(p j) w -> p (j w)", p=P),
                               edge_d.rearrange("p j w -> p (j w)")).then_inc(S("copied_d"), 16)
                pool.wait_ge(S("copied_d"), 16)
            with pool.Else():
                def scatter_d(i):
                    for k in range(2):
                        cols = bass.ds((2 * i + k) * BATCH, BATCH)
                        if not (isinstance(i, int) and i == 0):
                            pool.wait_ge(S(f"sorted_d_slot{k}"), i * (16 * BATCH))
                        pool.tensor_copy(where[k], pos_d[:, cols]).then_inc(S("staged_d"), 1)
                        pool.tensor_copy(rec2_out[k], edge_d[:, cols, :]).then_inc(S("staged_d"), 1)
                        pool.wait_ge(S("staged_d"), 4 * i + 2 * k + 2)
                        pool.sem_inc(S("pool_go"), 1)
                        for c in range(BATCH):
                            pool.indirect_dma_start(
                                rec_d, bass.IndirectOffsetOnAxis(ap=where[k][:, c:c + 1], axis=0),
                                rec2_out[k][:, c, :], None).then_inc(S(f"sorted_d_slot{k}"), 16)

                scatter_d(0)
                with pool.Fori(1, COLS // BATCH // 2) as i:
                    scatter_d(i)
                for k in range(2):
                    pool.wait_ge(S(f"sorted_d_slot{k}"), 16 * COLS // 2)
            pool.wait_ge(S("blank_d_out"), 16)
            pool.sem_inc(S("sorted_d"), 1)
            pool.sem_inc(S("arena_free"), 1)

            tile_inputs("h_ready", 1, "own_in", [(hs, F_IN)], "own_t")
            pool.wait_ge(S("h_table_out"), 16)
            pool.wait_ge(S("arena_free"), 1)

            def gather_h(of):
                g = of(0)
                if g is None:
                    return
                pool.wait_ge(S(f"rec_in{g.slot(4)}"), g.uses(4, 16))
                pool.sem_inc(S("pool_go"), 1)
                for u in range(U):
                    pool.indirect_dma_start(
                        xg[:, g.slot(4), u, 0:F_IN], None, h_table,
                        bass.IndirectOffsetOnAxis(
                            ap=xg[:, g.slot(4), u, KX - 2:KX - 1].bitcast(I32), axis=0)
                    ).then_inc(S(f"h_in{g.slot(4)}"), 16)

            pipelined(pool, GROUPS, 0, gather_h)

            tile_inputs("mlp_done", 1, "node_in", [(hs, F_IN), (agg, F_HID)], "node_t")
            for n, (heads, ch) in enumerate(LAYERS):
                row = row_words(heads, ch)
                node_in = hs if n == 0 else acc[:, 0:NT * F_HID].rearrange("p (t f) -> p t f", t=NT)
                tile_inputs("gat_in", n + 1, "gat_x", [(node_in, F_HID if n else F_IN)], "gat_t", n * NT)
                pool.wait_ge(S("table_out"), 16 * (n + 1))

                step = CODE_WORDS + row

                def gather_rows(of):
                    g = of(0)
                    if g is None:
                        return
                    r = g.slot(SLOTS)
                    if g.back(SLOTS).exists():
                        pool.wait_ge(S("msg_ready"), g.back(SLOTS).done())
                        pool.wait_ge(S("turned"), g.back(SLOTS).done())
                    pool.wait_ge(S(f"ids_in_{r}"), g.uses(SLOTS, 16))
                    pool.sem_inc(S("pool_go"), 1)
                    for u in range(U):
                        pool.indirect_dma_start(
                            g_rows[:, r, u * step + CODE_WORDS:(u + 1) * step], None, tables[n],
                            bass.IndirectOffsetOnAxis(ap=ids[:, r, u, 1:2].bitcast(I32), axis=0)
                        ).then_inc(S(f"gathered_{r}"), 16)

                attention_pipeline(pool, 0, gather_rows, n)

        @block.scalar
        def _(act):
            act.sem_inc(S("attr_used"), 2)
            act.wait_ge(S("pos_ready_s"), 1)
            act.wait_ge(S("weight_in"), 16)

            def stage(i):
                for k in range(2):
                    cols = bass.ds((2 * i + k) * BATCH, BATCH)
                    if not (isinstance(i, int) and i == 0):
                        act.wait_ge(S(f"sorted_s_slot{k}"), i * (16 * BATCH))
                    rec = rec_out[k]
                    act.activation(rec[:, :, F_EDGE], weight[:, cols], ACT.Copy, scale=1.0 / CUTOFF).then_inc(S("staging"), 1)
                    act.activation(rec[:, :, F_EDGE + 1], lane_s[:, cols], ACT.Copy).then_inc(S("staging"), 1)
                    act.activation(rec[:, :, F_EDGE + 2].bitcast(I32), dst_c[:, cols], ACT.Copy).then_inc(S("staging"), 1)
                    act.activation(where[k], pos_s[:, cols], ACT.Copy).then_inc(S("staging"), 1)
                    act.wait_ge(S(f"attr_in{k}"), 16 * i + 16)
                    act.activation(rec[:, :, 0:F_EDGE], attr_in[k], ACT.Copy).then_inc(S("attr_used"), 1)
                    act.wait_ge(S("attr_used"), 2 * i + k + 3)
                    act.wait_ge(S("staging"), 8 * i + 4 * (k + 1))
                    act.sem_inc(S("staged_s"), 1)

            stage(0)
            with act.Fori(1, COLS // BATCH // 2) as i:
                stage(i)

            act.wait_ge(S("var_ready"), 1)
            act.activation(stat[:, 1, :], stat[:, 1, :], ACT.Sqrt).then_inc(S("std_ready"), 1)

            def own_tiles(of):
                g = of(0)
                if g is not None:
                    if g.back(2).exists():
                        act.wait_ge(S("own_done"), g.back(2).done())
                    act.wait_ge(S("own_t"), g.done())
                    act.activation(tile_t[0:F_IN, g.slot(2), 0, :], ps[g.slot(2)][0:F_IN, 0:P], ACT.Copy).then_inc(S("own_tt"), 1)

            pipelined(act, NT, 0, own_tiles)

            def edge_mlp(of):
                g = of(3)
                if g is not None:
                    act.wait_ge(S("hidden2"), g.done())
                    if g.back(2).exists():
                        act.wait_ge(S("summed"), g.back(2).done())
                    act.activation(msg[:, g.slot(2)].rearrange("p u f -> p (u f)"), ps[4 + g.slot(2)][:, :], ACT.Silu).then_inc(S("message_ready"), 1)
                g = of(2)
                if g is not None:
                    act.wait_ge(S("hot_ready"), g.done())
                    if g.back(4).exists():
                        act.wait_ge(S("summed"), g.back(4).done())
                    act.activation(hot_f[:, g.slot(4)], hot[:, g.slot(4)], ACT.Copy).then_inc(S("hot_f_ready"), 1)
                    act.wait_ge(S("hidden1"), g.done())
                    if g.back(2).exists():
                        act.wait_ge(S("hidden2"), g.back(2).done())
                    act.activation(mid_e[:, g.slot(2), :], ps[2 + g.slot(2)][:, :], ACT.Silu).then_inc(S("mid_ready"), 1)
                g = of(1)
                if g is not None:
                    act.wait_ge(S("x_transposed"), g.done())
                    if g.back(2).exists():
                        act.wait_ge(S("hidden1"), g.back(2).done())
                    act.activation(x_t[0:KX, g.slot(2), :], ps[0][0:KX, :], ACT.Copy).then_inc(S("x_t_ready"), 1)

            pipelined(act, GROUPS, 3, edge_mlp)

            def node_mlp(of):
                g = of(0)
                if g is not None:
                    act.wait_ge(S("node_t"), g.done())
                    if g.back(2).exists():
                        act.wait_ge(S("node_mid"), g.back(2).done())
                    act.activation(tile_t[0:F_IN, g.slot(2), 0, :], ps[g.slot(2)][0:F_IN, 0:P], ACT.Copy).then_inc(S("node_tt"), 1)
                    act.activation(tile_t[:, g.slot(2), 1, :], ps[g.slot(2)][:, P:2 * P], ACT.Copy).then_inc(S("node_tt"), 1)
                g = of(1)
                if g is not None:
                    act.wait_ge(S("node_mid"), g.done())
                    if g.back(2).exists():
                        act.wait_ge(S("node_out"), g.back(2).done())
                    act.activation(mid_t[:, g.slot(2), :], ps[2 + g.slot(2)][:, 0:P], ACT.Silu, bias=nb1_col).then_inc(S("node_act"), 1)

            pipelined(act, NT, 1, node_mlp)
            act.wait_ge(S("var_ready"), 2)
            act.activation(stat[:, 1, :], stat[:, 1, :], ACT.Sqrt).then_inc(S("std_ready"), 1)

            for n, (heads, ch) in enumerate(LAYERS):
                width = heads * ch
                k_in = F_IN if n == 0 else F_HID

                def gat_tiles(of):
                    g = of(0)
                    if g is not None:
                        act.wait_ge(S("gat_t"), g.done())
                        if g.back(2).exists():
                            act.wait_ge(S("gat_mm"), g.back(2).done())
                        act.activation(tile_t[0:k_in, g.slot(2), 0, :], ps[g.slot(2)][0:k_in, 0:P], ACT.Copy).then_inc(S("gat_tt"), 1)

                pipelined(act, NT, 0, gat_tiles, n * NT)

                def attend(of):
                    g = of(5)
                    if g is not None:
                        act.wait_ge(S("max_step"), g.done(MAX_STEPS))
                        if g.back(SLOTS).exists():
                            act.wait_ge(S("a_shrunk"), g.back(SLOTS).done())
                        act.activation(shrink[:, g.slot(SLOTS), 0:heads], left[:, g.slot(4), 0:heads], ACT.Exp
                                       ).then_inc(S("shrink_ready"), 1)
                    g = of(0)
                    if g is not None:
                        act.wait_ge(S("a_lane_ready"), g.done(2))
                        if g.back(2).exists():
                            act.wait_ge(S("a_hot_ready"), g.back(2).done())
                        for u in range(U):
                            act.activation(lane_gap[:, g.slot(2), u, :], lanes_b, ACT.Square, bias=neg_lane[:, g.slot(4), u:u + 1]
                                           ).then_inc(S("lane_gap_ready"), 1)
                        if g.back(SLOTS).exists():
                            act.wait_ge(S("turned"), g.back(SLOTS).done())
                            act.wait_ge(S("a_hot_f_ready"), g.back(SLOTS).done())
                        act.wait_ge(S("lane_gap_ready"), g.done(U))
                        act.activation(a_hot[:, g.slot(SLOTS)], lane_gap[:, g.slot(2)], ACT.Relu, scale=-1.0, bias=1.0
                                       ).then_inc(S("a_hot_ready"), 1)
                    g = of(6)
                    if g is not None:
                        act.wait_ge(S("logit_step"), g.done(LOGIT_STEPS))
                        m = g_msg[:, g.slot(4), 0:U * (width + heads)].rearrange("p (u h c) -> p u h c", u=U, h=heads)
                        act.activation(m[:, :, :, ch], logit[:, g.slot(4), 0:U * heads].rearrange("p (u h) -> p u h", u=U), ACT.Exp
                                       ).then_inc(S("exp_ready"), 1)
                    g = of(1)
                    if g is not None:
                        act.wait_ge(S("turned"), g.done())
                        if g.back(SLOTS).exists():
                            act.wait_ge(S("looked_up"), g.back(SLOTS).done())
                            act.wait_ge(S(f"shown{(heads - 1) // 2}"), g.back(SLOTS).done())
                        bank = ps[(4, 7)[g.slot(2)]].bitcast(BF16)
                        act.activation(turned[0:CODE + 3 * heads, g.slot(SLOTS), 1, :], bank[0:CODE + 3 * heads, GE:2 * GE], ACT.Copy
                                       ).then_inc(S("turned_copied"), 1)
                        act.activation(turned[:, g.slot(SLOTS), 0, :], bank[:, 0:GE], ACT.Copy).then_inc(S("turned_copied"), 1)
                    g = of(6)
                    if g is not None:
                        if g.back(4).exists():
                            act.wait_ge(S("a_summed"), g.back(4).done())
                        act.activation(a_hot_f[:, g.slot(4)], a_hot[:, g.slot(SLOTS)], ACT.Copy).then_inc(S("a_hot_f_ready"), 1)

                attention_pipeline(act, 6, attend, n)

        @block.tensor
        def _(pe):
            pe.wait_ge(S("const1"), 5)
            pe.wait_ge(S("lane_code_ready"), 1)
            pe.transpose(ps[5][:, 0:P], lane_code, ident).then_inc(S("lane_code_t"), 1)
            for k in range(2):
                pe.wait_ge(S("counts_ready"), k + 1)
                pe.matmul(ps[7][:, 0:NB], lower, counts, start=True, stop=True)
                pe.matmul(ps[7][:, 256:256 + NB], ones, counts, start=True, stop=True).then_inc(S("prefix_ready"), 1)
            pe.wait_ge(S("falls_ready"), 1)
            pe.matmul(ps[6][:, 0:1], ones, falls, start=True, stop=True).then_inc(S("falls_summed"), 1)

            pe.wait_ge(S("weights_in"), 16 * N_WEIGHTS)
            pe.wait_ge(S("h_ready"), 1)

            def own_tiles(of):
                g = of(0)
                if g is not None:
                    if g.back(2).exists():
                        pe.wait_ge(S("own_tt"), g.back(2).done())
                    pe.wait_ge(S("own_in"), g.done())
                    pe.transpose(ps[g.slot(2)][:, 0:P], tile_in[:, g.slot(2), 0:P], ident).then_inc(S("own_t"), 1)
                g = of(1)
                if g is not None:
                    pe.wait_ge(S("own_tt"), g.done())
                    if g.back(2).exists():
                        pe.wait_ge(S("own_copied"), g.back(2).done())
                    pe.matmul(ps[2 + g.slot(2)][:, 0:F_HID], tile_t[0:F_IN, g.slot(2), 0, :], w_own, start=True, stop=True).then_inc(S("own_done"), 1)

            pipelined(pe, NT, 1, own_tiles)

            pe.wait_ge(S("own_parts_ready"), 1)
            pe.wait_ge(S("b_rows_in"), 16)

            def edge_mlp(of):
                g = of(4)
                if g is not None:
                    r = g.slot(2)
                    pe.wait_ge(S("message_ready"), g.done())
                    pe.wait_ge(S("hot_f_ready"), g.done())
                    if g.back(2).exists():
                        pe.wait_ge(S("added"), g.back(2).done())
                    for u in range(U):
                        mm = pe.matmul(ps[6 + r][:, 0:F_HID], hot_f[:, g.slot(4), u, :], msg[:, r, u, :],
                                       start=(u == 0), stop=(u == U - 1))
                    mm.then_inc(S("summed"), 1)
                g = of(3)
                if g is not None:
                    r = g.slot(2)
                    pe.wait_ge(S("mid_ready"), g.done())
                    if g.back(2).exists():
                        pe.wait_ge(S("message_ready"), g.back(2).done())
                    for u in range(U):
                        pe.matmul(ps[4 + r][:, u * P:(u + 1) * P], mid_e[:, r, u * P:(u + 1) * P], w_mid,
                                  start=(u == 0), stop=False, skip_group_check=True)
                    mm = pe.matmul(ps[4 + r][:, :].rearrange("p (u f) -> p u f", u=U), ones3,
                                   b_rows.unsqueeze(1).broadcast_to([3, U, F_HID]), start=False, stop=True,
                                   skip_group_check=True)
                    mm.then_inc(S("hidden2"), 1)
                g = of(2)
                if g is not None:
                    r = g.slot(2)
                    b = buckets.of(g)
                    pe.wait_ge(S("x_t_ready"), g.done())
                    if g.back(2).exists():
                        pe.wait_ge(S("mid_ready"), g.back(2).done())
                    pe.matmul(ps[2 + r][:, :], w_edge, x_t[0:KX, r, :], start=True, stop=False)
                    pe.wait_ge(S("hot_t_ready"), g.done())
                    for part in range(3):
                        mm = pe.matmul(ps[2 + r][:, :], own_parts[:, bass.ds(b, 1), part, :].rearrange("p a f -> p (a f)"), hot_t[:, r, :],
                                       start=False, stop=(part == 2))
                    mm.then_inc(S("hidden1"), 1)
                g = of(1)
                if g is not None:
                    pe.wait_ge(S(f"h_in{g.slot(4)}"), g.uses(4, 16 * U))
                    if g.back(1).exists():
                        pe.wait_ge(S("x_t_ready"), g.back(1).done())
                    for u in range(U):
                        mm = pe.transpose(ps[0][0:KX, u * P:(u + 1) * P], xg[:, g.slot(4), u, :], ident)
                    mm.then_inc(S("x_transposed"), 1)
                    pe.wait_ge(S("hot_ready"), g.done())
                    if g.back(1).exists():
                        pe.wait_ge(S("hot_t_ready"), g.back(1).done())
                    for u in range(U):
                        mm = pe.transpose(ps[1][:, 0:GE // 2].bitcast(BF16)[:, u * P:(u + 1) * P], hot[:, g.slot(4), u, :], ident_b)
                    mm.then_inc(S("hot_transposed"), 1)

            buckets = Buckets(pe, mybir.EngineType.PE, 0, UNROLL, 2 * UNROLL)
            pipelined(pe, GROUPS, 4, edge_mlp, each_round=buckets.load)

            pe.wait_ge(S("added"), GROUPS)

            def node_mlp(of):
                g = of(0)
                if g is not None:
                    r = g.slot(2)
                    if g.back(2).exists():
                        pe.wait_ge(S("node_tt"), g.back(2).done(2))
                    pe.wait_ge(S("node_in"), g.done(2))
                    pe.transpose(ps[r][:, 0:P], tile_in[:, r, 0:P], ident)
                    pe.transpose(ps[r][:, P:2 * P], tile_in[:, r, F_IN:], ident).then_inc(S("node_t"), 1)
                g = of(1)
                if g is not None:
                    r = g.slot(2)
                    pe.wait_ge(S("node_tt"), g.done(2))
                    if g.back(2).exists():
                        pe.wait_ge(S("node_act"), g.back(2).done())
                    pe.matmul(ps[2 + r][:, 0:P], w_node_h, tile_t[0:F_IN, r, 0, :], start=True, stop=False)
                    pe.matmul(ps[2 + r][:, 0:P], w_node_a, tile_t[:, r, 1, :], start=False, stop=True).then_inc(S("node_mid"), 1)
                g = of(2)
                if g is not None:
                    r = g.slot(2)
                    pe.wait_ge(S("node_act"), g.done())
                    if g.back(2).exists():
                        pe.wait_ge(S("node_added"), g.back(2).done())
                    pe.matmul(ps[4 + r][:, 0:F_IN], mid_t[:, r, :], w_out, start=True, stop=True).then_inc(S("node_out"), 1)

            pipelined(pe, NT, 2, node_mlp)

            for n, (heads, ch) in enumerate(LAYERS):
                row, width = row_words(heads, ch), heads * ch
                k_in = F_IN if n == 0 else F_HID

                def gat_tiles(of):
                    g = of(0)
                    if g is not None:
                        if g.back(2).exists():
                            pe.wait_ge(S("gat_tt"), g.back(2).done())
                        pe.wait_ge(S("gat_x"), g.done())
                        pe.transpose(ps[g.slot(2)][:, 0:P], tile_in[:, g.slot(2), 0:P], ident).then_inc(S("gat_t"), 1)
                    g = of(1)
                    if g is not None:
                        pe.wait_ge(S("gat_tt"), g.done())
                        if g.back(2).exists():
                            pe.wait_ge(S("gat_copied"), g.back(2).done())
                        pe.matmul(ps[2 + g.slot(2)][:, 0:width], tile_t[0:k_in, g.slot(2), 0, :], gat_w[n], start=True, stop=True).then_inc(S("gat_mm"), 1)

                pipelined(pe, NT, 1, gat_tiles, n * NT)

                step = CODE_WORDS + row
                pe.wait_ge(S("table_ready"), n + 1)
                pe.wait_ge(S("codes_in"), 1)

                def attend(of):
                    g = of(1)
                    if g is not None:
                        r = g.slot(SLOTS)
                        bank = ps[(4, 7)[g.slot(2)]].bitcast(BF16)
                        if g.back(2).exists():
                            pe.wait_ge(S("turned_copied"), g.back(2).done(2))
                        pe.wait_ge(S("a_hot_ready"), g.done())
                        for u in range(U):
                            pe.transpose(bank[:, u * P:(u + 1) * P], a_hot[:, r, u, :], ident_b)
                        pe.wait_ge(S("code_ready"), g.done(2))
                        pe.wait_ge(S(f"gathered_{r}"), g.uses(SLOTS, 16 * U))
                        for u in range(U):
                            mm = pe.transpose(bank[:, GE + u * P:GE + (u + 1) * P],
                                              g_rows[:, r, u * step:u * step + P // 2].bitcast(BF16), ident_b)
                        mm.then_inc(S("turned"), 1)
                    g = of(5)
                    if g is not None:
                        pe.wait_ge(S("max_step"), g.done(MAX_STEPS))
                        if g.back(1).exists():
                            pe.wait_ge(S("logit_step"), g.back(1).done(LOGIT_STEPS))
                        lk = look[:, g.slot(4), 0:6 * heads].rearrange("p (k w) -> p k w", k=3)
                        for u in range(U):
                            for part in range(3):
                                mm = pe.matmul(ps[5][:, u * 2 * heads:(u + 1) * 2 * heads], turned[:, g.slot(SLOTS), 0, u * P:(u + 1) * P],
                                               lk[:, part, :], start=(part == 0), stop=(part == 2))
                        mm.then_inc(S("looked_up"), 1)
                    g = of(7)
                    if g is not None:
                        out_w = width + heads
                        pe.wait_ge(S("a_hot_f_ready"), g.done())
                        pe.wait_ge(S("msg_ready"), g.done())
                        if g.back(1).exists():
                            pe.wait_ge(S("a_added"), g.back(1).done())
                        for u in range(U):
                            mm = pe.matmul(ps[6][:, 0:out_w], a_hot_f[:, g.slot(4), u, :], g_msg[:, g.slot(4), u * out_w:(u + 1) * out_w],
                                           start=(u == 0), stop=(u == U - 1))
                        mm.then_inc(S("a_summed"), 1)
                    g = of(2)
                    if g is not None:
                        pe.wait_ge(S("turned_copied"), g.done(2))
                        for h in range(heads):
                            if heads > 1:
                                if h % 2 == 0 and g.back(1).exists():
                                    pe.wait_ge(S(f"max_taken{h // 2}"), g.back(1).done())
                            elif g.back(2).exists():
                                pe.wait_ge(S("max_taken0"), g.back(2).done())
                            bank = ps[h] if heads > 1 else ps[g.slot(2)]
                            mm = pe.matmul(bank, picks[n][:, h, :], turned[0:CODE + 3 * heads, g.slot(SLOTS), 1, :], start=True, stop=True)
                            if h % 2 == 1 or heads == 1:
                                mm.then_inc(S(f"shown{h // 2}"), 1)

                attention_pipeline(pe, 7, attend, n)

        @block.vector
        def _(dve):
            link = Chain(dve, S("dve_step"))
            link(dve.memset(zero, 0.0))
            link(dve.memset(w_edge, 0.0))
            dve.sem_inc(S("zero_ready"), 1)
            dve.wait_ge(S("const1"), 5)
            link(dve.tensor_copy(ident_b, ident))
            link(dve.tensor_copy(lanes_b, lanes))
            link(dve.memset(lane_code, 0.0))
            for half in range(2):
                for bit in range(LANE_BITS + 1):
                    at = half * (CODE // 2) + bit
                    link(dve.memset(bit_masks[:, at:at + 1], 1 << bit if bit < LANE_BITS else -P))
            link(dve.tensor_tensor(lane_no, lane_no, bit_masks, ALU.bitwise_and))
            link(dve.tensor_scalar(lane_code[:, 0:CODE // 2], lane_no[:, 0:CODE // 2], 0.0, None, ALU.not_equal))
            link(dve.tensor_scalar(lane_code[:, CODE // 2:CODE], lane_no[:, CODE // 2:], 0.0, None, ALU.is_equal))
            dve.sem_inc(S("lane_code_ready"), 1)
            dve.wait_ge(S("lane_code_t"), 1)
            dve.wait_ge(S("picks_ready"), 6)
            for n, (heads, _) in enumerate(LAYERS):
                link(dve.tensor_copy(picks[n][0:CODE], ps[5][0:CODE, 0:P].unsqueeze(1).broadcast_to([CODE, heads, P])))
            dve.sem_inc(S("codes_in"), 1)
            link(dve.memset(ones3, 1.0))

            for order, (name, key, lane, pos) in enumerate((("s", src_i, lane_s, pos_s), ("d", dst_i, None, pos_d))):
                dve.wait_ge(S("src_in" if order == 0 else "dst_in"), 16)
                link(dve.tensor_scalar(rank.bitcast(I32), key, LANE_BITS, None, ALU.arith_shift_right))
                link(dve.tensor_copy(bucket, rank.bitcast(I32)))
                if name == "s":
                    link(dve.tensor_scalar(rank.bitcast(I32), key, P - 1, None, ALU.bitwise_and))
                    link(dve.tensor_copy(hit, rank.bitcast(I32)))
                    link(dve.tensor_scalar(lane, bucket, float(NT), None, ALU.is_ge))
                    link(dve.tensor_tensor(lane, hit, lane, ALU.subtract))
                else:
                    dve.wait_ge(S("next_in"), 16)
                    link(dve.tensor_tensor(hit, key, pos_d, ALU.is_gt))
                    link(dve.tensor_reduce(falls, hit, op=ALU.add, axis=AX.X))
                    dve.sem_inc(S("falls_ready"), 1)
                with link.loop(NB, 1) as b:
                    link(dve.tensor_scalar(hit, bucket, lanes[:, bass.ds(b, 1)], None, ALU.is_equal, ALU.add,
                                           accum_out=counts[:, bass.ds(b, 1)]))
                dve.sem_inc(S("counts_ready"), 1)
                dve.wait_ge(S("prefix_ready"), order + 1)
                link(dve.tensor_copy(total, ps[7][:, 256:256 + NB]))
                link(dve.tensor_scalar(n_groups_i, ps[7][:, 256:256 + NB], float(GE - 1), None, ALU.add))
                link(dve.tensor_scalar(n_groups_i, n_groups_i, GE_BITS, None, ALU.arith_shift_right))
                link(dve.tensor_copy(n_groups, n_groups_i))
                link(dve.tensor_tensor_scan(first_group, n_groups, zero.broadcast_to([P, NB]), 0.0, ALU.add, ALU.add))
                link(dve.tensor_tensor(first_group, first_group, n_groups, ALU.subtract))
                if name == "s":
                    link(dve.scalar_tensor_tensor(base, first_group, float(GE), ps[7][:, 0:NB], ALU.mult, ALU.add))
                else:
                    link(dve.tensor_tensor_scan(base, total, zero.broadcast_to([P, NB]), 0.0, ALU.add, ALU.add))
                    link(dve.tensor_tensor(base, base, total, ALU.subtract))
                    link(dve.tensor_tensor(base, base, ps[7][:, 0:NB], ALU.add))
                link(dve.tensor_scalar(base, base, -1.0, None, ALU.add))
                link(dve.memset(pos_f, 0.0))
                if name == "s":
                    with link.loop(NB // 2, 6) as pair:
                        for k in range(2):
                            no = lanes[:, bass.ds(2 * pair + k, 1)]
                            link(dve.tensor_scalar(hit, bucket, no, None, ALU.is_equal))
                            dve.wait_ge(S("places_added"), 2 * pair + k + 1)
                            link(dve.tensor_tensor_scan(places[k], hit, zero.broadcast_to([P, COLS]), base[:, bass.ds(2 * pair + k, 1)], ALU.add, ALU.add))
                            link(dve.scalar_tensor_tensor(places[k], bucket, no, places[k], ALU.is_equal, ALU.mult))
                            dve.sem_inc(S("places_ready"), 1)
                    dve.wait_ge(S("places_added"), NB + 2)
                else:
                    with link.loop(NB, 4) as b:
                        no = lanes[:, bass.ds(b, 1)]
                        link(dve.tensor_scalar(hit, bucket, no, None, ALU.is_equal))
                        link(dve.tensor_tensor_scan(rank, hit, zero.broadcast_to([P, COLS]), base[:, bass.ds(b, 1)], ALU.add, ALU.add))
                        link(dve.scalar_tensor_tensor(rank, bucket, no, rank, ALU.is_equal, ALU.mult))
                        link(dve.tensor_tensor(pos_f, pos_f, rank, ALU.add))
                link(dve.tensor_copy(pos, pos_f))
                if name == "s":
                    dve.wait_ge(S("dst_in"), 16)
                    link(dve.tensor_scalar(dst_c, dst_i, float(NT * P - 1), None, ALU.min))
                else:
                    link(dve.tensor_copy(edge_d[:, :, 0], dst_i))
                    link(dve.tensor_scalar(edge_d[:, :, 1].bitcast(I32), src_i, float(NT * P - 1), None, ALU.min))
                    dve.wait_ge(S("falls_summed"), 1)
                    link(dve.tensor_scalar(is_sorted, ps[6][0:1, 0:1], 0.0, None, ALU.is_equal))
                dve.sem_inc(S(f"pos_ready_{name}"), 1)
                link(dve.memset(bucket_f, 0.0))
                with link.loop(NT - 1, 1) as b:
                    link(dve.scalar_tensor_tensor(bucket_f, group_no, first_group[:, bass.ds(b + 1, 1)], bucket_f, ALU.is_ge, ALU.add))
                link(dve.tensor_copy(bucket_of[order][0:1, 0:ROW_GROUPS], bucket_f[0:1, :]))
                if name == "d":
                    link(dve.tensor_scalar(first_node, bucket_f, float(P), None, ALU.mult))
                    link(dve.scalar_tensor_tensor(gap, n_groups, -float(GE), total, ALU.mult, ALU.add))
                    link(dve.tensor_scalar(start_f, group_no, float(GE), None, ALU.mult))
                    with link.loop(NT - 1, 2) as b:
                        link(dve.tensor_scalar(room, group_no, first_group[:, bass.ds(b + 1, 1)], gap[:, bass.ds(b, 1)], ALU.is_ge, ALU.mult))
                        link(dve.tensor_tensor(start_f, start_f, room, ALU.add))
                    link(dve.tensor_scalar(start_f, start_f, float(LINEAR), None, ALU.min))
                    link(dve.tensor_copy(first_edge, start_f[0:1, :]))

            def layer_norm(which):
                if which == 0:
                    dve.wait_ge(S("x_in"), 16)
                link(dve.tensor_reduce(stat[:, 0, :], xs, op=ALU.add, axis=AX.X))
                link(dve.tensor_scalar(stat[:, 0, :], stat[:, 0, :], 1.0 / F_IN, None, ALU.mult))
                link(dve.tensor_tensor(hs, xs, stat[:, 0, :].unsqueeze(2).broadcast_to([P, NT, F_IN]), ALU.subtract))
                sq = tab[:, 0:NT * F_IN].rearrange("p (t f) -> p t f", t=NT)
                link(dve.tensor_tensor(sq, hs, hs, ALU.mult))
                link(dve.tensor_reduce(stat[:, 1, :], sq, op=ALU.add, axis=AX.X))
                link(dve.tensor_scalar(stat[:, 1, :], stat[:, 1, :], 1.0 / F_IN, 1e-5, ALU.mult, ALU.add))
                dve.sem_inc(S("var_ready"), 1)
                dve.wait_ge(S("std_ready"), which + 1)
                link(dve.reciprocal(stat[:, 0, :], stat[:, 1, :]))
                link(dve.tensor_tensor(hs, hs, stat[:, 0, :].unsqueeze(2).broadcast_to([P, NT, F_IN]), ALU.mult))
                link(dve.tensor_scalar(hs, hs, 0.0, None, ALU.max))

            layer_norm(0)
            dve.sem_inc(S("h_ready"), 1)
            dve.wait_ge(S("weights_in"), 16 * N_WEIGHTS)
            link(dve.tensor_copy(b_part[:, 0, :], b_mid))
            link(dve.tensor_tensor(b_rest, b_mid, b_part[:, 0, :], ALU.subtract))
            link(dve.tensor_copy(b_part[:, 1, :], b_rest))
            link(dve.tensor_tensor(b_rest, b_rest, b_part[:, 1, :], ALU.subtract))
            link(dve.tensor_copy(b_part[:, 2, :], b_rest))
            dve.sem_inc(S("b_part_ready"), 1)

            own = tab[:, 0:NT * F_HID].rearrange("p (t f) -> p t f", f=F_HID)

            def own_tiles(of):
                g = of(1)
                if g is not None:
                    dve.wait_ge(S("own_done"), g.done())
                    dve.tensor_copy(own[:, g.at, :], ps[2 + g.slot(2)][:, 0:F_HID]).then_inc(S("own_copied"), 1)

            pipelined(dve, NT, 1, own_tiles)
            dve.wait_ge(S("own_copied"), NT)
            dve.wait_ge(S("arena_free"), 1)
            for part in range(3):
                link(dve.tensor_copy(own_parts[:, :, part, :], own))
                if part < 2:
                    link(dve.tensor_tensor(own, own, own_parts[:, :, part, :], ALU.subtract))
            fills = ROW_GROUPS * GE // (P * FILL)
            dve.wait_ge(S("blank_d_out"), 16)
            dve.wait_ge(S("blank_s_out"), 16 * fills)
            link(dve.memset(acc, 0.0))
            dve.sem_inc(S("own_parts_ready"), 1)

            def edge_mlp(of):
                g = of(5)
                if g is not None:
                    b = bucket_reg(dve, 0, g)
                    if g.back(1).exists():
                        dve.wait_ge(S("added"), g.back(1).done())
                    dve.wait_ge(S("summed"), g.done())
                    to = agg[:, bass.ds(b, 1), :].rearrange("p a f -> p (a f)")
                    dve.tensor_tensor(to, to, ps[6 + g.slot(2)][:, 0:F_HID], ALU.add).then_inc(S("added"), 1)
                g = of(0)
                if g is not None:
                    r = g.slot(4)
                    dve.wait_ge(S(f"rec_in{r}"), g.uses(4, 16))
                    dve.tensor_copy(lane_e[:, g.slot(2), :], xg[:, r, :, KX - 3]).then_inc(S("lane_ready"), 1)
                    if g.back(4).exists():
                        dve.wait_ge(S("hot_transposed"), g.back(4).done())
                        dve.wait_ge(S("hot_f_ready"), g.back(4).done())
                    dve.wait_ge(S("lane_ready"), g.done())
                    dve.tensor_tensor(hot[:, r], lanes_b.unsqueeze(1).broadcast_to([P, U, P]),
                                      lane_e[:, g.slot(2), :].unsqueeze(2).broadcast_to([P, U, P]), ALU.is_equal).then_inc(S("hot_ready"), 1)
                g = of(1)
                if g is not None:
                    dve.wait_ge(S("hot_transposed"), g.done())
                    if g.back(2).exists():
                        dve.wait_ge(S("hidden1"), g.back(2).done())
                    dve.tensor_copy(hot_t[:, g.slot(2), :], ps[1][:, 0:GE // 2].bitcast(BF16)).then_inc(S("hot_t_ready"), 1)

            pipelined(dve, GROUPS, 5, edge_mlp)
            dve.wait_ge(S("added"), GROUPS)
            dve.sem_inc(S("mlp_done"), 1)

            link(dve.tensor_tensor(xs, xs, hs, ALU.add))
            link(dve.tensor_tensor(xs, xs, nb2_row.unsqueeze(1).broadcast_to([P, NT, F_IN]), ALU.add))

            def node_mlp(of):
                g = of(2)
                if g is not None:
                    dve.wait_ge(S("node_out"), g.done())
                    dve.tensor_tensor(xs[:, g.at, :], xs[:, g.at, :], ps[4 + g.slot(2)][:, 0:F_IN], ALU.add).then_inc(S("node_added"), 1)

            pipelined(dve, NT, 2, node_mlp)
            dve.wait_ge(S("node_added"), NT)
            layer_norm(1)
            dve.sem_inc(S("gat_in"), 1)

            for n, (heads, ch) in enumerate(LAYERS):
                row, width = row_words(heads, ch), heads * ch
                tb = tab[:, 0:NT * row].rearrange("p (t f) -> p t f", f=row)
                at_s, at_f = part_words(heads), part_words(heads) + heads
                tb_parts = tab[:, 0:NT * row].bitcast(BF16).rearrange("p (t f) -> p t f", t=NT)[
                    :, :, 0:3 * heads].rearrange("p t (k h) -> p t k h", k=3)
                ac = acc[:, 0:NT * (width + heads)].rearrange("p (t h c) -> p t h c", t=NT, h=heads)
                plain = acc[:, 0:NT * width].rearrange("p (t f) -> p t f", t=NT)
                a_s = alpha_s[:, 0:NT * heads].rearrange("p (t h) -> p t h", h=heads)
                a_d = alpha_d[:, 0:NT * heads].rearrange("p (t h) -> p t h", h=heads)
                sh = shift[:, 0:NT * heads].rearrange("p (t h) -> p t h", h=heads)
                rs = rest[:, 0:NT * heads].rearrange("p (t h) -> p t h", h=heads)
                dp = dst_parts[:, 0:NT * 3 * heads].rearrange("p (t k h) -> p t k h", t=NT, k=3)

                def gat_tiles(of):
                    g = of(1)
                    if g is not None:
                        dve.wait_ge(S("gat_mm"), g.done())
                        dve.tensor_copy(tb[:, g.at, at_f:row], ps[2 + g.slot(2)][:, 0:width]).then_inc(S("gat_copied"), 1)

                pipelined(dve, NT, 1, gat_tiles, n * NT)
                dve.wait_ge(S("gat_copied"), NT * (n + 1))
                for vec, to in ((att_s[n], a_s), (att_d[n], a_d)):
                    link(dve.tensor_tensor(plain, tb[:, :, at_f:row], vec.unsqueeze(1).broadcast_to([P, NT, width]), ALU.mult))
                    for h in range(heads):
                        link(dve.tensor_reduce(to[:, :, h], plain[:, :, h * ch:(h + 1) * ch], op=ALU.add, axis=AX.X))
                link(dve.memset(tb[:, :, 0:at_s], 0.0))
                link(dve.tensor_copy(tb[:, :, at_s:at_f], a_s))
                for value, to in ((a_s, tb_parts), (a_d, dp)):
                    link(dve.tensor_copy(rs, value))
                    for part in range(3):
                        link(dve.tensor_copy(to[:, :, part, :], rs))
                        if part < 2:
                            link(dve.tensor_tensor(rs, rs, to[:, :, part, :], ALU.subtract))
                link(dve.tensor_tensor(sh, a_s, a_d, ALU.add))
                link(dve.scalar_tensor_tensor(sh, sh, SLOPE, sh, ALU.mult, ALU.max))
                for h in range(heads):
                    link(dve.tensor_copy(ac[:, :, h, 0:ch], tb[:, :, at_f + h * ch:at_f + (h + 1) * ch]))
                link(dve.memset(ac[:, :, :, ch:ch + 1], 1.0))
                dve.sem_inc(S("table_ready"), 1)

                step = CODE_WORDS + row
                buckets = Buckets(dve, mybir.EngineType.DVE, 1, SLOTS, 2 * SLOTS)

                def edge_codes(g):
                    if g is None:
                        return
                    r = g.slot(SLOTS)
                    codes = g_rows[:, r, 0:U * step].bitcast(BF16).rearrange("p (u w) -> p u w", u=U)
                    bits = lane_bits[:, g.slot(4)]
                    first = first_node[:, bass.ds(g.at, 1)]
                    dve.wait_ge(S(f"ids_in_{r}"), g.uses(SLOTS, 16))
                    dve.tensor_scalar(lane_int[:, g.slot(4), :], ids[:, r, :, 0], first, None, ALU.subtract).then_inc(S("a_lane_ready"), 1)
                    if g.back(4).exists():
                        dve.wait_ge(S("a_hot_ready"), g.back(4).done())
                    dve.tensor_scalar(neg_lane[:, g.slot(4), :], ids[:, r, :, 0], -1.0, first, ALU.mult, ALU.add).then_inc(S("a_lane_ready"), 1)
                    yield
                    dve.wait_ge(S("a_lane_ready"), g.done(2))
                    dve.tensor_tensor(bits, lane_int[:, g.slot(4), :].unsqueeze(2).broadcast_to([P, U, CODE]),
                                      bit_masks.unsqueeze(1).broadcast_to([P, U, CODE]), ALU.bitwise_and).then_inc(S("bits_ready"), 1)
                    yield
                    if g.back(SLOTS).exists():
                        dve.wait_ge(S("turned"), g.back(SLOTS).done())
                    dve.wait_ge(S("bits_ready"), g.done())
                    dve.tensor_scalar(codes[:, :, 0:CODE // 2], bits[:, :, 0:CODE // 2], 0.0, -BIG, ALU.is_equal, ALU.mult
                                      ).then_inc(S("code_ready"), 1)
                    dve.tensor_scalar(codes[:, :, CODE // 2:CODE], bits[:, :, CODE // 2:], 0.0, -BIG, ALU.not_equal, ALU.mult
                                      ).then_inc(S("code_ready"), 1)

                def largest_shares(g):
                    if g is None:
                        return
                    if heads == 1:
                        dve.wait_ge(S("shown0"), g.done())
                        dve.tensor_reduce(part_max[:, g.slot(4), 0:1], ps[g.slot(2)], op=ALU.max, axis=AX.X).then_inc(S("max_taken0"), 1)
                        return
                    for pair in range(heads // 2):
                        dve.wait_ge(S(f"shown{pair}"), g.done())
                        dve.tensor_reduce(part_max[:, g.slot(4), 2 * pair:2 * pair + 2],
                                          ps_all[:, pair * 1024:(pair + 1) * 1024].rearrange("p (h e) -> p h e", h=2),
                                          op=ALU.max, axis=AX.X).then_inc(S(f"max_taken{pair}"), 1)
                        yield

                def new_shifts(g):
                    if g is None:
                        return
                    small = S("max_step")

                    def after(k):
                        dve.wait_ge(small, g.back(1).done(MAX_STEPS) + k)

                    b = buckets.of(g)
                    here = sh[:, bass.ds(b, 1), :].rearrange("p a h -> p (a h)")
                    dst_share = a_d[:, bass.ds(b, 1), :].rearrange("p a h -> p (a h)")
                    parts_here = dp[:, bass.ds(b, 1), :, :].rearrange("p a k h -> p (a k) h")
                    r = g.slot(4)
                    lk = look[:, r, 0:6 * heads].rearrange("p (k w) -> p k w", k=3)
                    nm, ns = new_max[:, r, 0:heads], new_shift[:, r, 0:heads]
                    lf = left[:, r, 0:heads]
                    if g.back(4).exists():
                        dve.wait_ge(S("looked_up"), g.back(4).done())
                        dve.wait_ge(S("shrink_ready"), g.back(4).done())
                    dve.tensor_scalar(lk[:, :, 0:heads], parts_here, 1.0, None, ALU.mult).then_inc(small, 1)
                    dve.wait_ge(S(f"max_taken{(heads - 1) // 2}"), g.done())
                    dve.tensor_tensor(nm, part_max[:, r, 0:heads], dst_share, ALU.add).then_inc(small, 1)
                    yield
                    after(2)
                    dve.scalar_tensor_tensor(nm, nm, SLOPE, nm, ALU.mult, ALU.max).then_inc(small, 1)
                    yield
                    after(3)
                    dve.tensor_tensor(ns, nm, here, ALU.max).then_inc(small, 1)
                    yield
                    after(4)
                    dve.tensor_tensor(lf, here, ns, ALU.subtract).then_inc(small, 1)
                    dve.tensor_copy(lk[:, 0, heads:], ns).then_inc(small, 1)
                    yield
                    after(6)
                    dve.tensor_scalar(here, ns, 1.0, None, ALU.mult).then_inc(small, 1)
                    dve.tensor_tensor(nm, ns, lk[:, 0, heads:], ALU.subtract).then_inc(small, 1)
                    yield
                    after(8)
                    dve.tensor_copy(lk[:, 1, heads:], nm).then_inc(small, 1)
                    yield
                    after(9)
                    dve.tensor_tensor(lk[:, 2, heads:], nm, lk[:, 1, heads:], ALU.subtract).then_inc(small, 1)

                def logits(g):
                    if g is None:
                        return
                    small = S("logit_step")

                    def after(k):
                        dve.wait_ge(small, g.back(1).done(LOGIT_STEPS) + k)

                    r = g.slot(4)
                    rows = g_rows[:, g.slot(SLOTS), 0:U * step].rearrange("p (u w) -> p u w", u=U)[:, :, CODE_WORDS:]
                    found = ps[5][:, 0:U * 2 * heads].rearrange("p (u w) -> p u w", u=U)
                    lg = logit[:, r, 0:U * heads].rearrange("p (u h) -> p u h", u=U)
                    l2 = logit2[:, r, 0:U * heads].rearrange("p (u h) -> p u h", u=U)
                    dve.wait_ge(S("looked_up"), g.done())
                    dve.tensor_tensor(l2, rows[:, :, at_s:at_f], found[:, :, 0:heads], ALU.add).then_inc(small, 1)
                    yield
                    if g.back(4).exists():
                        dve.wait_ge(S("exp_ready"), g.back(4).done())
                    after(1)
                    dve.scalar_tensor_tensor(lg, l2, SLOPE, l2, ALU.mult, ALU.max).then_inc(small, 1)
                    yield
                    after(2)
                    dve.tensor_tensor(l2, lg, found[:, :, heads:], ALU.subtract).then_inc(small, 1)
                    yield
                    after(3)
                    dve.tensor_scalar(lg, l2, 0.0, None, ALU.min).then_inc(small, 1)

                def messages(g):
                    if g is None:
                        return
                    rows = g_rows[:, g.slot(SLOTS), 0:U * step].rearrange("p (u w) -> p u w", u=U)[:, :, CODE_WORDS:]
                    m = g_msg[:, g.slot(4), 0:U * (width + heads)].rearrange("p (u h c) -> p u h c", u=U, h=heads)
                    dve.wait_ge(S("exp_ready"), g.done())
                    dve.tensor_tensor(m[:, :, :, 0:ch], rows[:, :, at_f:row].rearrange("p u (h c) -> p u h c", h=heads),
                                      m[:, :, :, ch:ch + 1].broadcast_to([P, U, heads, ch]), ALU.mult).then_inc(S("msg_ready"), 1)

                def sums(g):
                    if g is None:
                        return
                    b = buckets.of(g)
                    to = ac[:, bass.ds(b, 1), :, :].rearrange("p a h c -> p (a h) c")
                    if g.back(1).exists():
                        dve.wait_ge(S("a_added"), g.back(1).done())
                    dve.wait_ge(S("shrink_ready"), g.done())
                    dve.tensor_tensor(to, to, shrink[:, g.slot(SLOTS), 0:heads].unsqueeze(2).broadcast_to([P, heads, ch + 1]), ALU.mult
                                      ).then_inc(S("a_shrunk"), 1)
                    yield
                    dve.wait_ge(S("a_summed"), g.done())
                    dve.wait_ge(S("a_shrunk"), g.done())
                    dve.tensor_tensor(to, to, ps[6][:, 0:width + heads].rearrange("p (h c) -> p h c", h=heads), ALU.add
                                      ).then_inc(S("a_added"), 1)

                def attend(of):
                    codes, large, shifts = edge_codes(of(0)), largest_shares(of(3)), new_shifts(of(4))
                    logs, adds = logits(of(6)), sums(of(8))
                    for part in (shifts, codes, logs, shifts, adds, logs, shifts, codes, logs, shifts, adds, logs,
                                 large, shifts, large, shifts):
                        next(part, None)
                    messages(of(6))
                    for part in (shifts, codes, shifts):
                        next(part, None)

                attention_pipeline(dve, 8, attend, n, buckets.load)
                dve.wait_ge(S("a_added"), GROUPS * (n + 1))
                link(dve.tensor_scalar(rs, ac[:, :, :, ch], 1e-16, None, ALU.add))
                link(dve.reciprocal(rs, rs))
                res = tab[:, 0:NT * width].rearrange("p (t f) -> p t f", t=NT)
                for h in range(heads):
                    link(dve.tensor_tensor(res[:, :, h * ch:(h + 1) * ch], ac[:, :, h, 0:ch],
                                           rs[:, :, h:h + 1].broadcast_to([P, NT, ch]), ALU.mult))
                link(dve.tensor_tensor(res, res, gat_b[n].unsqueeze(1).broadcast_to([P, NT, width]), ALU.add))
                if n == 0:
                    link(dve.tensor_scalar(plain, res, 0.0, None, ALU.max))
                    dve.sem_inc(S("gat_in"), 1)
                else:
                    link(dve.tensor_tensor(hs, xs, res, ALU.add))
                    dve.sem_inc(S("out_ready"), 1)


_INS = ["x", "src", "dst", "dst_next", "edge_attr_16", "edge_weight", "L0_gnn_ew1", "L0_gnn_eb1", "L0_gnn_ew2",
        "L0_gnn_eb2", "L0_gnn_nw1", "L0_gnn_nb1", "L0_gnn_nw2", "L0_gnn_nb2", "L1_gnn_W1",
        "L1_gnn_a_src1", "L1_gnn_a_dst1", "L1_gnn_b1", "L1_gnn_W2", "L1_gnn_a_src2",
        "L1_gnn_a_dst2", "L1_gnn_b2"]


def kernel(**inputs):
    import numpy as np
    import concourse.bacc as bacc
    from concourse.bass_utils import run_bass_kernel_spmd

    def padded(a, rows, fill):
        full = np.full((rows,) + a.shape[1:], fill, a.dtype)
        full[:a.shape[0]] = a
        return full

    nc = bacc.Bacc("TRN2", target_bir_lowering=False, num_devices=1)
    arrays, args = {}, []
    for name in _INS:
        a = np.ascontiguousarray(inputs["dst"][1:] if name == "dst_next" else inputs[name])
        if name == "x":
            a = padded(a, NT * P, 0)
        elif name in ("src", "dst", "dst_next"):
            a = padded(a, COLS * P, NT * P)
        elif name.startswith("edge"):
            a = padded(a, COLS * P, 0)
        arrays[f"in_{name}"] = a
        args.append(nc.dram_tensor(f"in_{name}", a.shape, mybir.dt.from_np(a.dtype), kind="ExternalInput").ap())
    args.append(nc.dram_tensor("out_0", (NT * P, F_IN), F32, kind="ExternalOutput").ap())
    gnn_kernel(nc, *args)
    r = run_bass_kernel_spmd(nc, [arrays], core_ids=[0])
    return r.results[0]["out_0"][:N_NODES]
```
